# Optimizing a Trainium2 kernel written in Bass

```python
import numpy as np
import jax
import jax.numpy as jnp

def _softmax(x, axis=-1):
    return jax.nn.softmax(x, axis=axis)

def _gelu(x):
    return jax.nn.gelu(x, approximate=True)

def _silu(x):
    return jax.nn.silu(x)

def _sigmoid(x):
    return jax.nn.sigmoid(x)

def _layernorm(x, axis=-1, eps=1e-05):
    m = jnp.mean(x, axis=axis, keepdims=True)
    v = jnp.var(x, axis=axis, keepdims=True)
    return (x - m) / jnp.sqrt(v + eps)

def _scatter_add(tgt, idx, src, axis=0):
    return tgt.at[idx].add(src)

def _segment_sum(src, seg, n):
    return jax.ops.segment_sum(src, seg, n)
kernel_name = 'mk_recurrent_d1_jaxref_r4_4041e5'

def setup_inputs(seed: int=0):
    np.random.seed(seed)
    _w = jnp.asarray

    def _L0_attn_setup():
        import jax, jax.numpy as jnp
        import numpy as np
        B, T, HID, H, DH, K = (2, 256, 256, 16, 64, 4)
        ROPE_BASE = 10000.0
        EPS = 1e-06

        def _causal_dwconv(x, w, b):
            xc = jnp.transpose(x, (0, 2, 1))
            y = jax.lax.conv_general_dilated(xc, w, window_strides=(1,), padding=[(K - 1, 0)], dimension_numbers=('NCH', 'OIH', 'NCH'), feature_group_count=xc.shape[1])
            y = y + b[None, :, None]
            return jax.nn.silu(jnp.transpose(y, (0, 2, 1)))

        def _rope(x, cos, sin):
            c = cos[None, :, None, :]
            s = sin[None, :, None, :]
            x1, x2 = (x[..., ::2], x[..., 1::2])
            return jnp.concatenate([x1 * c[..., ::2] - x2 * s[..., ::2], x1 * s[..., ::2] + x2 * c[..., ::2]], axis=-1)

        def _delta_rule(q, k, v, alpha, beta, D_param):
            qs = jnp.moveaxis(q, 1, 0).astype(jnp.float32)
            ks = jnp.moveaxis(k, 1, 0).astype(jnp.float32)
            vs = jnp.moveaxis(v, 1, 0).astype(jnp.float32)
            als = jnp.moveaxis(alpha, 1, 0).astype(jnp.float32)
            bes = jnp.moveaxis(beta, 1, 0).astype(jnp.float32)

            def step(S, inp):
                qt, kt, vt, at, bt = inp
                ot = jnp.einsum('bhd,bhde->bhe', qt, S)
                ot = ot + D_param[None, :, None] * jnp.sum(qt * kt, -1, keepdims=True) * vt
                kS = jnp.einsum('bhd,bhde->bhe', kt, S)
                at_ = at[..., None, None]
                bt_ = bt[..., None, None]
                S_new = at_ * (S - bt_ * kt[..., :, None] * kS[..., None, :]) + bt_ * kt[..., :, None] * vt[..., None, :]
                return (S_new, ot)
            S0 = jnp.zeros((q.shape[0], H, DH, DH), jnp.float32)
            _, outs = jax.lax.scan(step, S0, (qs, ks, vs, als, bes))
            return jnp.moveaxis(outs, 0, 1)

        def _forward(x, Wq, Wk, Wv, Wg, Wo, bw, bb, gkw, gkb, qcw, qcb, kcw, kcb, vcw, vcb, A_log, D_param, dt_bias, onorm_w):
            Bb, Tt, _ = x.shape
            q = _causal_dwconv(x @ Wq, qcw, qcb).reshape(Bb, Tt, H, DH)
            k = _causal_dwconv(x @ Wk, kcw, kcb).reshape(Bb, Tt, H, DH)
            v = _causal_dwconv(x @ Wv, vcw, vcb).reshape(Bb, Tt, H, DH)
            t = jnp.arange(Tt, dtype=jnp.float32)
            inv_freq = 1.0 / ROPE_BASE ** (jnp.arange(0, DH, 2, dtype=jnp.float32) / DH)
            freqs = jnp.outer(t, inv_freq)
            emb = jnp.concatenate([freqs, freqs], -1)
            cos, sin = (jnp.cos(emb), jnp.sin(emb))
            q = _rope(q, cos, sin)
            k = _rope(k, cos, sin)
            q = q * jax.lax.rsqrt(jnp.sum(q * q, -1, keepdims=True) + EPS)
            k = k * jax.lax.rsqrt(jnp.sum(k * k, -1, keepdims=True) + EPS)
            beta = jax.nn.sigmoid(x @ bw + bb)
            alpha = jnp.exp(-jnp.exp(A_log) * jax.nn.softplus(x @ gkw + gkb + dt_bias))
            o = _delta_rule(q, k, v, alpha, beta, D_param)
            g = (x @ Wg).reshape(Bb, Tt, H, DH)
            on = o * jax.lax.rsqrt(jnp.mean(o * o, -1, keepdims=True) + EPS) * onorm_w
            o = g * jax.nn.silu(on)
            return o.reshape(Bb, Tt, H * DH) @ Wo
        key = jax.random.key(seed)
        ks = jax.random.split(key, 20)
        w = lambda i, shape, s=0.02: jax.random.normal(ks[i], shape, jnp.float32) * s
        return {'x': jax.random.normal(ks[0], (B, T, HID), jnp.float32), 'Wq': w(1, (HID, H * DH)), 'Wk': w(2, (HID, H * DH)), 'Wv': w(3, (HID, H * DH)), 'Wg': w(4, (HID, H * DH)), 'Wo': w(5, (H * DH, HID)), 'bw': w(6, (HID, H)), 'bb': jnp.zeros((H,), jnp.float32), 'gkw': w(7, (HID, H)), 'gkb': jnp.zeros((H,), jnp.float32), 'qcw': w(8, (H * DH, 1, K), 0.3), 'qcb': jnp.zeros((H * DH,), jnp.float32), 'kcw': w(9, (H * DH, 1, K), 0.3), 'kcb': jnp.zeros((H * DH,), jnp.float32), 'vcw': w(10, (H * DH, 1, K), 0.3), 'vcb': jnp.zeros((H * DH,), jnp.float32), 'A_log': jnp.log(jax.random.uniform(ks[11], (H,), jnp.float32, 1.0, 16.0)), 'D_param': jnp.ones((H,), jnp.float32), 'dt_bias': jax.random.uniform(ks[12], (H,), jnp.float32, -0.01, 0.01), 'onorm_w': jnp.ones((DH,), jnp.float32)}
    _L0_attn_in = _L0_attn_setup()

    def _L0_ffn_setup():
        import jax, jax.numpy as jnp
        import numpy as np
        DIM = 256
        DEPTH = 2
        HEADS = 8
        DIM_HEAD = 64
        WINDOW = 128
        INNER = HEADS * DIM_HEAD
        HID = int(DIM * 4 * 2 / 3)
        B, N = (2, 2048)
        QK_SCALE = 8.0

        def shift_token(t):
            t1, t2 = jnp.split(t, 2, axis=-1)
            t2 = jnp.pad(t2, ((0, 0), (1, 0), (0, 0)))[:, :-1]
            return jnp.concatenate([t1, t2], axis=-1)

        def l2norm(t):
            return t / jnp.clip(jnp.linalg.norm(t, axis=-1, keepdims=True), 1e-12)

        def rotate_half(x):
            x1, x2 = jnp.split(x, 2, axis=-1)
            return jnp.concatenate([-x2, x1], axis=-1)

        def rotary_xpos(q, k):
            n = q.shape[-2]
            half_idx = jnp.arange(0, DIM_HEAD, 2, dtype=jnp.float32)
            inv_freq = 1.0 / 10000.0 ** (half_idx / DIM_HEAD)
            t = jnp.arange(n, dtype=jnp.float32)
            freqs = t[:, None] * inv_freq[None, :]
            freqs = jnp.concatenate([freqs, freqs], axis=-1)
            base = (half_idx + 0.4 * DIM_HEAD) / (1.4 * DIM_HEAD)
            power = (t - n // 2) / float(WINDOW // 2)
            scale = base[None, :] ** power[:, None]
            scale = jnp.concatenate([scale, scale], axis=-1)
            cos, sin = (jnp.cos(freqs), jnp.sin(freqs))
            q = q * cos * scale + rotate_half(q) * sin * scale
            k = k * cos / scale + rotate_half(k) * sin / scale
            return (q, k)

        def local_attention(q, k, v):
            b, h, n, d = q.shape
            w = n // WINDOW
            bq = q.reshape(b, h, w, WINDOW, d) * QK_SCALE
            bk = k.reshape(b, h, w, WINDOW, d)
            bv = v.reshape(b, h, w, WINDOW, d)

            def look_around(t):
                p = jnp.pad(t, ((0, 0), (0, 0), (1, 0), (0, 0), (0, 0)))
                return jnp.concatenate([p[:, :, :w], p[:, :, 1:]], axis=3)
            bk, bv = (look_around(bk), look_around(bv))
            bt = jnp.arange(n).reshape(w, WINDOW)
            btp = jnp.pad(bt, ((1, 0), (0, 0)), constant_values=-1)
            btk = jnp.concatenate([btp[:w], btp[1:]], axis=1)
            sim = jnp.einsum('bhwid,bhwjd->bhwij', bq, bk)
            i = bt[:, :, None]
            j = btk[:, None, :]
            mask = (i < j) | (i > j + WINDOW) | (j == -1)
            sim = jnp.where(mask, -jnp.finfo(sim.dtype).max, sim)
            attn = jax.nn.softmax(sim, axis=-1)
            out = jnp.einsum('bhwij,bhwjd->bhwid', attn, bv)
            return out.reshape(b, h, n, d)

        def _layer(x, wqkv, qs, ksc, wo, lg, lb, w1, b1, w2, b2):
            b, n, _ = x.shape
            h = shift_token(x)
            qkv = h @ wqkv
            q, k, v = jnp.split(qkv, 3, axis=-1)
            to_heads = lambda t: t.reshape(b, n, HEADS, DIM_HEAD).transpose(0, 2, 1, 3)
            q, k, v = (to_heads(q), to_heads(k), to_heads(v))
            q = l2norm(q) * qs
            k = l2norm(k) * ksc
            q, k = rotary_xpos(q, k)
            o = local_attention(q, k, v)
            o = o.transpose(0, 2, 1, 3).reshape(b, n, INNER)
            x = x + o @ wo
            h = shift_token(x)
            mu = h.mean(-1, keepdims=True)
            var = h.var(-1, keepdims=True)
            h = (h - mu) / jnp.sqrt(var + 1e-05) * lg + lb
            h = h @ w1 + b1
            a, g = jnp.split(h, 2, axis=-1)
            h = a * jax.nn.gelu(g, approximate=False)
            x = x + h @ w2 + b2
            return x
        key = jax.random.key(seed)
        ks = jax.random.split(key, 6)
        return {'x': jax.random.normal(ks[0], (B, N, DIM), jnp.float32), 'wqkv': jax.random.normal(ks[1], (DEPTH, DIM, 3 * INNER), jnp.float32) * 0.02, 'q_scale': jnp.ones((DEPTH, DIM_HEAD), jnp.float32), 'k_scale': jnp.ones((DEPTH, DIM_HEAD), jnp.float32), 'wo': jax.random.normal(ks[2], (DEPTH, INNER, DIM), jnp.float32) * 0.02, 'ln_g': jnp.ones((DEPTH, DIM), jnp.float32), 'ln_b': jnp.zeros((DEPTH, DIM), jnp.float32), 'w1': jax.random.normal(ks[3], (DEPTH, DIM, 2 * HID), jnp.float32) * 0.02, 'b1': jnp.zeros((DEPTH, 2 * HID), jnp.float32), 'w2': jax.random.normal(ks[4], (DEPTH, HID, DIM), jnp.float32) * 0.02, 'b2': jnp.zeros((DEPTH, DIM), jnp.float32)}
    _L0_ffn_in = _L0_ffn_setup()
    _d = {'L0_attn_x': _L0_attn_in['x'], 'L0_attn_Wq': _L0_attn_in['Wq'], 'L0_attn_Wk': _L0_attn_in['Wk'], 'L0_attn_Wv': _L0_attn_in['Wv'], 'L0_attn_Wg': _L0_attn_in['Wg'], 'L0_attn_Wo': _L0_attn_in['Wo'], 'L0_attn_bw': _L0_attn_in['bw'], 'L0_attn_bb': _L0_attn_in['bb'], 'L0_attn_gkw': _L0_attn_in['gkw'], 'L0_attn_gkb': _L0_attn_in['gkb'], 'L0_attn_qcw': _L0_attn_in['qcw'], 'L0_attn_qcb': _L0_attn_in['qcb'], 'L0_attn_kcw': _L0_attn_in['kcw'], 'L0_attn_kcb': _L0_attn_in['kcb'], 'L0_attn_vcw': _L0_attn_in['vcw'], 'L0_attn_vcb': _L0_attn_in['vcb'], 'L0_attn_A_log': _L0_attn_in['A_log'], 'L0_attn_D_param': _L0_attn_in['D_param'], 'L0_attn_dt_bias': _L0_attn_in['dt_bias'], 'L0_attn_onorm_w': _L0_attn_in['onorm_w'], 'L0_ffn_wqkv': _L0_ffn_in['wqkv'], 'L0_ffn_q_scale': _L0_ffn_in['q_scale'], 'L0_ffn_k_scale': _L0_ffn_in['k_scale'], 'L0_ffn_wo': _L0_ffn_in['wo'], 'L0_ffn_ln_g': _L0_ffn_in['ln_g'], 'L0_ffn_ln_b': _L0_ffn_in['ln_b'], 'L0_ffn_w1': _L0_ffn_in['w1'], 'L0_ffn_b1': _L0_ffn_in['b1'], 'L0_ffn_w2': _L0_ffn_in['w2'], 'L0_ffn_b2': _L0_ffn_in['b2']}
    _x0 = _d['L0_attn_x']
    _d['L0_attn_x'] = jax.random.normal(jax.random.fold_in(jax.random.key(seed), 1), (8, 512, 256), dtype=_x0.dtype)
    del _x0
    return _d

def reference(L0_attn_x, L0_attn_Wq, L0_attn_Wk, L0_attn_Wv, L0_attn_Wg, L0_attn_Wo, L0_attn_bw, L0_attn_bb, L0_attn_gkw, L0_attn_gkb, L0_attn_qcw, L0_attn_qcb, L0_attn_kcw, L0_attn_kcb, L0_attn_vcw, L0_attn_vcb, L0_attn_A_log, L0_attn_D_param, L0_attn_dt_bias, L0_attn_onorm_w, L0_ffn_wqkv, L0_ffn_q_scale, L0_ffn_k_scale, L0_ffn_wo, L0_ffn_ln_g, L0_ffn_ln_b, L0_ffn_w1, L0_ffn_b1, L0_ffn_w2, L0_ffn_b2):

    def _L0_attn_ref(x, Wq, Wk, Wv, Wg, Wo, bw, bb, gkw, gkb, qcw, qcb, kcw, kcb, vcw, vcb, A_log, D_param, dt_bias, onorm_w):
        import jax, jax.numpy as jnp
        import numpy as np
        B, T, HID, H, DH, K = (2, 256, 256, 16, 64, 4)
        ROPE_BASE = 10000.0
        EPS = 1e-06

        def _causal_dwconv(x, w, b):
            xc = jnp.transpose(x, (0, 2, 1))
            y = jax.lax.conv_general_dilated(xc, w, window_strides=(1,), padding=[(K - 1, 0)], dimension_numbers=('NCH', 'OIH', 'NCH'), feature_group_count=xc.shape[1])
            y = y + b[None, :, None]
            return jax.nn.silu(jnp.transpose(y, (0, 2, 1)))

        def _rope(x, cos, sin):
            c = cos[None, :, None, :]
            s = sin[None, :, None, :]
            x1, x2 = (x[..., ::2], x[..., 1::2])
            return jnp.concatenate([x1 * c[..., ::2] - x2 * s[..., ::2], x1 * s[..., ::2] + x2 * c[..., ::2]], axis=-1)

        def _delta_rule(q, k, v, alpha, beta, D_param):
            qs = jnp.moveaxis(q, 1, 0).astype(jnp.float32)
            ks = jnp.moveaxis(k, 1, 0).astype(jnp.float32)
            vs = jnp.moveaxis(v, 1, 0).astype(jnp.float32)
            als = jnp.moveaxis(alpha, 1, 0).astype(jnp.float32)
            bes = jnp.moveaxis(beta, 1, 0).astype(jnp.float32)

            def step(S, inp):
                qt, kt, vt, at, bt = inp
                ot = jnp.einsum('bhd,bhde->bhe', qt, S)
                ot = ot + D_param[None, :, None] * jnp.sum(qt * kt, -1, keepdims=True) * vt
                kS = jnp.einsum('bhd,bhde->bhe', kt, S)
                at_ = at[..., None, None]
                bt_ = bt[..., None, None]
                S_new = at_ * (S - bt_ * kt[..., :, None] * kS[..., None, :]) + bt_ * kt[..., :, None] * vt[..., None, :]
                return (S_new, ot)
            S0 = jnp.zeros((q.shape[0], H, DH, DH), jnp.float32)
            _, outs = jax.lax.scan(step, S0, (qs, ks, vs, als, bes))
            return jnp.moveaxis(outs, 0, 1)

        def _forward(x, Wq, Wk, Wv, Wg, Wo, bw, bb, gkw, gkb, qcw, qcb, kcw, kcb, vcw, vcb, A_log, D_param, dt_bias, onorm_w):
            Bb, Tt, _ = x.shape
            q = _causal_dwconv(x @ Wq, qcw, qcb).reshape(Bb, Tt, H, DH)
            k = _causal_dwconv(x @ Wk, kcw, kcb).reshape(Bb, Tt, H, DH)
            v = _causal_dwconv(x @ Wv, vcw, vcb).reshape(Bb, Tt, H, DH)
            t = jnp.arange(Tt, dtype=jnp.float32)
            inv_freq = 1.0 / ROPE_BASE ** (jnp.arange(0, DH, 2, dtype=jnp.float32) / DH)
            freqs = jnp.outer(t, inv_freq)
            emb = jnp.concatenate([freqs, freqs], -1)
            cos, sin = (jnp.cos(emb), jnp.sin(emb))
            q = _rope(q, cos, sin)
            k = _rope(k, cos, sin)
            q = q * jax.lax.rsqrt(jnp.sum(q * q, -1, keepdims=True) + EPS)
            k = k * jax.lax.rsqrt(jnp.sum(k * k, -1, keepdims=True) + EPS)
            beta = jax.nn.sigmoid(x @ bw + bb)
            alpha = jnp.exp(-jnp.exp(A_log) * jax.nn.softplus(x @ gkw + gkb + dt_bias))
            o = _delta_rule(q, k, v, alpha, beta, D_param)
            g = (x @ Wg).reshape(Bb, Tt, H, DH)
            on = o * jax.lax.rsqrt(jnp.mean(o * o, -1, keepdims=True) + EPS) * onorm_w
            o = g * jax.nn.silu(on)
            return o.reshape(Bb, Tt, H * DH) @ Wo
        return _forward(x, Wq, Wk, Wv, Wg, Wo, bw, bb, gkw, gkb, qcw, qcb, kcw, kcb, vcw, vcb, A_log, D_param, dt_bias, onorm_w)

    def _L0_ffn_ref(x, wqkv, q_scale, k_scale, wo, ln_g, ln_b, w1, b1, w2, b2):
        import jax, jax.numpy as jnp
        import numpy as np
        DIM = 256
        DEPTH = 2
        HEADS = 8
        DIM_HEAD = 64
        WINDOW = 128
        INNER = HEADS * DIM_HEAD
        HID = int(DIM * 4 * 2 / 3)
        B, N = (2, 2048)
        QK_SCALE = 8.0

        def shift_token(t):
            t1, t2 = jnp.split(t, 2, axis=-1)
            t2 = jnp.pad(t2, ((0, 0), (1, 0), (0, 0)))[:, :-1]
            return jnp.concatenate([t1, t2], axis=-1)

        def l2norm(t):
            return t / jnp.clip(jnp.linalg.norm(t, axis=-1, keepdims=True), 1e-12)

        def rotate_half(x):
            x1, x2 = jnp.split(x, 2, axis=-1)
            return jnp.concatenate([-x2, x1], axis=-1)

        def rotary_xpos(q, k):
            n = q.shape[-2]
            half_idx = jnp.arange(0, DIM_HEAD, 2, dtype=jnp.float32)
            inv_freq = 1.0 / 10000.0 ** (half_idx / DIM_HEAD)
            t = jnp.arange(n, dtype=jnp.float32)
            freqs = t[:, None] * inv_freq[None, :]
            freqs = jnp.concatenate([freqs, freqs], axis=-1)
            base = (half_idx + 0.4 * DIM_HEAD) / (1.4 * DIM_HEAD)
            power = (t - n // 2) / float(WINDOW // 2)
            scale = base[None, :] ** power[:, None]
            scale = jnp.concatenate([scale, scale], axis=-1)
            cos, sin = (jnp.cos(freqs), jnp.sin(freqs))
            q = q * cos * scale + rotate_half(q) * sin * scale
            k = k * cos / scale + rotate_half(k) * sin / scale
            return (q, k)

        def local_attention(q, k, v):
            b, h, n, d = q.shape
            w = n // WINDOW
            bq = q.reshape(b, h, w, WINDOW, d) * QK_SCALE
            bk = k.reshape(b, h, w, WINDOW, d)
            bv = v.reshape(b, h, w, WINDOW, d)

            def look_around(t):
                p = jnp.pad(t, ((0, 0), (0, 0), (1, 0), (0, 0), (0, 0)))
                return jnp.concatenate([p[:, :, :w], p[:, :, 1:]], axis=3)
            bk, bv = (look_around(bk), look_around(bv))
            bt = jnp.arange(n).reshape(w, WINDOW)
            btp = jnp.pad(bt, ((1, 0), (0, 0)), constant_values=-1)
            btk = jnp.concatenate([btp[:w], btp[1:]], axis=1)
            sim = jnp.einsum('bhwid,bhwjd->bhwij', bq, bk)
            i = bt[:, :, None]
            j = btk[:, None, :]
            mask = (i < j) | (i > j + WINDOW) | (j == -1)
            sim = jnp.where(mask, -jnp.finfo(sim.dtype).max, sim)
            attn = jax.nn.softmax(sim, axis=-1)
            out = jnp.einsum('bhwij,bhwjd->bhwid', attn, bv)
            return out.reshape(b, h, n, d)

        def _layer(x, wqkv, qs, ksc, wo, lg, lb, w1, b1, w2, b2):
            b, n, _ = x.shape
            h = shift_token(x)
            qkv = h @ wqkv
            q, k, v = jnp.split(qkv, 3, axis=-1)
            to_heads = lambda t: t.reshape(b, n, HEADS, DIM_HEAD).transpose(0, 2, 1, 3)
            q, k, v = (to_heads(q), to_heads(k), to_heads(v))
            q = l2norm(q) * qs
            k = l2norm(k) * ksc
            q, k = rotary_xpos(q, k)
            o = local_attention(q, k, v)
            o = o.transpose(0, 2, 1, 3).reshape(b, n, INNER)
            x = x + o @ wo
            h = shift_token(x)
            mu = h.mean(-1, keepdims=True)
            var = h.var(-1, keepdims=True)
            h = (h - mu) / jnp.sqrt(var + 1e-05) * lg + lb
            h = h @ w1 + b1
            a, g = jnp.split(h, 2, axis=-1)
            h = a * jax.nn.gelu(g, approximate=False)
            x = x + h @ w2 + b2
            return x
        for l in range(DEPTH):
            x = _layer(x, wqkv[l], q_scale[l], k_scale[l], wo[l], ln_g[l], ln_b[l], w1[l], b1[l], w2[l], b2[l])
        return x
    x = L0_attn_x
    xn = _layernorm(x, axis=-1)
    s = _L0_attn_ref(xn, L0_attn_Wq, L0_attn_Wk, L0_attn_Wv, L0_attn_Wg, L0_attn_Wo, L0_attn_bw, L0_attn_bb, L0_attn_gkw, L0_attn_gkb, L0_attn_qcw, L0_attn_qcb, L0_attn_kcw, L0_attn_kcb, L0_attn_vcw, L0_attn_vcb, L0_attn_A_log, L0_attn_D_param, L0_attn_dt_bias, L0_attn_onorm_w)
    g = _silu(_L0_ffn_ref(xn, L0_ffn_wqkv, L0_ffn_q_scale, L0_ffn_k_scale, L0_ffn_wo, L0_ffn_ln_g, L0_ffn_ln_b, L0_ffn_w1, L0_ffn_b1, L0_ffn_w2, L0_ffn_b2))
    x = x + s * g
    return x

_drawn_inputs = setup_inputs


def setup_inputs(seed=0):
    import zlib

    import numpy as np

    out = dict(_drawn_inputs(seed))
    spreads = {'L0_attn_bb': (0.0, 0.8),
     'L0_attn_gkb': (0.0, 0.8),
     'L0_attn_qcb': (0.0, 0.1),
     'L0_attn_kcb': (0.0, 0.1),
     'L0_attn_vcb': (0.0, 0.1),
     'L0_attn_D_param': (1.0, 0.6),
     'L0_attn_onorm_w': (1.0, 0.6),
     'L0_ffn_q_scale': (1.0, 0.6),
     'L0_ffn_k_scale': (1.0, 0.6),
     'L0_ffn_ln_g': (1.0, 0.6),
     'L0_ffn_ln_b': (0.0, 0.8),
     'L0_ffn_b1': (0.0, 0.8),
     'L0_ffn_b2': (0.0, 0.761)}
    factors = {'L0_attn_bw': 8.0,
     'L0_attn_gkw': 8.0,
     'L0_attn_A_log': 6.76,
     'L0_attn_dt_bias': 8.0,
     'L0_ffn_wqkv': 8.0,
     'L0_ffn_wo': 8.0,
     'L0_ffn_w1': 8.0,
     'L0_ffn_w2': 8.0}
    for name, (base, spread) in spreads.items():
        noise = np.random.default_rng([zlib.crc32(name.encode()), seed]).standard_normal(out[name].shape)
        drawn = base * np.exp(spread * noise) if base else spread * noise
        out[name] = jnp.asarray(drawn.astype(out[name].dtype))
    for name, factor in factors.items():
        out[name] = (out[name] * factor).astype(out[name].dtype)
    return out
```

```python
import numpy as np
import concourse.bass as bass
from concourse import mybir
from contextlib import ExitStack

F32 = mybir.dt.float32
ALU = mybir.AluOpType
ACT = mybir.ActivationFunctionType
AX = mybir.AxisListType

B, T, D = 8, 512, 256
P = 128
NT = T // P
KC = D // P
LAYERS, FH, DH = 2, 8, 64
INNER = FH * DH
HID = int(D * 4 * 2 / 3)
HM = -(-HID // P)
HROWS = [min(P, HID - m * P) for m in range(HM)]
PAIRS = FH // 2
LN_EPS = 1e-5
NEG = -1e30
W1C = 2 * HID


def ffn_phase(nc, ctx, io, scratch):

    def sb(name, shape):
        return ctx.enter_context(nc.sbuf_tensor("f_" + name, shape, F32))

    sems = []

    def sem(name):
        sems.append(ctx.enter_context(nc.semaphore("f_" + name)))
        return sems[-1]

    wqkv = sb("wqkv", [P, LAYERS, KC, 3 * INNER])
    wo = sb("wo", [P, LAYERS, PAIRS, D])
    w1 = sb("w1", [P, LAYERS, KC, W1C])
    w2 = sb("w2", [P, LAYERS, HM, D])
    b1 = sb("b1", [P, LAYERS, 2, HM])
    vecs = sb("vecs", [P, LAYERS, 3, KC])
    scales = sb("scales", [P, LAYERS, 4, DH])
    trig = sb("trig", [P, NT, 4, DH])
    rope = sb("rope", [P, LAYERS, NT, 4, DH])
    ident = sb("ident", [P, P])
    mask = sb("mask", [P, 2 * P])
    mean_w = sb("mean_w", [P, P])

    xin = sb("xin", [P, NT, D])
    xnorm = sb("xnorm", [P, NT, D])
    stats = sb("stats", [P, NT, 6])
    mv = sb("mv", [P, NT, 2])
    rstd = sb("rstd", [P, NT])
    nmr = sb("nmr", [P, NT])
    xT = sb("xT", [P, KC, T + 2])
    qk = sb("qk", [P, NT, 2, INNER])
    v = sb("v", [P, NT, INNER])
    m1 = sb("m1", [P, 2, INNER])
    m2 = sb("m2", [P, 2, INNER])
    sq = sb("sq", [P, 2, INNER])
    ssq = sb("ssq", [P, NT, 2, FH])
    nrm = sb("nrm", [P, NT, 2, FH])
    rn = sb("rn", [P, NT, 2, FH])
    qsc = sb("qsc", [P, 2, NT, FH])
    qT = sb("qT", [P, PAIRS, T])
    kT = sb("kT", [P, PAIRS, T])
    sm = sb("sm", [P, 2, 2, 2 * P])
    pr = sb("pr", [P, 2, 2, 2 * P])
    mx = sb("mx", [P, 2, 2])
    nb = sb("nb", [P, 2, 2])
    rsum = sb("rsum", [P, NT, FH])
    rinv = sb("rinv", [P, NT, FH])
    pT = sb("pT", [P, 2, 4, P])
    osb = sb("osb", [P, 2, INNER])
    oT = sb("oT", [P, PAIRS, T])
    xc, xsq = m1, m2
    std = sb("std", [P, T])
    rst = sb("rst", [P, T])
    xh = sq
    hn = sb("hn", [P, KC, T])
    gact = sb("gact", [P, 2, T])
    hh = qk[:, :, :, :].rearrange("p w k n -> p (w k) n")
    gate = sb("gate", [P, KC, T])
    ps = ctx.enter_context(nc.psum_tensor("f_ps", [P, 8, 512], F32))

    loaded = sem("loaded")
    x_in = sem("x_in")
    xn_st = sem("xn_st")
    gate_st = sem("gate_st")
    rope_rdy = sem("rope_rdy")
    zero_rdy = sem("zero_rdy")
    ln_step = sem("ln_step")
    ln_std = sem("ln_std")
    xn_rdy = sem("xn_rdy")
    xnT_ps = sem("xnT_ps")
    xT_rdy = sem("xT_rdy")
    qkv_ps = sem("qkv_ps")
    qkv_act = sem("qkv_act")
    rot_m = sem("rot_m")
    rot_mid = sem("rot_mid")
    rot_rdy = sem("rot_rdy")
    ssq_rdy = sem("ssq_rdy")
    nrm_rdy = sem("nrm_rdy")
    rn_step = sem("rn_step")
    k_rdy = sem("k_rdy")
    qkT_ps = sem("qkT_ps")
    qkT_rdy = sem("qkT_rdy")
    sc_ps = sem("sc_ps")
    sm_rdy = sem("sm_rdy")
    nb_rdy = sem("nb_rdy")
    pr_rdy = sem("pr_rdy")
    pT_ps = sem("pT_ps")
    pT_rdy = sem("pT_rdy")
    o_ps = sem("o_ps")
    ri_rdy = sem("ri_rdy")
    o_rdy = sem("o_rdy")
    oT_ps = sem("oT_ps")
    oT_rdy = sem("oT_rdy")
    wo_ps = sem("wo_ps")
    x1_rdy = sem("x1_rdy")
    mean_ps = sem("mean_ps")
    xc_rdy = sem("xc_rdy")
    xsq_rdy = sem("xsq_rdy")
    var_ps = sem("var_ps")
    std_rdy = sem("std_rdy")
    rst_rdy = sem("rst_rdy")
    xh_rdy = sem("xh_rdy")
    hn_rdy = sem("hn_rdy")
    up_ps = sem("up_ps")
    g_rdy = sem("g_rdy")
    hh_rdy = sem("hh_rdy")
    dn_ps = sem("dn_ps")
    x2_rdy = sem("x2_rdy")
    gate_rdy = sem("gate_rdy")
    passed = sem("passed")
    bn_rdy = sem("bn_rdy")
    eps_t = sb("eps", [P, 1])
    eps_ap = eps_t[:, 0:1]

    loads = [(wqkv, io["wqkv"]), (wo, io["wo"]), (w1, io["w1"]), (w2, io["w2"]), (b1, io["b1"]), (vecs, io["vecs"]),
             (scales, io["scales"]), (trig, io["trig"]), (ident, io["ident"]), (mask, io["mask"]), (mean_w, io["mean_w"])]
    LOADED = 16 * len(loads)

    block = ctx.enter_context(nc.Block())

    def flat(t):
        return t[(slice(None),) * len(t.shape)]

    @block.sync
    def _(sp):
        for x in sems:
            sp.sem_inc(x, 1)
        sp.dma_start(flat(xin), io["x"][0, :, :, :]).then_inc(x_in, 16)
        for dst, src in loads[::-1]:
            sp.dma_start(flat(dst), src).then_inc(loaded, 16)
        def store(b):
            sp.wait_ge(xT_rdy, 1 + b * KC + KC)
            sp.sem_inc(passed, 1)
            sp.dma_start(scratch["xnT"][b, :, :, :], xT[:, :, 1:T + 1]).then_inc(xn_st, 16)

        def store_gate(b):
            sp.wait_ge(gate_rdy, 1 + b * KC + KC)
            sp.sem_inc(passed, 1)
            sp.dma_start(scratch["gate"][b, :, :, :], flat(gate)).then_inc(gate_st, 16)

        with sp.Fori(0, B - 1) as b:
            store(b)
            sp.wait_ge(xn_rdy, 1 + b * NT + NT)
            sp.sem_inc(passed, 1)
            sp.dma_start(flat(xin), io["x"][b + 1, :, :, :]).then_inc(x_in, 16)
            store_gate(b)
        store(B - 1)
        store_gate(B - 1)
        sp.wait_ge(xn_st, 1 + B * 16)
        sp.dma_start(scratch["xnT"][B, :, :, :], scratch["xnT"][0, :, :, :]).then_inc(xn_st, 16)
        sp.wait_ge(xn_st, 1 + (B + 1) * 16)
        sp.wait_ge(gate_st, 1 + B * 16)

    @block.gpsimd
    def _(pool):
        nc.gpsimd.memset(xT[:, :, 0:1], 0.0).then_inc(zero_rdy, 1)
        with pool.Fori(0, B) as b:
            for l in range(LAYERS):
                it = b * LAYERS + l
                for n in range(2 * NT):
                    w, part = n // 2, n % 2
                    pool.wait_ge(rot_m, 1 + it * 2 * NT + n + 1)
                    if n == 0:
                        pool.wait_ge(qkT_ps, 1 + it * 2 * NT)
                    nc.gpsimd.tensor_tensor(qk[:, w, part, :], m1[:, n % 2, :], m2[:, n % 2, :],
                                            ALU.add).then_inc(rot_rdy, 1)
                pool.wait_ge(rn_step, 1 + it * 4 + 4)
                pool.wait_ge(rot_rdy, 1 + it * 2 * NT + 2 * NT)
                for w in range(NT):
                    kw = qk[:, w, 1, :].rearrange("p (h d) -> p h d", h=FH)
                    nc.gpsimd.tensor_tensor(kw, kw, rn[:, w, 1, :].rearrange("p (h o) -> p h o", o=1)
                                            .to_broadcast([P, FH, DH]), ALU.mult).then_inc(k_rdy, 1)

    def evac_oT(act, it, w):
        act.wait_ge(oT_ps, 1 + it * NT + w + 1)
        if w == 0:
            act.wait_ge(wo_ps, 1 + it * KC)
        nc.scalar.activation(oT[:, :, w * P:(w + 1) * P], ps[:, 7, :].rearrange("p (a t) -> p a t", a=PAIRS),
                             ACT.Copy).then_inc(oT_rdy, 1)

    @block.scalar
    def _(act):
        act.wait_ge(loaded, 1 + LOADED)
        with act.Fori(0, B) as b:
            act.wait_ge(ln_step, 1 + b * 5 + 1)
            nc.scalar.activation(rstd[:, :], mv[:, :, 1], ACT.Sqrt).then_inc(ln_std, 1)
            for c in range(KC):
                act.wait_ge(xnT_ps, 1 + b * KC + c + 1)
                if c == 0:
                    act.wait_ge(gate_rdy, 1 + b * KC)
                    act.wait_ge(zero_rdy, 1 + 1)
                nc.scalar.activation(xT[:, c, 1:T + 1], ps[:, 6 + c, :], ACT.Copy).then_inc(xT_rdy, 1)
            for l in range(LAYERS):
                it = b * LAYERS + l
                for n in range(3 * NT):
                    w, part = n // 3, n % 3
                    act.wait_ge(qkv_ps, 1 + it * 3 * NT + n + 1)
                    src = ps[:, n % 4, :]
                    if part < 2:
                        i = 2 * w + part
                        act.wait_ge(ssq_rdy, 1 + it * 2 * NT + max(0, i - 1))
                        act.wait_ge(rot_m, 1 + it * 2 * NT + i + 1)
                        nc.scalar.activation(sq[:, i % 2, :], src, ACT.Square).then_inc(qkv_act, 1)
                    else:
                        if w == 0:
                            act.wait_ge(o_ps, 1 + it * PAIRS * NT)
                        nc.scalar.activation(v[:, w, :], src, ACT.Copy).then_inc(qkv_act, 1)
                act.wait_ge(ssq_rdy, 1 + it * 2 * NT + 2 * NT)
                nc.scalar.activation(flat(nrm), flat(ssq), ACT.Sqrt).then_inc(nrm_rdy, 1)
                for n in range(2 * NT):
                    part, w = n // NT, n % NT
                    act.wait_ge(qkT_ps, 1 + it * 2 * NT + n + 1)
                    dst = (qT, kT)[part]
                    if n == 0:
                        act.wait_ge(sc_ps, 1 + it * PAIRS * NT)
                    nc.scalar.activation(dst[:, :, w * P:(w + 1) * P],
                                         ps[:, 4 + n % 2, :].rearrange("p (a t) -> p a t", a=PAIRS),
                                         ACT.Copy).then_inc(qkT_rdy, 1)
                for u in range(NT * PAIRS):
                    w = u // PAIRS
                    act.wait_ge(nb_rdy, 1 + it * NT * PAIRS + u + 1)
                    act.wait_ge(pT_ps, 1 + it * NT * PAIRS + max(0, u - 1))
                    k0 = P if w == 0 else 0
                    for j in range(2):
                        h = 2 * (u % PAIRS) + j
                        if u == 0 and j == 0:
                            act.wait_ge(o_rdy, 1 + it * NT)
                        nc.scalar.activation(pr[:, u % 2, j, k0:], sm[:, u % 2, j, k0:], ACT.Exp,
                                             bias=nb[:, u % 2, j:j + 1], scale=qsc[:, 0, w, h:h + 1],
                                             accum_out=rsum[:, w, h:h + 1]).then_inc(pr_rdy, 1)
                    if u % PAIRS == PAIRS - 1 and w > 0:
                        evac_oT(act, it, w - 1)
                evac_oT(act, it, NT - 1)
                for c in range(KC):
                    act.wait_ge(xc_rdy, 1 + it * KC + c + 1)
                    nc.scalar.activation(xsq[:, c, :], xc[:, c, :], ACT.Square).then_inc(xsq_rdy, 1)
                act.wait_ge(var_ps, 1 + it + 1)
                nc.scalar.activation(std[:, :], ps[:, 3, :], ACT.Sqrt, bias=eps_ap).then_inc(std_rdy, 1)
                for c in range(KC):
                    act.wait_ge(xh_rdy, 1 + it * KC + c + 1)
                    if c == 0:
                        act.wait_ge(up_ps, 1 + it * HM)
                    nc.scalar.activation(hn[:, c, :], xh[:, c, :], ACT.Identity, bias=vecs[:, l, 1, c:c + 1],
                                         scale=vecs[:, l, 0, c:c + 1]).then_inc(hn_rdy, 1)
                for m in range(HM):
                    r = HROWS[m]
                    act.wait_ge(up_ps, 1 + it * HM + m + 1)
                    act.wait_ge(hh_rdy, 1 + it * HM + max(0, m - 1))
                    nc.scalar.activation(gact[:r, m % 2, :], ps[:r, 5 + 2 * (m % 2), :], ACT.Gelu,
                                         bias=b1[:r, l, 1, m:m + 1]).then_inc(g_rdy, 1)
            for c in range(KC):
                act.wait_ge(x2_rdy, 1 + b * LAYERS * KC + (LAYERS - 1) * KC + c + 1)
                if c == 0:
                    act.wait_ge(gate_st, 1 + b * 16)
                nc.scalar.activation(gate[:, c, :], xT[:, c, 1:T + 1], ACT.Silu).then_inc(gate_rdy, 1)

    @block.vector
    def _(dve):
        nc.vector.memset(eps_t[:, :], LN_EPS).then_inc(rope_rdy, 1)
        dve.wait_ge(loaded, 1 + LOADED)
        for l in range(LAYERS):
            for k in range(4):
                nc.vector.tensor_tensor(rope[:, l, :, k, :], trig[:, :, k, :],
                                        scales[:, l, k:k + 1, :].to_broadcast([P, NT, DH]),
                                        ALU.mult).then_inc(rope_rdy, 1)
        dve.wait_ge(rope_rdy, 1 + 4 * LAYERS + 1)
        with dve.Fori(0, B) as b:
            dve.wait_ge(x_in, 1 + b * 16 + 16)
            for w in range(NT):
                nc.vector.bn_stats(stats[:, w, :], xin[:, w, :]).then_inc(bn_rdy, 1)
            dve.wait_ge(bn_rdy, 1 + b * 2 * NT + NT)
            dve.sem_inc(passed, 1)
            for w in range(NT):
                nc.vector.bn_aggr(mv[:, w, :], stats[:, w, :]).then_inc(bn_rdy, 1)
            dve.wait_ge(bn_rdy, 1 + b * 2 * NT + 2 * NT)
            nc.vector.tensor_scalar(mv[:, :, 1], mv[:, :, 1], LN_EPS, None, ALU.add).then_inc(ln_step, 1)
            dve.wait_ge(ln_std, 1 + b + 1)
            nc.vector.reciprocal(rstd[:, :], rstd[:, :]).then_inc(ln_step, 1)
            dve.wait_ge(ln_step, 1 + b * 5 + 2)
            nc.vector.tensor_tensor(nmr[:, :], mv[:, :, 0], rstd[:, :], ALU.mult).then_inc(ln_step, 1)
            dve.wait_ge(ln_step, 1 + b * 5 + 3)
            nc.vector.tensor_scalar(nmr[:, :], nmr[:, :], -1.0, None, ALU.mult).then_inc(ln_step, 2)
            dve.wait_ge(ln_step, 1 + b * 5 + 5)
            dve.wait_ge(xnT_ps, 1 + b * KC)
            for w in range(NT):
                nc.vector.tensor_scalar(xnorm[:, w, :], xin[:, w, :], mv[:, w, 0:1], rstd[:, w:w + 1],
                                        ALU.subtract, ALU.mult).then_inc(xn_rdy, 1)
            for l in range(LAYERS):
                it = b * LAYERS + l
                for n in range(2 * NT):
                    w, part = n // 2, n % 2
                    bank = (3 * w + part) % 4
                    dve.wait_ge(qkv_ps, 1 + it * 3 * NT + 3 * w + part + 1)
                    dve.wait_ge(rot_rdy, 1 + it * 2 * NT + max(0, n - 1))
                    src = ps[:, bank, :].rearrange("p (h d) -> p h d", h=FH)
                    a = m1[:, n % 2, :].rearrange("p (h d) -> p h d", h=FH)
                    c = m2[:, n % 2, :].rearrange("p (h d) -> p h d", h=FH)
                    H2 = DH // 2
                    nc.vector.tensor_tensor(a, src, rope[:, l, w, 2 * part:2 * part + 1, :]
                                            .to_broadcast([P, FH, DH]), ALU.mult).then_inc(rot_mid, 1)
                    nc.vector.tensor_tensor(c[:, :, 0:H2], src[:, :, H2:], rope[:, l, w, 2 * part + 1:2 * part + 2, 0:H2]
                                            .to_broadcast([P, FH, H2]), ALU.mult).then_inc(rot_mid, 1)
                    nc.vector.tensor_tensor(c[:, :, H2:], src[:, :, 0:H2], rope[:, l, w, 2 * part + 1:2 * part + 2, H2:]
                                            .to_broadcast([P, FH, H2]), ALU.mult).then_inc(rot_m, 1)
                    dve.wait_ge(qkv_act, 1 + it * 3 * NT + 3 * w + part + 1)
                    if n == 0:
                        dve.wait_ge(nrm_rdy, 1 + it)
                    nc.vector.tensor_reduce(ssq[:, w, part, :], sq[:, n % 2, :].rearrange("p (h d) -> p h d", h=FH),
                                            AX.X, ALU.add).then_inc(ssq_rdy, 1)
                dve.wait_ge(nrm_rdy, 1 + it + 1)
                nc.vector.tensor_scalar(flat(nrm), flat(nrm), 1e-12, None, ALU.max).then_inc(rn_step, 1)
                dve.wait_ge(rn_step, 1 + it * 4 + 1)
                dve.wait_ge(k_rdy, 1 + it * NT)
                nc.vector.reciprocal(flat(rn), flat(nrm)).then_inc(rn_step, 1)
                dve.wait_ge(rn_step, 1 + it * 4 + 2)
                dve.wait_ge(pr_rdy, 1 + it * FH * NT)
                nc.vector.tensor_scalar(qsc[:, 0, :, :], rn[:, :, 0, :], 8.0, None, ALU.mult).then_inc(rn_step, 1)
                nc.vector.tensor_scalar(qsc[:, 1, :, :], rn[:, :, 0, :], -8.0, None, ALU.mult).then_inc(rn_step, 1)
                dve.wait_ge(rn_step, 1 + it * 4 + 4)

                def masked_max(u):
                    w = u // PAIRS
                    k0 = P if w == 0 else 0
                    dve.wait_ge(sc_ps, 1 + it * NT * PAIRS + u + 1)
                    dve.wait_ge(pr_rdy, 1 + it * NT * FH + max(0, 2 * (u - 1)))
                    dve.sem_inc(passed, 1)
                    for j in range(2):
                        nc.vector.tensor_tensor_reduce(
                            out=sm[:, u % 2, j, k0:], in0=ps[:, 2 * (u % 2) + j, k0:2 * P],
                            in1=mask[:, k0:], scale=1.0, scalar=-3e38, op0=ALU.add, op1=ALU.max,
                            accum_out=mx[:, u % 2, j:j + 1]).then_inc(sm_rdy, 1)
                    dve.wait_ge(sm_rdy, 1 + it * NT * FH + 2 * u + 2)
                    h = 2 * (u % PAIRS)
                    nc.vector.tensor_tensor(nb[:, u % 2, :], mx[:, u % 2, :], qsc[:, 1, w, h:h + 2],
                                            ALU.mult).then_inc(nb_rdy, 1)

                def evac_pT(u):
                    w = u // PAIRS
                    dve.wait_ge(pT_ps, 1 + it * NT * PAIRS + u + 1)
                    dve.wait_ge(o_ps, 1 + it * NT * PAIRS + max(0, u - 1))
                    k0 = 1 if w == 0 else 0
                    nc.vector.tensor_copy(pT[:, u % 2, :, :].rearrange("p (j k) t -> p j k t", j=2)[:, :, k0:, :],
                                          ps[:, 4 + u % 2, :].rearrange("p (j k t) -> p j k t", j=2, k=2)[:, :, k0:, :]
                                          ).then_inc(pT_rdy, 1)

                def window_out(w):
                    dve.wait_ge(pr_rdy, 1 + it * NT * FH + FH * (w + 1))
                    nc.vector.reciprocal(rinv[:, w, :], rsum[:, w, :]).then_inc(ri_rdy, 1)
                    dve.wait_ge(ri_rdy, 1 + it * NT + w + 1)
                    dve.wait_ge(o_ps, 1 + it * NT * PAIRS + PAIRS * (w + 1))
                    dve.wait_ge(oT_ps, 1 + it * NT + max(0, w - 1))
                    nc.vector.tensor_tensor(osb[:, w % 2, :].rearrange("p (h d) -> p h d", h=FH),
                                            ps[:, 6, :].rearrange("p (h d) -> p h d", h=FH),
                                            rinv[:, w, :].rearrange("p (h o) -> p h o", o=1)
                                            .to_broadcast([P, FH, DH]), ALU.mult).then_inc(o_rdy, 1)

                U = NT * PAIRS
                masked_max(0)
                masked_max(1)
                for u in range(U):
                    evac_pT(u)
                    if u + 2 < U:
                        masked_max(u + 2)
                    if u % PAIRS == PAIRS - 1:
                        window_out(u // PAIRS)
                if l == 0:
                    dve.wait_ge(xn_st, 1 + b * 16 + 16)
                for c in range(KC):
                    dve.wait_ge(wo_ps, 1 + it * KC + c + 1)
                    nc.vector.tensor_tensor(xT[:, c, 1:T + 1], xT[:, c, 1:T + 1], ps[:, c, :],
                                            ALU.add).then_inc(x1_rdy, 1)
                dve.wait_ge(x1_rdy, 1 + it * KC + KC)
                dve.wait_ge(mean_ps, 1 + it + 1)
                for c in range(KC):
                    nc.vector.tensor_tensor(xc[:, c, :], xT[:, c, 1 - c:T + 1 - c], ps[:, 2, :],
                                            ALU.subtract).then_inc(xc_rdy, 1)
                dve.wait_ge(std_rdy, 1 + it + 1)
                nc.vector.reciprocal(rst[:, :], std[:, :]).then_inc(rst_rdy, 1)
                dve.wait_ge(rst_rdy, 1 + it + 1)
                dve.wait_ge(hn_rdy, 1 + it * KC)
                for c in range(KC):
                    nc.vector.tensor_tensor(xh[:, c, :], xc[:, c, :], rst[:, :], ALU.mult).then_inc(xh_rdy, 1)
                for m in range(HM):
                    r = HROWS[m]
                    dve.wait_ge(g_rdy, 1 + it * HM + m + 1)
                    nc.vector.scalar_tensor_tensor(out=hh[:r, m, :], in0=ps[:r, 4 + 2 * (m % 2), :],
                                                   scalar=b1[:r, l, 0, m:m + 1], in1=gact[:r, m % 2, :],
                                                   op0=ALU.add, op1=ALU.mult).then_inc(hh_rdy, 1)
                for c in range(KC):
                    dve.wait_ge(dn_ps, 1 + it * KC + c + 1)
                    nc.vector.scalar_tensor_tensor(out=xT[:, c, 1:T + 1], in0=ps[:, c, :],
                                                   scalar=vecs[:, l, 2, c:c + 1], in1=xT[:, c, 1:T + 1],
                                                   op0=ALU.add, op1=ALU.add).then_inc(x2_rdy, 1)
                dve.wait_ge(x2_rdy, 1 + it * KC + KC)

    @block.tensor
    def _(pe):
        pe.wait_ge(loaded, 1 + LOADED)
        mm = nc.tensor.matmul

        def shifted(c, t0, t1):
            return xT[:, c, 1 - c + t0:1 - c + t1]

        with pe.Fori(0, B) as b:
            for c in range(KC):
                if c == 0:
                    pe.wait_ge(x2_rdy, 1 + b * LAYERS * KC)
                    pe.wait_ge(xn_rdy, 1 + b * NT + NT)
                for w in range(NT):
                    last = nc.tensor.transpose(ps[:, 6 + c, w * P:(w + 1) * P], xnorm[:, w, c * P:(c + 1) * P], ident[:, :])
                last.then_inc(xnT_ps, 1)
            for l in range(LAYERS):
                it = b * LAYERS + l
                if l == 0:
                    pe.wait_ge(xT_rdy, 1 + b * KC + KC)
                pe.wait_ge(x2_rdy, 1 + it * KC)
                for n in range(3 * NT):
                    w, part = n // 3, n % 3
                    if n >= 4:
                        pe.wait_ge(qkv_act, 1 + it * 3 * NT + n - 3)
                        pe.wait_ge(rot_m, 1 + it * 2 * NT + 2 * ((n - 3) // 3) + min((n - 3) % 3, 2))
                    for c in range(KC):
                        last = mm(ps[:, n % 4, :], shifted(c, w * P, (w + 1) * P),
                                  wqkv[:, l, c, part * INNER:(part + 1) * INNER], start=c == 0, stop=c == KC - 1)
                    last.then_inc(qkv_ps, 1)
                for n in range(2 * NT):
                    part, w = n // NT, n % NT
                    if part == 0:
                        pe.wait_ge(rot_rdy, 1 + it * 2 * NT + 2 * w + 1)
                    else:
                        pe.wait_ge(k_rdy, 1 + it * NT + w + 1)
                    pe.wait_ge(qkT_rdy, 1 + it * 2 * NT + max(0, n - 1))
                    for a in range(PAIRS):
                        last = nc.tensor.transpose(ps[:, 4 + n % 2, a * P:(a + 1) * P],
                                                   qk[:, w, part, a * P:(a + 1) * P], ident[:, :])
                    last.then_inc(qkT_ps, 1)

                def scores(u):
                    w, a = u // PAIRS, u % PAIRS
                    if u < 2:
                        pe.wait_ge(qkv_act, 1 + it * 3 * NT + 3 * NT)
                        pe.wait_ge(rot_m, 1 + it * 2 * NT + 2 * NT)
                        pe.wait_ge(qkT_rdy, 1 + it * 2 * NT + 2 * NT)
                    else:
                        pe.wait_ge(sm_rdy, 1 + it * NT * FH + 2 * (u - 1))
                    k0 = P if w == 0 else 0
                    for j in range(2):
                        rows = slice(j * DH, (j + 1) * DH)
                        last = mm(ps[:, 2 * (u % 2) + j, k0:2 * P], qT[rows, a, w * P:(w + 1) * P],
                                  kT[rows, a, (w - 1) * P + k0:(w + 1) * P], start=True, stop=True)
                    last.then_inc(sc_ps, 1)

                def transpose_p(u):
                    w = u // PAIRS
                    pe.wait_ge(pr_rdy, 1 + it * NT * FH + 2 * u + 2)
                    pe.wait_ge(pT_rdy, 1 + it * NT * PAIRS + max(0, u - 1))
                    for j in range(2):
                        for k in range(1 if w == 0 else 0, 2):
                            last = nc.tensor.transpose(ps[:, 4 + u % 2, (2 * j + k) * P:(2 * j + k + 1) * P],
                                                       pr[:, u % 2, j, k * P:(k + 1) * P], ident[:, :])
                    last.then_inc(pT_ps, 1)

                def weigh_v(u):
                    w, a = u // PAIRS, u % PAIRS
                    pe.wait_ge(pT_rdy, 1 + it * NT * PAIRS + u + 1)
                    if a == 0:
                        pe.wait_ge(o_rdy, 1 + it * NT + w)
                    k0 = 1 if w == 0 else 0
                    for j in range(2):
                        h = 2 * a + j
                        for k in range(k0, 2):
                            last = mm(ps[:, 6, h * DH:(h + 1) * DH], pT[:, u % 2, 2 * j + k, :],
                                      v[:, w - 1 + k, h * DH:(h + 1) * DH], start=k == k0, stop=k == 1)
                    last.then_inc(o_ps, 1)

                def transpose_o(w):
                    pe.wait_ge(o_rdy, 1 + it * NT + w + 1)
                    if w == 0:
                        pe.wait_ge(x2_rdy, 1 + it * KC)
                    pe.wait_ge(oT_rdy, 1 + it * NT + w)
                    for a in range(PAIRS):
                        last = nc.tensor.transpose(ps[:, 7, a * P:(a + 1) * P], osb[:, w % 2, a * P:(a + 1) * P], ident[:, :])
                    last.then_inc(oT_ps, 1)

                U = NT * PAIRS
                scores(0)
                scores(1)
                for u in range(U):
                    if u == 0:
                        transpose_p(0)
                    if u + 2 < U:
                        scores(u + 2)
                    if u + 1 < U:
                        transpose_p(u + 1)
                    weigh_v(u)
                    if u % PAIRS == 0 and u > 0:
                        transpose_o(u // PAIRS - 1)
                transpose_o(NT - 1)
                pe.wait_ge(oT_rdy, 1 + it * NT + NT)
                pe.wait_ge(sm_rdy, 1 + it * NT * FH + NT * FH)
                for c in range(KC):
                    for a in range(PAIRS):
                        last = mm(ps[:, c, :], wo[:, l, a, c * P:(c + 1) * P], oT[:, a, :], start=a == 0, stop=a == PAIRS - 1)
                    last.then_inc(wo_ps, 1)
                for c in range(KC):
                    pe.wait_ge(x1_rdy, 1 + it * KC + c + 1)
                    last = mm(ps[:, 2, :], mean_w[:, :], shifted(c, 0, T), start=c == 0, stop=c == KC - 1)
                last.then_inc(mean_ps, 1)
                for c in range(KC):
                    pe.wait_ge(xsq_rdy, 1 + it * KC + c + 1)
                    last = mm(ps[:, 3, :], mean_w[:, :], xsq[:, c, :], start=c == 0, stop=c == KC - 1)
                last.then_inc(var_ps, 1)
                pe.wait_ge(hn_rdy, 1 + it * KC + KC)
                for m in range(HM):
                    r = HROWS[m]
                    if m >= 2:
                        pe.wait_ge(hh_rdy, 1 + it * HM + m - 1)
                    for part in range(2):
                        for c in range(KC):
                            last = mm(ps[:r, 4 + 2 * (m % 2) + part, :],
                                      w1[:, l, c, part * HID + m * P:part * HID + m * P + r], hn[:, c, :],
                                      start=c == 0, stop=c == KC - 1)
                    last.then_inc(up_ps, 1)
                for c in range(KC):
                    for m in range(HM):
                        r = HROWS[m]
                        if c == 0:
                            pe.wait_ge(hh_rdy, 1 + it * HM + m + 1)
                        last = mm(ps[:, c, :], w2[:r, l, m, c * P:(c + 1) * P], hh[:r, m, :], start=m == 0, stop=m == HM - 1)
                    last.then_inc(dn_ps, 1)


def ffn_constants():
    i = np.arange(0, DH, 2, dtype=np.float32)
    inv = (1.0 / 10000.0 ** (i / DH)).astype(np.float32)
    t = np.arange(T, dtype=np.float32)
    fr = t[:, None] * inv[None, :]
    fr = np.concatenate([fr, fr], -1)
    base = (i + 0.4 * DH) / (1.4 * DH)
    power = (t - T // 2) / 64.0
    s = base[None, :] ** power[:, None]
    s = np.concatenate([s, s], -1)
    sign = np.where(np.arange(DH) < DH // 2, -1.0, 1.0)
    trig = np.stack([np.cos(fr) * s, np.sin(fr) * s * sign, np.cos(fr) / s, np.sin(fr) / s * sign], 1)
    trig = trig.astype(np.float32).reshape(NT, P, 4, DH).transpose(1, 0, 2, 3)
    ii, jj = np.arange(P)[:, None], np.arange(P)[None, :]
    mask = np.concatenate([np.where(jj < ii, NEG, 0.0), np.where(jj > ii, NEG, 0.0)], 1).astype(np.float32)
    return dict(trig=np.ascontiguousarray(trig), mask=mask, ident=np.eye(P, dtype=np.float32),
                mean_w=np.full((P, P), 1.0 / D, np.float32))


def ffn_layout(i):
    c = ffn_constants()
    g = lambda n: np.asarray(i["L0_ffn_" + n])
    chunks = lambda a: np.ascontiguousarray(a.reshape(LAYERS, -1, P, a.shape[-1]).transpose(2, 0, 1, 3))
    w2 = np.zeros((LAYERS, HM * P, D), np.float32)
    w2[:, :HID] = g("w2")
    b1 = np.zeros((LAYERS, 2, HM * P), np.float32)
    b1[:, :, :HID] = g("b1").reshape(LAYERS, 2, HID)
    vec = np.stack([g("ln_g"), g("ln_b"), g("b2")], 1)
    swap = lambda a: np.concatenate([a[:, DH // 2:], a[:, :DH // 2]], 1)
    sc = np.stack([g("q_scale"), swap(g("q_scale")), g("k_scale"), swap(g("k_scale"))], 1)
    c |= dict(x=np.asarray(i["L0_attn_x"]), wqkv=chunks(g("wqkv")), wo=chunks(g("wo")), w1=chunks(g("w1")),
              w2=chunks(w2), b1=np.ascontiguousarray(b1.reshape(LAYERS, 2, HM, P).transpose(3, 0, 1, 2)),
              vecs=np.ascontiguousarray(vec.reshape(LAYERS, 3, KC, P).transpose(3, 0, 1, 2)),
              scales=np.ascontiguousarray(np.broadcast_to(sc[None], (P, LAYERS, 4, DH))))
    return c


H, TAPS = 16, 4
GH = 4
GW = GH * DH
NG = H // GH
GP = GH // 2
CT = GW // P
NQ = NT * GH
BL = 16
NBL = P // BL
RMS_EPS = 1e-6
LOG_FLOOR = -200.0


def delta_phase(nc, ctx, io, scratch, out):

    def sb(name, shape):
        return ctx.enter_context(nc.sbuf_tensor("d_" + name, shape, F32))

    sems = []

    def sem(name):
        sems.append(ctx.enter_context(nc.semaphore("d_" + name)))
        return sems[-1]

    wqkv = sb("wqkv", [P, 3, KC, H * DH])
    wg = sb("wg", [P, KC, H * DH])
    wo = sb("wo", [P, H * DH // P, D])
    wgate = sb("wgate", [P, KC, 2 * H])
    cw = sb("cw", [P, 3, H * DH // P, TAPS + 1])
    rows = sb("rows", [P, 5, H])
    onw = sb("onw", [P, DH])
    rope = sb("rope", [P, NT, 2, 2, DH // 2])
    tri = sb("tri", [P, 4, P])
    mshift = sb("mshift", [P, P])
    m16 = sb("m16", [P, 2 * BL])
    ident = sb("ident", [P, P])
    INCL, EXCL, AFTER, ALL = range(4)

    xnT = sb("xnT", [P, KC, T])
    zg = sb("zg", [P, NT, 2 * H])
    eb = sb("eb", [P, NT, H])
    ab = sb("ab", [P, NT, H])
    sp1 = sb("sp1", [P, NT, H])
    expA = sb("expA", [P, H])
    la = sb("la", [P, NT, H])
    coef = sb("coef", [P, 6, NT, H])
    BETA, G_INCL, G_EXCL, G_AFTER, G_ALL, B_AFTER = range(6)
    acc = sb("acc", [P, 2, T])
    xc = sb("xc", [P, 3, CT, T])
    gsb = sb("gsb", [P, 2, NT, GW])
    m1 = sb("m1", [P, 2 * GW])
    m2 = sb("m2", [P, 2 * GW])
    qk = sb("qk", [P, 2, GW])
    ss = sb("ss", [P, 2 * GH])
    rn = sb("rn", [P, 2 * GH])
    qkd = sb("qkd", [P, GH])
    sq, qkp = m1, m2
    kbg = sb("kbg", [P, 2, GW])
    qg = sb("qg", [P, GW])
    kqT = sb("kqT", [P, GP, 2, P])
    kbT = sb("kbT", [P, GP, P])
    lm = sb("lm", [P, GH, P])
    ex = sb("ex", [P, GH, P])
    em = sb("em", [P, GH, P])
    LT = sb("LT", [P, NT, GH, P])
    AT = sb("AT", [P, 2, NT, GH, P])
    kgT = sb("kgT", [P, 2, NT, GP, P])
    qgT = sb("qgT", [P, 2, NT, GP, P])
    kl = sb("kl", [P, 2, NT, GW])
    v = sb("v", [P, 2, NT, GW])
    dq = sb("dq", [P, 2, NT, GH])
    gt = sb("gt", [P, 2, NT, GP])
    LB = sb("LB", [P, BL, BL])
    TB = sb("TB", [P, BL, BL])
    pb = sb("pb", [P, BL * BL])
    T16 = sb("T16", [P, NQ, 2 * BL])
    R16 = sb("R16", [P, NQ, 2 * BL])
    Y16 = sb("Y16", [P, NQ, 2 * BL])
    T32 = sb("T32", [P, NQ, 32])
    R32, Y32 = R16, Y16
    T64 = sb("T64", [P, NQ, 64])
    Y64 = T64
    Rf = sb("Rf", [P, NQ, P])
    St = sb("St", [P, 2, GP, DH])
    Sg = sb("Sg", [P, GP, DH])
    rh = sb("rh", [P, GP, 2, DH])
    us = sb("us", [P, GH, DH])
    vq = sb("vq", [P, GP, 2, DH])
    os_ = vq
    osq = pb
    ms = sb("ms", [P, GH])
    ro = sb("ro", [P, GH])
    on = sb("on", [P, NT, GW])
    oT = sb("oT", [P, H * DH // P, T])
    gate = sb("gate", [P, KC, T])
    z = on[:, :, :].rearrange("p (m a) n -> p m (a n)", m=KC)
    xio = sb("xio", [P, NT, D])
    mhalf = sb("mhalf", [P, 2 * GH])
    ps = ctx.enter_context(nc.psum_tensor("d_ps", [P, 8, 512], F32))

    passed = sem("passed")
    loaded = sem("loaded")
    xn_in = sem("xn_in")
    gate_in = sem("gate_in")
    x_in = sem("x_in")
    ld_wr = sem("ld_wr")
    lb_rd = sem("lb_rd")
    tb_wr = sem("tb_wr")
    t16_rd = sem("t16_rd")
    out_st = sem("out_st")
    init0 = sem("init0")
    init1 = sem("init1")
    zg_ps = sem("zg_ps")
    zg_rdy = sem("zg_rdy")
    eb_rdy = sem("eb_rdy")
    ab_rdy = sem("ab_rdy")
    abe_rdy = sem("abe_rdy")
    sp_rdy = sem("sp_rdy")
    gstep = sem("gstep")
    la_rdy = sem("la_rdy")
    sum_ps = sem("sum_ps")
    sum_rdy = sem("sum_rdy")
    coef_rdy = sem("coef_rdy")
    cv_ps = sem("cv_ps")
    cv_t0 = sem("cv_t0")
    cv_mid = sem("cv_mid")
    cv_acc = sem("cv_acc")
    cv_rdy = sem("cv_rdy")
    g_ps = sem("g_ps")
    g_rdy = sem("g_rdy")
    in_ps = sem("in_ps")
    v_rdy = sem("v_rdy")
    mA = sem("mA")
    mB = sem("mB")
    qk_rdy = sem("qk_rdy")
    sq_rdy = sem("sq_rdy")
    ss_mid = sem("ss_mid")
    ss_rdy = sem("ss_rdy")
    rn_rdy = sem("rn_rdy")
    qkn_rdy = sem("qkn_rdy")
    qkp_rdy = sem("qkp_rdy")
    qkd_mid = sem("qkd_mid")
    dq_rdy = sem("dq_rdy")
    kbg_rdy = sem("kbg_rdy")
    kl_rdy = sem("kl_rdy")
    qg_rdy = sem("qg_rdy")
    gt_rdy = sem("gt_rdy")
    lm_rdy = sem("lm_rdy")
    e_ps = sem("e_ps")
    ex_rdy = sem("ex_rdy")
    em_rdy = sem("em_rdy")
    kq_ps = sem("kq_ps")
    kqT_rdy = sem("kqT_rdy")
    kb_ps = sem("kb_ps")
    kbT_rdy = sem("kbT_rdy")
    kgT_rdy = sem("kgT_rdy")
    qg_ps = sem("qg_ps")
    qgT_rdy = sem("qgT_rdy")
    kk_ps = sem("kk_ps")
    lt_rdy = sem("lt_rdy")
    at_rdy = sem("at_rdy")
    tb_step = sem("tb_step")
    tbs = sem("tbs")
    r16_rdy = sem("r16_rdy")
    y16_ps = sem("y16_ps")
    y16_rdy = sem("y16_rdy")
    r16_ps = sem("r16_ps")
    t16_ps = sem("t16_ps")
    r32_rdy = sem("r32_rdy")
    t32_rdy = sem("t32_rdy")
    y32_ps = sem("y32_ps")
    y32_rdy = sem("y32_rdy")
    r32_ps = sem("r32_ps")
    t32_ps = sem("t32_ps")
    rf_a = sem("rf_a")
    rf_b = sem("rf_b")
    t64_rdy = sem("t64_rdy")
    y64_ps = sem("y64_ps")
    y64_rdy = sem("y64_rdy")
    r64_ps = sem("r64_ps")
    rf_c = sem("rf_c")
    x_ps = sem("x_ps")
    rh_rdy = sem("rh_rdy")
    u_ps = sem("u_ps")
    us_rdy = sem("us_rdy")
    o_ps = sem("o_ps")
    s_ps = sem("s_ps")
    sg_rdy = sem("sg_rdy")
    st_rdy = sem("st_rdy")
    vq_rdy = sem("vq_rdy")
    os_rdy = sem("os_rdy")
    osq_rdy = sem("osq_rdy")
    ms_mid = sem("ms_mid")
    ms_rdy = sem("ms_rdy")
    ro_rdy = sem("ro_rdy")
    on_mid = sem("on_mid")
    on_rdy = sem("on_rdy")
    sl_rdy = sem("sl_rdy")
    og_rdy = sem("og_rdy")
    oT_ps = sem("oT_ps")
    oT_rdy = sem("oT_rdy")
    wo_ps = sem("wo_ps")
    z_rdy = sem("z_rdy")
    zT_ps = sem("zT_ps")
    xo_rdy = sem("xo_rdy")

    loads = [(t, io[n]) for t, n in ((wqkv, "dwqkv"), (wg, "dwg"), (wo, "dwo"), (wgate, "dwgate"), (cw, "dcw"),
             (rows, "drows"), (onw, "donw"), (rope, "drope"), (tri, "dtri"), (mshift, "dmshift"), (m16, "dm16"),
             (ident, "ident"), (TB, "deye"))]
    LOADED = 16 * len(loads)
    one_t = sb("one", [P, 1])
    one_ap = one_t[:, 0:1]
    block = ctx.enter_context(nc.Block())

    def flat(t):
        return t[(slice(None),) * len(t.shape)]

    def heads(ap, n=GH):
        return ap.rearrange("p (h o) -> p h o", o=1).to_broadcast([P, n, DH])

    def hd(ap, n=GH):
        return ap.rearrange("p (h d) -> p h d", h=n)

    def val(i, n, k):
        return i * n + k

    @block.sync
    def _(sp):
        for x in sems:
            sp.sem_inc(x, 1)

        def inverse_io(i):
            sp.wait_ge(lt_rdy, 1 + val(i, 2 * NT, 2 * NT))
            sp.sem_inc(passed, 1)
            sp.wait_ge(lb_rd, 1 + i * 16)
            sp.sem_inc(passed, 1)
            for k in range(NBL):
                r = slice(k * BL, (k + 1) * BL)
                sp.dma_start(scratch["Ld"][k, :, :, :].rearrange("q j t -> j q t"),
                             LT[r, :, :, r].rearrange("j c h t -> j (c h) t")).then_inc(ld_wr, 16)
            sp.wait_ge(ld_wr, 1 + val(i, 16 * NBL, 16 * NBL))
            sp.sem_inc(passed, 1)
            sp.wait_ge(tb_step, 1 + i)
            sp.sem_inc(passed, 1)
            sp.dma_start(LB[:, :, :], scratch["Ld"].rearrange("k q j t -> (k q) j t")).then_inc(lb_rd, 16)

        def inverse_back(i):
            sp.wait_ge(tb_step, 1 + i + 1)
            sp.sem_inc(passed, 1)
            sp.wait_ge(t16_rd, 1 + i * 16 * NBL)
            sp.sem_inc(passed, 1)
            sp.dma_start(scratch["Td"].rearrange("k q t c -> (k q) t c"), TB[:, :, :]).then_inc(tb_wr, 16)
            sp.wait_ge(tb_wr, 1 + i * 16 + 16)
            sp.sem_inc(passed, 1)
            sp.wait_ge(t32_rdy, 1 + i)
            sp.sem_inc(passed, 1)
            sp.wait_ge(r16_rdy, 1 + i)
            sp.sem_inc(passed, 1)
            sp.wait_ge(t16_ps, 1 + i)
            sp.sem_inc(passed, 1)
            sp.wait_ge(y16_ps, 1 + i)
            sp.sem_inc(passed, 1)
            for k in range(NBL):
                r = slice(k * BL, (k + 1) * BL)
                c0 = (k % 2) * BL
                sp.dma_start(T16[r, :, c0:c0 + BL], scratch["Td"][k, :, :, :].rearrange("q t c -> t q c")).then_inc(t16_rd, 16)

        for dst, src in loads[::-1]:
            sp.dma_start(flat(dst), src).then_inc(loaded, 16)
        sp.dma_start(flat(xnT), scratch["xnT"][0, :, :, :]).then_inc(xn_in, 16)
        inverse_io(0)
        inverse_back(0)
        with sp.Fori(0, B) as b:
            for s in range(NG):
                i = b * NG + s
                if s == 0:
                    sp.wait_ge(z_rdy, 1 + b * KC)
                    sp.sem_inc(passed, 1)
                    sp.dma_start(flat(gate), scratch["gate"][b, :, :, :]).then_inc(gate_in, 16)
                    sp.wait_ge(out_st, 1 + b * 16)
                    sp.sem_inc(passed, 1)
                    sp.dma_start(flat(xio), io["x"][b, :, :, :]).then_inc(x_in, 16)
                inverse_io(i + 1)
                if s == 1:
                    sp.wait_ge(cv_ps, 1 + val(i + 2, 6, 6))
                    sp.sem_inc(passed, 1)
                    sp.wait_ge(g_ps, 1 + val(i + 2, NT, NT))
                    sp.sem_inc(passed, 1)
                    sp.dma_start(flat(xnT), scratch["xnT"][b + 1, :, :, :]).then_inc(xn_in, 16)
                inverse_back(i + 1)
            sp.wait_ge(xo_rdy, 1 + b * 2 + 2)
            sp.sem_inc(passed, 1)
            sp.dma_start(out[b, :, :, :], flat(xio)).then_inc(out_st, 16)
        sp.wait_ge(out_st, 1 + B * 16)
        sp.sem_inc(passed, 1)

    @block.gpsimd
    def _(pool):
        tt = nc.gpsimd.tensor_tensor

        nc.gpsimd.memset(em[:, :, 0:1], 0.0).then_inc(init1, 1)
        nc.gpsimd.memset(flat(T16), 0.0).then_inc(init1, 1)
        nc.gpsimd.memset(flat(T64), 0.0).then_inc(init1, 1)
        nc.gpsimd.memset(flat(Rf), 0.0).then_inc(init1, 1)
        nc.gpsimd.memset(flat(mhalf), -0.5).then_inc(init1, 1)
        pool.wait_ge(init1, 1 + 5)
        pool.wait_ge(loaded, 1 + LOADED)

        def prepare(i, s, bt, c):
            n = lambda k=1, m=1: i * NT * m + c * m + k
            par, h0 = s % 2, s * GH
            hs = slice(h0, h0 + GH)
            pool.wait_ge(e_ps, 1 + n(0))
            pool.wait_ge(coef_rdy, 1 + bt + 1)
            tt(lm[:, :, :], tri[:, INCL:INCL + 1, :].to_broadcast([P, GH, P]),
               la[:, c, hs].rearrange("p (h o) -> p h o", o=1).to_broadcast([P, GH, P]), ALU.mult).then_inc(lm_rdy, 1)
            pool.wait_ge(mB, 1 + n())
            pool.wait_ge(kq_ps, 1 + n(0))
            pool.wait_ge(kl_rdy, 1 + n(0))
            tt(qk[:, :, :].rearrange("p a n -> p (a n)"), m1[:, :], m2[:, :], ALU.add).then_inc(qk_rdy, 1)
            pool.wait_ge(ss_rdy, 1 + n())
            tt(rn[:, :], ss[:, :], mhalf[:, :], ALU.pow).then_inc(rn_rdy, 1)
            pool.wait_ge(rn_rdy, 1 + n())
            pool.wait_ge(sq_rdy, 1 + n())
            q8 = qk[:, :, :].rearrange("p a (h d) -> p (a h) d", d=DH)
            tt(q8, q8, heads(rn[:, :], 2 * GH), ALU.mult).then_inc(qkn_rdy, 1)
            pool.wait_ge(qkn_rdy, 1 + n())
            qn, kn = qk[:, 0, :], qk[:, 1, :]
            pool.wait_ge(kb_ps, 1 + n(0))
            tt(kbg[:, 0, :].rearrange("p (h d) -> p h d", d=DH), hd(kn), heads(coef[:, BETA, c, hs]), ALU.mult).then_inc(kbg_rdy, 1)
            tt(kbg[:, 1, :].rearrange("p (h d) -> p h d", d=DH), hd(kn), heads(coef[:, G_INCL, c, hs]), ALU.mult).then_inc(kbg_rdy, 1)
            pool.wait_ge(qg_ps, 1 + n(0))
            tt(hd(qg[:, :]), hd(qn), heads(coef[:, G_EXCL, c, hs]), ALU.mult).then_inc(qg_rdy, 1)
            pool.wait_ge(ex_rdy, 1 + n())
            pool.wait_ge(at_rdy, 1 + 2 * n(0))
            tt(em[:, :, 1:], ex[:, :, 0:P - 1], mshift[:, 1:].rearrange("p (o t) -> p o t", o=1).to_broadcast([P, GH, P - 1]),
               ALU.mult).then_inc(em_rdy, 1)
            pool.wait_ge(qkd_mid, 1 + n(0))
            pool.wait_ge(ss_rdy, 1 + n())
            tt(qkp[:, 0:GW], qn, kn, ALU.mult).then_inc(qkp_rdy, 1)
            tt(hd(kl[:, par, c, :]), hd(kn), heads(coef[:, B_AFTER, c, hs]), ALU.mult).then_inc(kl_rdy, 1)

        def recur(i, s, bt, c):
            n = lambda k=1, m=1: i * NT * m + c * m + k
            par = s % 2
            pool.wait_ge(dq_rdy, 1 + val(i, NT, c + 1))
            pool.wait_ge(os_rdy, 1 + 2 * n(0))
            pool.wait_ge(on_mid, 1 + n(0))
            pool.wait_ge(osq_rdy, 1 + n(0))
            pool.wait_ge(v_rdy, 1 + val(i, NT, c + 1))
            tt(vq[:, :, :, :].rearrange("p a j d -> p (a j) d"), hd(v[:, par, c, :]), heads(dq[:, par, c, :]), ALU.mult).then_inc(vq_rdy, 1)
            if 0 < c < NT - 1:
                pool.wait_ge(st_rdy, 1 + val(i, NT - 1, c))
                pool.wait_ge(gt_rdy, 1 + 2 * n())
                tt(Sg[:, :, :], St[:, (c - 1) % 2, :, :], heads(gt[:, par, c, :], GP), ALU.mult).then_inc(sg_rdy, 1)
            pool.wait_ge(ms_rdy, 1 + n())
            tt(ro[:, :], ms[:, :], mhalf[:, 0:GH], ALU.pow).then_inc(ro_rdy, 1)
            pool.wait_ge(ro_rdy, 1 + n())
            if c == 0:
                pool.wait_ge(og_rdy, 1 + i)
                pool.wait_ge(oT_ps, 1 + 2 * i)
                pool.wait_ge(zT_ps, 1 + 2 * bt)
            o3 = os_[:, :, :, :].rearrange("p a j d -> p (a j) d")
            tt(hd(on[:, c, :]), o3, heads(ro[:, :]), ALU.mult).then_inc(on_mid, 1)
            pool.wait_ge(on_mid, 1 + n())
            tt(hd(on[:, c, :]), hd(on[:, c, :]), onw[:, :].rearrange("p (o d) -> p o d", o=1).to_broadcast([P, GH, DH]),
               ALU.mult).then_inc(on_rdy, 1)

        def gate_heads(i, s):
            pool.wait_ge(sl_rdy, 1 + i + 1)
            pool.wait_ge(g_rdy, 1 + val(i, NT, NT))
            tt(flat(on).rearrange("p c n -> p (c n)"), flat(on).rearrange("p c n -> p (c n)"),
               gsb[:, s % 2, :, :].rearrange("p c n -> p (c n)"), ALU.mult).then_inc(og_rdy, 1)

        for c in range(NT):
            prepare(0, 0, 0, c)
        with pool.Fori(0, B) as b:
            for s in range(NG):
                i = b * NG + s
                for c in range(NT):
                    recur(i, s, b, c)
                    prepare(i + 1, (s + 1) % NG, b + (s + 1) // NG, c)
                gate_heads(i, s)

    @block.scalar
    def _(act):
        A = nc.scalar.activation

        def gates(nb):
            act.wait_ge(zg_rdy, 1 + 2 * nb + 2)
            A(eb[:, :, :], zg[:, :, 0:H], ACT.Exp, scale=-1.0).then_inc(eb_rdy, 1)
            A(ab[:, :, :], zg[:, :, H:], ACT.Abs).then_inc(ab_rdy, 1)
            act.wait_ge(ab_rdy, 1 + nb + 1)
            A(ab[:, :, :], ab[:, :, :], ACT.Exp, scale=-1.0).then_inc(abe_rdy, 1)
            act.wait_ge(abe_rdy, 1 + nb + 1)
            A(sp1[:, :, :], ab[:, :, :], ACT.Ln, bias=one_ap).then_inc(sp_rdy, 1)
            act.wait_ge(sum_ps, 1 + nb + 1)
            act.wait_ge(kl_rdy, 1 + nb * NG * NT)
            A(coef[:, G_INCL:G_ALL + 1, :, :].rearrange("p k c h -> p (k c h)"), ps[:, 4, 0:4 * NT * H], ACT.Exp).then_inc(sum_rdy, 1)

        def conv(i, s):
            for n in range(6):
                X, t = n // CT, n % CT
                act.wait_ge(cv_ps, 1 + val(i, 6, n + 1))
                act.wait_ge(cv_rdy, 1 + val(i, 6, max(0, n - 1)))
                A(acc[:, n % 2, :], ps[:, 4 + n % 4, :], ACT.Identity, bias=cw[:, X, s * CT + t, TAPS:TAPS + 1],
                  scale=cw[:, X, s * CT + t, TAPS - 1:TAPS]).then_inc(cv_t0, 1)
                if n > 0:
                    silu(i, n - 1)
            silu(i, 5)

        def silu(i, n):
            X, t = n // CT, n % CT
            act.wait_ge(cv_acc, 1 + val(i, 6, n + 1))
            if n == 0:
                act.wait_ge(in_ps, 1 + i * NT)
            A(xc[:, X, t, :], acc[:, n % 2, :], ACT.Silu).then_inc(cv_rdy, 1)

        def g_copies(i, s):
            if not (isinstance(i, int) and i < 2):
                act.wait_ge(og_rdy, 1 + i - 1)
            for c in range(NT):
                act.wait_ge(g_ps, 1 + val(i, NT, c + 1))
                A(gsb[:, s % 2, c, :], ps[:, 4 + c % 2, 0:GW], ACT.Copy).then_inc(g_rdy, 1)

        def prepare(i, s, bt, c):
            n = lambda k=1, m=1: i * NT * m + c * m + k
            par = s % 2
            act.wait_ge(in_ps, 1 + n())
            A(v[:, par, c, :], ps[:, 5, 0:GW], ACT.Copy).then_inc(v_rdy, 1)
            act.wait_ge(coef_rdy, 1 + bt + 1)
            if not (isinstance(i, int) and i < 2):
                act.wait_ge(sg_rdy, 1 + (i - 1) * (NT - 2))
            for j in range(2):
                r = slice(j * DH, (j + 1) * DH)
                A(gt[r, par, c, :], coef[r, G_ALL, c, s * GH:(s + 1) * GH].rearrange("p (a j) -> p a j", j=2)[:, :, j],
                  ACT.Copy).then_inc(gt_rdy, 1)
            act.wait_ge(e_ps, 1 + n())
            act.wait_ge(lt_rdy, 1 + 2 * n(0))
            act.wait_ge(em_rdy, 1 + n(0))
            A(flat(ex).rearrange("p h t -> p (h t)"), ps[:, 6, :], ACT.Exp).then_inc(ex_rdy, 1)
            act.wait_ge(qk_rdy, 1 + n())
            A(sq[:, :], qk[:, :, :].rearrange("p a n -> p (a n)"), ACT.Square).then_inc(sq_rdy, 1)
            act.wait_ge(kq_ps, 1 + n())
            act.wait_ge(kk_ps, 1 + n(0))
            A(flat(kqT).rearrange("p a k t -> p (a k t)"), ps[:, 7, :], ACT.Copy).then_inc(kqT_rdy, 1)
            act.wait_ge(kb_ps, 1 + n())
            A(flat(kbT).rearrange("p a t -> p (a t)"), ps[:, 4, 0:GW], ACT.Copy).then_inc(kbT_rdy, 1)
            A(kgT[:, par, c, :, :].rearrange("p a t -> p (a t)"), ps[:, 4, GW:2 * GW], ACT.Copy).then_inc(kgT_rdy, 1)
            act.wait_ge(qg_ps, 1 + n())
            A(qgT[:, par, c, :, :].rearrange("p a t -> p (a t)"), ps[:, 5, 0:GW], ACT.Copy).then_inc(qgT_rdy, 1)

        def recur(i, s, bt, c):
            n = lambda k=1, m=1: i * NT * m + c * m + k
            act.wait_ge(u_ps, 1 + n())
            act.wait_ge(o_ps, 1 + n(0))
            A(flat(us).rearrange("p h d -> p (h d)"), ps[:, 2, 0:GW], ACT.Copy).then_inc(us_rdy, 1)
            act.wait_ge(os_rdy, 1 + 2 * n())
            act.wait_ge(ms_mid, 1 + n(0))
            A(osq[:, :], flat(os_).rearrange("p a j d -> p (a j d)"), ACT.Square).then_inc(osq_rdy, 1)

        def out_heads(i, s):
            act.wait_ge(on_rdy, 1 + val(i, NT, NT))
            A(flat(on), flat(on), ACT.Silu).then_inc(sl_rdy, 1)

        def out_heads_T(i, s, bt):
            for k in range(CT):
                act.wait_ge(oT_ps, 1 + 2 * i + k + 1)
                if s == 0 and k == 0:
                    act.wait_ge(wo_ps, 1 + KC * bt)
                A(oT[:, s * CT + k, :], ps[:, 2 + k, :], ACT.Copy).then_inc(oT_rdy, 1)

        def merge(i):
            act.wait_ge(y32_ps, 1 + i + 1)
            for r in range(2):
                q = slice(64 * r + 32, 64 * r + 64)
                A(Y32[q, :, :].rearrange("p q t -> p (q t)"), ps[q, 7, :], ACT.Copy).then_inc(y32_rdy, 1)
            act.wait_ge(r32_ps, 1 + i + 1)
            for r in range(2):
                q = slice(64 * r, 64 * r + 32)
                A(Rf[q, :, 64 * r + 32:64 * r + 64], ps[q, 4, :].rearrange("p (q t) -> p q t", q=NQ), ACT.Copy,
                  scale=-1.0).then_inc(rf_b, 1)
            act.wait_ge(y64_ps, 1 + i + 1)
            for k in range(2):
                A(Y64[64:, 8 * k:8 * k + 8, :].rearrange("p q t -> p (q t)"), ps[64:, 6 + k, :], ACT.Copy).then_inc(y64_rdy, 1)
            act.wait_ge(r64_ps, 1 + i + 1)
            for k in range(2):
                A(Rf[0:64, 8 * k:8 * k + 8, 64:], ps[0:64, 4 + k, :].rearrange("p (q t) -> p q t", q=8), ACT.Copy,
                  scale=-1.0).then_inc(rf_c, 1)

        act.wait_ge(loaded, 1 + LOADED)
        act.wait_ge(init0, 1 + 1)
        A(expA[:, :], rows[:, 3, :], ACT.Exp).then_inc(init0, 1)
        gates(0)
        g_copies(0, 0)
        conv(0, 0)
        for c in range(NT):
            prepare(0, 0, 0, c)
        g_copies(1, 1)
        conv(1, 1)
        act.wait_ge(init1, 1 + 5)
        merge(0)
        with act.Fori(0, B) as b:
            for s in range(NG):
                i = b * NG + s
                for c in range(NT):
                    recur(i, s, b, c)
                    prepare(i + 1, (s + 1) % NG, b + (s + 1) // NG, c)
                if s == 2:
                    gates(b + 1)
                out_heads(i, s)
                g_copies(i + 2, (s + 2) % NG)
                conv(i + 2, (s + 2) % NG)
                out_heads_T(i, s, b)
                merge(i + 1)

    @block.vector
    def _(dve):
        V = nc.vector
        V.memset(one_t[:, :], 1.0).then_inc(init0, 1)
        dve.wait_ge(loaded, 1 + LOADED)
        dve.wait_ge(init0, 1 + 2)

        def gates(nb):
            dve.wait_ge(zg_ps, 1 + nb + 1)
            dve.wait_ge(kl_rdy, 1 + nb * NG * NT)
            z3 = zg[:, :, :]
            dve.wait_ge(eb_rdy, 1 + nb)
            V.tensor_tensor(z3, ps[:, 5, 0:2 * H * NT].rearrange("p (c h) -> p c h", c=NT),
                            rows[:, 0:2, :].rearrange("p (o a) h -> p o (a h)", o=1).to_broadcast([P, NT, 2 * H]),
                            ALU.add).then_inc(zg_rdy, 1)
            dve.wait_ge(zg_rdy, 1 + 2 * nb + 1)
            V.tensor_tensor(zg[:, :, H:], zg[:, :, H:], rows[:, 2:3, :].to_broadcast([P, NT, H]), ALU.add).then_inc(zg_rdy, 1)
            dve.wait_ge(zg_rdy, 1 + 2 * nb + 2)
            dve.wait_ge(eb_rdy, 1 + nb + 1)
            V.tensor_scalar(eb[:, :, :], eb[:, :, :], 1.0, None, ALU.add).then_inc(gstep, 1)
            dve.wait_ge(gstep, 1 + nb * 4 + 1)
            V.reciprocal(coef[:, BETA, :, :], eb[:, :, :]).then_inc(gstep, 1)
            dve.wait_ge(sp_rdy, 1 + nb + 1)
            V.scalar_tensor_tensor(out=sp1[:, :, :], in0=zg[:, :, H:], scalar=0.0, in1=sp1[:, :, :],
                                   op0=ALU.max, op1=ALU.add).then_inc(gstep, 1)
            dve.wait_ge(gstep, 1 + nb * 4 + 3)
            V.scalar_tensor_tensor(out=sp1[:, :, :], in0=sp1[:, :, :], scalar=-1.0,
                                   in1=expA[:, :].rearrange("p (o h) -> p o h", o=1).to_broadcast([P, NT, H]),
                                   op0=ALU.mult, op1=ALU.mult).then_inc(gstep, 1)
            dve.wait_ge(gstep, 1 + nb * 4 + 4)
            V.tensor_scalar(la[:, :, :], sp1[:, :, :], LOG_FLOOR, None, ALU.max).then_inc(la_rdy, 1)
            dve.wait_ge(sum_rdy, 1 + nb + 1)
            V.tensor_tensor(coef[:, B_AFTER, :, :], coef[:, BETA, :, :], coef[:, G_AFTER, :, :], ALU.mult).then_inc(coef_rdy, 1)

        def conv_items(i, s, ns):
            for n in ns:
                X, t = n // CT, n % CT
                dve.wait_ge(cv_t0, 1 + val(i, 6, n + 1))
                a = acc[:, n % 2, :]
                for k in range(1, TAPS):
                    if k > 1:
                        dve.wait_ge(cv_mid, 1 + val(i, 12, 2 * n + k - 1))
                    V.scalar_tensor_tensor(out=a[:, k:], in0=ps[:, 4 + n % 4, 0:T - k],
                                           scalar=cw[:, X, s * CT + t, TAPS - 1 - k:TAPS - k], in1=a[:, k:],
                                           op0=ALU.mult, op1=ALU.add).then_inc(cv_mid if k < TAPS - 1 else cv_acc, 1)

        def prepare(i, s, bt, c):
            n = lambda k=1, m=1: i * NT * m + c * m + k
            par = s % 2
            dve.wait_ge(in_ps, 1 + n())
            dve.wait_ge(qk_rdy, 1 + n(0))
            dve.wait_ge(dq_rdy, 1 + n(0))
            src = ps[:, 4, :].rearrange("p (h i e) -> p h e i", h=2 * GH, e=2)
            for e, m, name in ((0, m1, mA), (1, m2, mB)):
                V.tensor_tensor(m[:, :].rearrange("p (h a i) -> p h a i", h=2 * GH, a=2),
                                src[:, :, e:e + 1, :].to_broadcast([P, 2 * GH, 2, DH // 2]),
                                rope[:, c, e:e + 1, :, :].to_broadcast([P, 2 * GH, 2, DH // 2]), ALU.mult).then_inc(name, 1)
            dve.wait_ge(sq_rdy, 1 + n())
            dve.wait_ge(rn_rdy, 1 + n(0))
            V.tensor_reduce(ss[:, :], hd(sq[:, :], 2 * GH), AX.X, ALU.add).then_inc(ss_mid, 1)
            dve.wait_ge(ss_mid, 1 + n())
            V.tensor_scalar(ss[:, :], ss[:, :], RMS_EPS, None, ALU.add).then_inc(ss_rdy, 1)
            dve.wait_ge(kk_ps, 1 + n())
            dve.wait_ge(em_rdy, 1 + n())
            for j in range(2):
                bank = ps[:, 6 + j, :].rearrange("p (a k t) -> p a k t", a=GP, k=2)
                pick = lambda t: t.rearrange("p (a j) t -> p a j t", j=2)[:, :, j, :]
                V.tensor_tensor(pick(LT[:, c, :, :]), bank[:, :, 0, :], pick(ex[:, :, :]), ALU.mult).then_inc(lt_rdy, 1)
                V.tensor_tensor(pick(AT[:, par, c, :, :]), bank[:, :, 1, :], pick(em[:, :, :]), ALU.mult).then_inc(at_rdy, 1)
            dve.wait_ge(qkp_rdy, 1 + n())
            V.tensor_reduce(qkd[:, :], hd(qkp[:, 0:GW]), AX.X, ALU.add).then_inc(qkd_mid, 1)
            dve.wait_ge(qkd_mid, 1 + n())
            V.tensor_tensor(dq[:, par, c, :], qkd[:, :], rows[:, 4, s * GH:(s + 1) * GH], ALU.mult).then_inc(dq_rdy, 1)

        def substitute(i):
            dve.wait_ge(lb_rd, 1 + i * 16 + 16)
            dve.wait_ge(tb_wr, 1 + i * 16)
            for t in range(1, BL):
                k = val(i, 2 * (BL - 1), 2 * t - 1)
                pv = pb[:, 0:t * t].rearrange("p (c j) -> p c j", c=t)
                V.tensor_tensor(pv, LB[:, 0:t, t:t + 1].rearrange("p j o -> p o j").to_broadcast([P, t, t]),
                                TB[:, 0:t, 0:t].rearrange("p j c -> p c j"), ALU.mult).then_inc(tbs, 1)
                dve.wait_ge(tbs, 1 + k)
                last = V.tensor_reduce(TB[:, t, 0:t], pv, AX.X, ALU.add, negate=True).then_inc(tbs, 1)
                dve.wait_ge(tbs, 1 + k + 1)
            V.memset(pb[:, 0:1], 0.0).then_inc(tb_step, 1)

        def merge16(i):
            dve.wait_ge(t16_rd, 1 + val(i, 16 * NBL, 16 * NBL))
            V.transpose(flat(R16).rearrange("p q t -> p (q t)"), flat(T16).rearrange("p q t -> p (q t)")).then_inc(r16_rdy, 1)
            dve.wait_ge(y16_ps, 1 + i + 1)
            dve.wait_ge(r32_ps, 1 + i)
            dve.wait_ge(t32_ps, 1 + i)
            V.tensor_tensor(flat(Y16), ps[:, 4, :].rearrange("p (q t) -> p q t", q=NQ),
                            m16[:, :].rearrange("p (o t) -> p o t", o=1).to_broadcast([P, NQ, 32]), ALU.mult).then_inc(y16_rdy, 1)
            dve.wait_ge(r16_ps, 1 + i + 1)
            dve.wait_ge(t16_ps, 1 + i + 1)
            dve.wait_ge(r16_rdy, 1 + i + 1)
            V.tensor_tensor(flat(R32).rearrange("p q t -> p (q t)"), flat(R16).rearrange("p q t -> p (q t)"), ps[:, 5, :],
                            ALU.subtract).then_inc(r32_rdy, 1)
            dve.wait_ge(t16_ps, 1 + i + 1)
            V.tensor_tensor(flat(T32).rearrange("p q t -> p (q t)"), flat(T16).rearrange("p q t -> p (q t)"), ps[:, 6, :],
                            ALU.subtract).then_inc(t32_rdy, 1)

        def merge32(i):
            dve.wait_ge(r32_rdy, 1 + i + 1)
            dve.wait_ge(t32_rdy, 1 + i + 1)
            dve.wait_ge(u_ps, 1 + i * NT)
            for r in range(4):
                q = slice(32 * r, 32 * r + 32)
                V.tensor_copy(Rf[q, :, q], R32[q, :, :]).then_inc(rf_a, 1)
            dve.wait_ge(y64_ps, 1 + i)
            for r in range(2):
                q = slice(32 * r, 32 * r + 32)
                V.tensor_copy(T64[q, :, q], T32[q, :, :]).then_inc(t64_rdy, 1)
            dve.wait_ge(t32_ps, 1 + i + 1)
            V.tensor_scalar(T64[32:64, :, 0:32], ps[32:64, 5, :].rearrange("p (q t) -> p q t", q=NQ), -1.0, None,
                            ALU.mult).then_inc(t64_rdy, 1)

        def recur(i, s, bt, c):
            n = lambda k=1, m=1: i * NT * m + c * m + k
            par = s % 2
            if c > 0:
                dve.wait_ge(x_ps, 1 + val(i, NT - 1, c))
                dve.wait_ge(u_ps, 1 + n(0))
                dve.wait_ge(v_rdy, 1 + n())
                for j in range(2):
                    V.tensor_tensor(rh[:, :, j, :], v[:, par, c, :].rearrange("p (a j d) -> p a j d", a=GP, j=2)[:, :, j, :],
                                    ps[:, j, 0:GP * DH].rearrange("p (a d) -> p a d", a=GP), ALU.subtract).then_inc(rh_rdy, 1)
            if c < NT - 1:
                dve.wait_ge(s_ps, 1 + val(i, NT - 1, c + 1))
                dst = St[:, c % 2, :, :].rearrange("p a d -> p (a d)")
                src = ps[:, 2, GW:GW + GP * DH]
                if c == 0:
                    V.tensor_copy(dst, src).then_inc(st_rdy, 1)
                else:
                    dve.wait_ge(sg_rdy, 1 + val(i, NT - 2, c))
                    V.tensor_tensor(dst, flat(Sg).rearrange("p a d -> p (a d)"), src, ALU.add).then_inc(st_rdy, 1)
            dve.wait_ge(o_ps, 1 + n())
            dve.wait_ge(vq_rdy, 1 + n())
            dve.wait_ge(on_mid, 1 + n(0))
            for j in range(2):
                V.tensor_tensor(os_[:, :, j, :], ps[:, j, 0:GP * DH].rearrange("p (a d) -> p a d", a=GP), vq[:, :, j, :],
                                ALU.add).then_inc(os_rdy, 1)
            dve.wait_ge(osq_rdy, 1 + n())
            dve.wait_ge(ro_rdy, 1 + n(0))
            V.tensor_reduce(ms[:, :], hd(osq[:, :]), AX.X, ALU.add).then_inc(ms_mid, 1)
            dve.wait_ge(ms_mid, 1 + n())
            V.tensor_scalar(ms[:, :], ms[:, :], 1.0 / DH, RMS_EPS, ALU.mult, ALU.add).then_inc(ms_rdy, 1)

        def output(b):
            for m in range(KC):
                dve.wait_ge(wo_ps, 1 + b * KC + m + 1)
                if m == 0:
                    dve.wait_ge(gate_in, 1 + b * 16 + 16)
                    dve.wait_ge(zT_ps, 1 + b * 2)
                V.tensor_tensor(z[:, m, :], ps[:, m, :], gate[:, m, :], ALU.mult).then_inc(z_rdy, 1)
            dve.wait_ge(x_in, 1 + b * 16 + 16)
            for k in range(2):
                dve.wait_ge(zT_ps, 1 + b * 2 + k + 1)
                xv = xio[:, 2 * k:2 * k + 2, :].rearrange("p w n -> p (w n)")
                V.tensor_tensor(xv, xv, ps[:, 2 + k, :], ALU.add).then_inc(xo_rdy, 1)

        gates(0)
        conv_items(0, 0, range(6))
        for c in range(NT):
            prepare(0, 0, 0, c)
        conv_items(1, 1, range(0, 3))
        substitute(0)
        conv_items(1, 1, range(3, 6))
        dve.wait_ge(init1, 1 + 5)
        merge16(0)
        merge32(0)
        with dve.Fori(0, B) as b:
            for s in range(NG):
                i = b * NG + s
                for c in range(NT):
                    recur(i, s, b, c)
                    prepare(i + 1, (s + 1) % NG, b + (s + 1) // NG, c)
                if s == 2:
                    gates(b + 1)
                conv_items(i + 2, (s + 2) % NG, range(0, 3))
                substitute(i + 1)
                conv_items(i + 2, (s + 2) % NG, range(3, 6))
                merge16(i + 1)
                merge32(i + 1)
            output(b)

    @block.tensor
    def _(pe):
        mm, tr = nc.tensor.matmul, nc.tensor.transpose

        def gates(nb):
            pe.wait_ge(xn_in, 1 + nb * 16 + 16)
            pe.wait_ge(qgT_rdy, 1 + nb * NG * NT)
            for c in range(NT):
                for k in range(KC):
                    last = mm(ps[:, 5, c * 2 * H:(c + 1) * 2 * H], xnT[:, k, c * P:(c + 1) * P], wgate[:, k, :],
                              start=k == 0, stop=k == KC - 1)
            last.then_inc(zg_ps, 1)

        def gate_sums(nb):
            pe.wait_ge(la_rdy, 1 + nb + 1)
            for k in range(4):
                last = mm(ps[:, 4, k * NT * H:(k + 1) * NT * H], tri[:, k, :], la[:, :, :].rearrange("p c h -> p (c h)"),
                          start=True, stop=True)
            last.then_inc(sum_ps, 1)

        def g_proj(i, s, bt):
            for c in range(NT):
                if c < 2:
                    if not (isinstance(i, int) and i == 0):
                        pe.wait_ge(qgT_rdy, 1 + i * NT)
                        pe.wait_ge(at_rdy, 1 + i * 2 * NT)
                    if s == 0:
                        pe.wait_ge(sum_rdy, 1 + bt + 1)
                else:
                    pe.wait_ge(g_rdy, 1 + val(i, NT, c - 1))
                for k in range(KC):
                    last = mm(ps[:, 4 + c % 2, 0:GW], xnT[:, k, c * P:(c + 1) * P], wg[:, k, s * GW:(s + 1) * GW],
                              start=k == 0, stop=k == KC - 1)
                last.then_inc(g_ps, 1)

        def conv(i, s):
            for n in range(6):
                X, t = n // CT, n % CT
                if n < 4:
                    pe.wait_ge(g_rdy, 1 + val(i, NT, NT))
                    pe.wait_ge(at_rdy, 1 + i * 2 * NT)
                else:
                    pe.wait_ge(cv_acc, 1 + val(i, 6, n - 3))
                for k in range(KC):
                    last = mm(ps[:, 4 + n % 4, :], wqkv[:, X, k, s * GW + t * P:s * GW + (t + 1) * P], xnT[:, k, :],
                              start=k == 0, stop=k == KC - 1)
                last.then_inc(cv_ps, 1)

        def prepare(i, s, bt, c):
            n = lambda k=1, m=1: i * NT * m + c * m + k
            if c == 0:
                pe.wait_ge(cv_rdy, 1 + val(i, 6, 6))
                pe.wait_ge(rf_c, 1 + 2 * i)
                pe.wait_ge(cv_acc, 1 + val(i, 6, 6))
            pe.wait_ge(kgT_rdy, 1 + n(0))
            pe.wait_ge(qgT_rdy, 1 + n(0))
            for X in range(3):
                for t in range(CT):
                    dst = ps[:, 4, X * GW + t * P:X * GW + (t + 1) * P] if X < 2 else ps[:, 5, t * P:(t + 1) * P]
                    last = tr(dst, xc[:, X, t, c * P:(c + 1) * P], ident[:, :])
            last.then_inc(in_ps, 1)
            pe.wait_ge(lm_rdy, 1 + n())
            pe.wait_ge(lt_rdy, 1 + 2 * n(0))
            pe.wait_ge(at_rdy, 1 + 2 * n(0))
            mm(ps[:, 6, :], tri[:, AFTER, :], lm[:, :, :].rearrange("p h t -> p (h t)"), start=True, stop=True).then_inc(e_ps, 1)
            pe.wait_ge(qkn_rdy, 1 + n())
            for t in range(GP):
                for k, part in ((0, 1), (1, 0)):
                    last = tr(ps[:, 7, (2 * t + k) * P:(2 * t + k + 1) * P], qk[:, part, t * P:(t + 1) * P], ident[:, :])
            last.then_inc(kq_ps, 1)
            pe.wait_ge(kbg_rdy, 1 + 2 * n())
            pe.wait_ge(mB, 1 + n())
            for k in range(2):
                for t in range(GP):
                    last = tr(ps[:, 4, k * GW + t * P:k * GW + (t + 1) * P], kbg[:, k, t * P:(t + 1) * P], ident[:, :])
            last.then_inc(kb_ps, 1)
            pe.wait_ge(qg_rdy, 1 + n())
            pe.wait_ge(v_rdy, 1 + n())
            for t in range(GP):
                last = tr(ps[:, 5, t * P:(t + 1) * P], qg[:, t * P:(t + 1) * P], ident[:, :])
            last.then_inc(qg_ps, 1)
            pe.wait_ge(kqT_rdy, 1 + n())
            pe.wait_ge(kbT_rdy, 1 + n())
            pe.wait_ge(ex_rdy, 1 + n())
            for j in range(2):
                r = slice(j * DH, (j + 1) * DH)
                for a in range(GP):
                    last = mm(ps[:, 6 + j, a * 2 * P:(a + 1) * 2 * P], kbT[r, a, :],
                              kqT[r, a, :, :].rearrange("p k t -> p (k t)"), start=True, stop=True)
            last.then_inc(kk_ps, 1)

        LTq = LT[:, :, :, :].rearrange("p c h t -> p (c h) t")

        def merge16(i):
            pe.wait_ge(t16_rd, 1 + val(i, 16 * NBL, 16 * NBL))
            pe.wait_ge(cv_acc, 1 + val(i + 1, 6, 6))
            pe.sem_inc(passed, 1)
            for r in range(4):
                q = slice(32 * r, 32 * r + 32)
                for m in range(NQ):
                    last = mm(ps[q, 4, 32 * m:32 * m + 32], LTq[q, m, q], T16[q, m, :], start=True, stop=True)
            last.then_inc(y16_ps, 1)
            pe.wait_ge(y16_rdy, 1 + i + 1)
            pe.wait_ge(r16_rdy, 1 + i + 1)
            pe.sem_inc(passed, 1)
            for bank, name in ((5, r16_ps), (6, t16_ps)):
                for r in range(4):
                    q = slice(32 * r, 32 * r + 32)
                    for m in range(NQ):
                        x, y = (Y16, R16) if bank == 5 else (R16, Y16)
                        last = mm(ps[q, bank, 32 * m:32 * m + 32], x[q, m, :], y[q, m, :], start=True, stop=True)
                last.then_inc(name, 1)

        def merge32(i):
            pe.wait_ge(t32_rdy, 1 + i + 1)
            pe.sem_inc(passed, 1)
            for r in range(2):
                q1, q2 = slice(64 * r, 64 * r + 32), slice(64 * r + 32, 64 * r + 64)
                for m in range(NQ):
                    last = mm(ps[q2, 7, 32 * m:32 * m + 32], LTq[q1, m, q2], T32[q1, m, :], start=True, stop=True)
            last.then_inc(y32_ps, 1)
            pe.wait_ge(y32_rdy, 1 + 2 * i + 2)
            pe.sem_inc(passed, 1)
            for r in range(2):
                q1, q2 = slice(64 * r, 64 * r + 32), slice(64 * r + 32, 64 * r + 64)
                for m in range(NQ):
                    last = mm(ps[q1, 4, 32 * m:32 * m + 32], Y32[q2, m, :], R32[q2, m, :], start=True, stop=True)
            last.then_inc(r32_ps, 1)
            q2 = slice(32, 64)
            for m in range(NQ):
                last = mm(ps[q2, 5, 32 * m:32 * m + 32], R32[q2, m, :], Y32[q2, m, :], start=True, stop=True)
            last.then_inc(t32_ps, 1)

        def merge64(i):
            pe.wait_ge(t64_rdy, 1 + 3 * i + 3)
            pe.sem_inc(passed, 1)
            for m in range(NQ):
                last = mm(ps[64:, 6 + m // 8, 64 * (m % 8):64 * (m % 8) + 64], LTq[0:64, m, 64:], T64[0:64, m, :], start=True, stop=True)
            last.then_inc(y64_ps, 1)
            pe.wait_ge(y64_rdy, 1 + 2 * i + 2)
            pe.wait_ge(rf_a, 1 + 4 * i + 4)
            pe.wait_ge(rf_b, 1 + 2 * i + 2)
            pe.sem_inc(passed, 1)
            for m in range(NQ):
                last = mm(ps[0:64, 4 + m // 8, 64 * (m % 8):64 * (m % 8) + 64], Y64[64:, m, :], Rf[64:, m, 64:], start=True, stop=True)
            last.then_inc(r64_ps, 1)

        def recur(i, s, bt, c):
            n = lambda k=1, m=1: i * NT * m + c * m + k
            par = s % 2
            if c == 0:
                pe.wait_ge(rf_a, 1 + 4 * i + 4)
                pe.wait_ge(rf_b, 1 + 2 * i + 2)
                pe.wait_ge(rf_c, 1 + 2 * i + 2)
                pe.wait_ge(oT_rdy, 1 + CT * i)
                pe.wait_ge(kl_rdy, 1 + val(i, NT, NT))
                pe.wait_ge(v_rdy, 1 + val(i, NT, NT))
                pe.wait_ge(at_rdy, 1 + val(i, 2 * NT, 2 * NT))
                pe.wait_ge(xo_rdy, 1 + 2 * bt)
            pe.wait_ge(os_rdy, 1 + 2 * n(0))
            if c > 0:
                pe.wait_ge(st_rdy, 1 + val(i, NT - 1, c))
                for j in range(2):
                    r = slice(j * DH, (j + 1) * DH)
                    for a in range(GP):
                        last = mm(ps[:, j, a * DH:(a + 1) * DH], kgT[r, par, c, a, :], St[r, (c - 1) % 2, a, :], start=True, stop=True)
                last.then_inc(x_ps, 1)
                pe.wait_ge(rh_rdy, 1 + val(i, 2 * (NT - 1), 2 * c))
            for h in range(GH):
                rhs = rh[:, h // 2, h % 2, :] if c > 0 else v[:, par, c, h * DH:(h + 1) * DH]
                last = mm(ps[:, 2, h * DH:(h + 1) * DH], Rf[:, c * GH + h, :], rhs, start=True, stop=True)
            last.then_inc(u_ps, 1)
            pe.wait_ge(us_rdy, 1 + n())
            if c < NT - 1:
                for h in range(GH):
                    a, j = h // 2, h % 2
                    last = mm(ps[j * DH:(j + 1) * DH, 2, GW + a * DH:GW + (a + 1) * DH], kl[:, par, c, h * DH:(h + 1) * DH],
                              us[:, h, :], start=True, stop=True)
                last.then_inc(s_ps, 1)
            for h in range(GH):
                a, j = h // 2, h % 2
                r = slice(j * DH, (j + 1) * DH)
                dst = ps[:, j, a * DH:(a + 1) * DH]
                if c > 0:
                    mm(dst, qgT[r, par, c, a, :], St[r, (c - 1) % 2, a, :], start=True, stop=False)
                last = mm(dst, AT[:, par, c, h, :], us[:, h, :], start=c == 0, stop=True)
            last.then_inc(o_ps, 1)

        def out_heads(i, s):
            pe.wait_ge(og_rdy, 1 + i + 1)
            pe.wait_ge(os_rdy, 1 + val(i, 2 * NT, 2 * NT))
            pe.wait_ge(st_rdy, 1 + val(i, NT - 1, NT - 1))
            for k in range(CT):
                for c in range(NT):
                    last = tr(ps[:, 2 + k, c * P:(c + 1) * P], on[:, c, k * P:(k + 1) * P], ident[:, :])
                last.then_inc(oT_ps, 1)

        def output(b):
            pe.wait_ge(oT_rdy, 1 + b * NG * CT + NG * CT)
            for m in range(KC):
                for k in range(H * DH // P):
                    last = mm(ps[:, m, :], wo[:, k, m * P:(m + 1) * P], oT[:, k, :], start=k == 0, stop=k == H * DH // P - 1)
                last.then_inc(wo_ps, 1)
            pe.wait_ge(z_rdy, 1 + b * KC + KC)
            for k in range(2):
                for w in range(2):
                    for m in range(KC):
                        last = tr(ps[:, 2 + k, w * D + m * P:w * D + (m + 1) * P], z[:, m, (2 * k + w) * P:(2 * k + w + 1) * P], ident[:, :])
                last.then_inc(zT_ps, 1)

        pe.wait_ge(loaded, 1 + LOADED)
        gates(0)
        gate_sums(0)
        g_proj(0, 0, 0)
        conv(0, 0)
        for c in range(NT):
            prepare(0, 0, 0, c)
        g_proj(1, 1, 0)
        conv(1, 1)
        pe.wait_ge(init1, 1 + 5)
        merge16(0)
        merge32(0)
        merge64(0)
        with pe.Fori(0, B) as b:
            for s in range(NG):
                i = b * NG + s
                for c in range(NT):
                    recur(i, s, b, c)
                    prepare(i + 1, (s + 1) % NG, b + (s + 1) // NG, c)
                if s == 2:
                    gates(b + 1)
                    gate_sums(b + 1)
                g_proj(i + 2, (s + 2) % NG, b + (s + 2) // NG)
                conv(i + 2, (s + 2) % NG)
                out_heads(i, s)
                merge16(i + 1)
                merge32(i + 1)
                merge64(i + 1)
            output(b)


def delta_layout(i):
    g = lambda n: np.asarray(i["L0_attn_" + n])
    chunks = lambda a: np.ascontiguousarray(a.reshape(-1, P, a.shape[-1]).transpose(1, 0, 2))
    w = np.stack([chunks(g("W" + n)) for n in "qkv"], 1)
    wg, wo = chunks(g("Wg")), chunks(g("Wo"))
    wgate = chunks(np.concatenate([g("bw"), g("gkw")], 1))
    cw = np.stack([np.concatenate([g(n + "cw").reshape(-1, TAPS), g(n + "cb")[:, None]], 1) for n in "qkv"], 0)
    cw = np.ascontiguousarray(cw.reshape(3, -1, P, TAPS + 1).transpose(2, 0, 1, 3))
    rows = np.stack([g(n) for n in ("bb", "gkb", "dt_bias", "A_log", "D_param")])
    full = lambda a: np.ascontiguousarray(np.broadcast_to(a[None], (P,) + a.shape))
    t = np.arange(T, dtype=np.float32)
    inv = (1.0 / 10000.0 ** (np.arange(0, DH, 2, dtype=np.float32) / DH)).astype(np.float32)
    emb = np.concatenate([np.outer(t, inv)] * 2, -1).astype(np.float32)
    co, si = np.cos(emb)[:, ::2], np.sin(emb)[:, ::2]
    rope = np.stack([np.stack([co, si], 1), np.stack([-si, co], 1)], 1).astype(np.float32)
    rope = np.ascontiguousarray(rope.reshape(NT, P, 2, 2, DH // 2).transpose(1, 0, 2, 3, 4))
    a, c = np.arange(P)[:, None], np.arange(P)[None, :]
    tri = np.stack([a <= c, a < c, a > c, np.ones((P, P), bool)], 1).astype(np.float32)
    r, k = np.arange(P)[:, None] % 32, np.arange(32)[None, :]
    return dict(dwqkv=w, dwg=wg, dwo=wo, dwgate=wgate, dcw=cw, drows=full(rows), donw=full(g("onorm_w")), drope=rope,
                dtri=tri, dmshift=(c > a).astype(np.float32), dm16=((r >= 16) & (k < 16)).astype(np.float32),
                deye=full(np.eye(BL, dtype=np.float32)))


def program(nc, io, out):
    xnT = nc.dram_tensor("xnT_scratch", (B + 1, P, KC, T), F32).ap()
    gate = nc.dram_tensor("gate_scratch", (B, P, KC, T), F32).ap()
    Ld = nc.dram_tensor("blocks_scratch", (NBL, NQ, BL, BL), F32).ap()
    Td = nc.dram_tensor("inverse_scratch", (NBL, NQ, BL, BL), F32).ap()
    scratch = dict(xnT=xnT, gate=gate, Ld=Ld, Td=Td)
    tiles = lambda ap: ap.rearrange("b (w p) d -> b p w d", p=P)
    io = dict(io, x=tiles(io["x"]))
    with ExitStack() as ctx:
        ffn_phase(nc, ctx, io, scratch)
    with ExitStack() as ctx:
        delta_phase(nc, ctx, io, scratch, tiles(out))


def kernel(**inputs):
    import concourse.bacc as bacc
    from concourse.bass_utils import run_bass_kernel_spmd

    nc = bacc.Bacc("TRN2", target_bir_lowering=False, num_devices=1)
    arrays = {"in_" + n: a for n, a in (ffn_layout(inputs) | delta_layout(inputs)).items()}
    io = {n[3:]: nc.dram_tensor(n, a.shape, F32, kind="ExternalInput").ap() for n, a in arrays.items()}
    out = nc.dram_tensor("out", (B, T, D), F32, kind="ExternalOutput").ap()
    program(nc, io, out)
    got = run_bass_kernel_spmd(nc, [arrays], core_ids=[0])
    return got.results[0]["out"]
```

```python
import numpy as np
import concourse.bass as bass
from concourse import mybir
from contextlib import ExitStack

F32 = mybir.dt.float32
ALU = mybir.AluOpType
ACT = mybir.ActivationFunctionType
AX = mybir.AxisListType

B, T, D = 8, 512, 256
P = 128
NT = T // P
KC = D // P
LAYERS, FH, DH = 2, 8, 64
INNER = FH * DH
HID = int(D * 4 * 2 / 3)
HM = -(-HID // P)
HROWS = [min(P, HID - m * P) for m in range(HM)]
PAIRS = FH // 2
LN_EPS = 1e-5
NEG = -1e30
W1C = 2 * HID


def ffn_phase(nc, ctx, io, scratch):

    def sb(name, shape):
        return ctx.enter_context(nc.sbuf_tensor("f_" + name, shape, F32))

    sems = []

    def sem(name):
        sems.append(ctx.enter_context(nc.semaphore("f_" + name)))
        return sems[-1]

    wqkv = sb("wqkv", [P, LAYERS, KC, 3 * INNER])
    wo = sb("wo", [P, LAYERS, PAIRS, D])
    w1 = sb("w1", [P, LAYERS, KC, W1C])
    w2 = sb("w2", [P, LAYERS, HM, D])
    b1 = sb("b1", [P, LAYERS, 2, HM])
    vecs = sb("vecs", [P, LAYERS, 3, KC])
    scales = sb("scales", [P, LAYERS, 4, DH])
    trig = sb("trig", [P, NT, 4, DH])
    rope = sb("rope", [P, LAYERS, NT, 4, DH])
    ident = sb("ident", [P, P])
    mask = sb("mask", [P, 2 * P])
    mean_w = sb("mean_w", [P, P])

    xin = sb("xin", [P, NT, D])
    xnorm = sb("xnorm", [P, NT, D])
    stats = sb("stats", [P, NT, 6])
    mv = sb("mv", [P, NT, 2])
    rstd = sb("rstd", [P, NT])
    nmr = sb("nmr", [P, NT])
    xT = sb("xT", [P, KC, T + 2])
    qk = sb("qk", [P, NT, 2, INNER])
    v = sb("v", [P, NT, INNER])
    m1 = sb("m1", [P, 2, INNER])
    m2 = sb("m2", [P, 2, INNER])
    sq = sb("sq", [P, 2, INNER])
    ssq = sb("ssq", [P, NT, 2, FH])
    nrm = sb("nrm", [P, NT, 2, FH])
    rn = sb("rn", [P, NT, 2, FH])
    qsc = sb("qsc", [P, 2, NT, FH])
    qT = sb("qT", [P, PAIRS, T])
    kT = sb("kT", [P, PAIRS, T])
    sm = sb("sm", [P, 2, 2, 2 * P])
    pr = sb("pr", [P, 2, 2, 2 * P])
    mx = sb("mx", [P, 2, 2])
    nb = sb("nb", [P, 2, 2])
    rsum = sb("rsum", [P, NT, FH])
    rinv = sb("rinv", [P, NT, FH])
    pT = sb("pT", [P, 2, 4, P])
    osb = sb("osb", [P, 2, INNER])
    oT = sb("oT", [P, PAIRS, T])
    xc, xsq = m1, m2
    std = sb("std", [P, T])
    rst = sb("rst", [P, T])
    xh = sq
    hn = sb("hn", [P, KC, T])
    gact = sb("gact", [P, 2, T])
    hh = qk[:, :, :, :].rearrange("p w k n -> p (w k) n")
    gate = sb("gate", [P, KC, T])
    ps = ctx.enter_context(nc.psum_tensor("f_ps", [P, 8, 512], F32))

    loaded = sem("loaded")
    x_in = sem("x_in")
    xn_st = sem("xn_st")
    gate_st = sem("gate_st")
    rope_rdy = sem("rope_rdy")
    zero_rdy = sem("zero_rdy")
    ln_step = sem("ln_step")
    ln_std = sem("ln_std")
    xn_rdy = sem("xn_rdy")
    xnT_ps = sem("xnT_ps")
    xT_rdy = sem("xT_rdy")
    qkv_ps = sem("qkv_ps")
    qkv_act = sem("qkv_act")
    rot_m = sem("rot_m")
    rot_mid = sem("rot_mid")
    rot_rdy = sem("rot_rdy")
    ssq_rdy = sem("ssq_rdy")
    nrm_rdy = sem("nrm_rdy")
    rn_step = sem("rn_step")
    k_rdy = sem("k_rdy")
    qkT_ps = sem("qkT_ps")
    qkT_rdy = sem("qkT_rdy")
    sc_ps = sem("sc_ps")
    sm_rdy = sem("sm_rdy")
    nb_rdy = sem("nb_rdy")
    pr_rdy = sem("pr_rdy")
    pT_ps = sem("pT_ps")
    pT_rdy = sem("pT_rdy")
    o_ps = sem("o_ps")
    ri_rdy = sem("ri_rdy")
    o_rdy = sem("o_rdy")
    oT_ps = sem("oT_ps")
    oT_rdy = sem("oT_rdy")
    wo_ps = sem("wo_ps")
    x1_rdy = sem("x1_rdy")
    mean_ps = sem("mean_ps")
    xc_rdy = sem("xc_rdy")
    xsq_rdy = sem("xsq_rdy")
    var_ps = sem("var_ps")
    std_rdy = sem("std_rdy")
    rst_rdy = sem("rst_rdy")
    xh_rdy = sem("xh_rdy")
    hn_rdy = sem("hn_rdy")
    up_ps = sem("up_ps")
    g_rdy = sem("g_rdy")
    hh_rdy = sem("hh_rdy")
    dn_ps = sem("dn_ps")
    x2_rdy = sem("x2_rdy")
    gate_rdy = sem("gate_rdy")
    passed = sem("passed")
    bn_rdy = sem("bn_rdy")
    eps_t = sb("eps", [P, 1])
    eps_ap = eps_t[:, 0:1]

    loads = [(wqkv, io["wqkv"]), (wo, io["wo"]), (w1, io["w1"]), (w2, io["w2"]), (b1, io["b1"]), (vecs, io["vecs"]),
             (scales, io["scales"]), (trig, io["trig"]), (ident, io["ident"]), (mask, io["mask"]), (mean_w, io["mean_w"])]
    LOADED = 16 * len(loads)

    block = ctx.enter_context(nc.Block())

    def flat(t):
        return t[(slice(None),) * len(t.shape)]

    @block.sync
    def _(sp):
        for x in sems:
            sp.sem_inc(x, 1)
        sp.dma_start(flat(xin), io["x"][0, :, :, :]).then_inc(x_in, 16)
        for dst, src in loads[::-1]:
            sp.dma_start(flat(dst), src).then_inc(loaded, 16)
        def store(b):
            sp.wait_ge(xT_rdy, 1 + b * KC + KC)
            sp.sem_inc(passed, 1)
            sp.dma_start(scratch["xnT"][b, :, :, :], xT[:, :, 1:T + 1]).then_inc(xn_st, 16)

        def store_gate(b):
            sp.wait_ge(gate_rdy, 1 + b * KC + KC)
            sp.sem_inc(passed, 1)
            sp.dma_start(scratch["gate"][b, :, :, :], flat(gate)).then_inc(gate_st, 16)

        with sp.Fori(0, B - 1) as b:
            store(b)
            sp.wait_ge(xn_rdy, 1 + b * NT + NT)
            sp.sem_inc(passed, 1)
            sp.dma_start(flat(xin), io["x"][b + 1, :, :, :]).then_inc(x_in, 16)
            store_gate(b)
        store(B - 1)
        store_gate(B - 1)
        sp.wait_ge(xn_st, 1 + B * 16)
        sp.dma_start(scratch["xnT"][B, :, :, :], scratch["xnT"][0, :, :, :]).then_inc(xn_st, 16)
        sp.wait_ge(xn_st, 1 + (B + 1) * 16)
        sp.wait_ge(gate_st, 1 + B * 16)

    @block.gpsimd
    def _(pool):
        nc.gpsimd.memset(xT[:, :, 0:1], 0.0).then_inc(zero_rdy, 1)
        with pool.Fori(0, B) as b:
            for l in range(LAYERS):
                it = b * LAYERS + l
                for n in range(2 * NT):
                    w, part = n // 2, n % 2
                    pool.wait_ge(rot_m, 1 + it * 2 * NT + n + 1)
                    if n == 0:
                        pool.wait_ge(qkT_ps, 1 + it * 2 * NT)
                    nc.gpsimd.tensor_tensor(qk[:, w, part, :], m1[:, n % 2, :], m2[:, n % 2, :],
                                            ALU.add).then_inc(rot_rdy, 1)
                pool.wait_ge(rn_step, 1 + it * 4 + 4)
                pool.wait_ge(rot_rdy, 1 + it * 2 * NT + 2 * NT)
                for w in range(NT):
                    kw = qk[:, w, 1, :].rearrange("p (h d) -> p h d", h=FH)
                    nc.gpsimd.tensor_tensor(kw, kw, rn[:, w, 1, :].rearrange("p (h o) -> p h o", o=1)
                                            .to_broadcast([P, FH, DH]), ALU.mult).then_inc(k_rdy, 1)

    def evac_oT(act, it, w):
        act.wait_ge(oT_ps, 1 + it * NT + w + 1)
        if w == 0:
            act.wait_ge(wo_ps, 1 + it * KC)
        nc.scalar.activation(oT[:, :, w * P:(w + 1) * P], ps[:, 7, :].rearrange("p (a t) -> p a t", a=PAIRS),
                             ACT.Copy).then_inc(oT_rdy, 1)

    @block.scalar
    def _(act):
        act.wait_ge(loaded, 1 + LOADED)
        with act.Fori(0, B) as b:
            act.wait_ge(ln_step, 1 + b * 5 + 1)
            nc.scalar.activation(rstd[:, :], mv[:, :, 1], ACT.Sqrt).then_inc(ln_std, 1)
            for c in range(KC):
                act.wait_ge(xnT_ps, 1 + b * KC + c + 1)
                if c == 0:
                    act.wait_ge(gate_rdy, 1 + b * KC)
                    act.wait_ge(zero_rdy, 1 + 1)
                nc.scalar.activation(xT[:, c, 1:T + 1], ps[:, 6 + c, :], ACT.Copy).then_inc(xT_rdy, 1)
            for l in range(LAYERS):
                it = b * LAYERS + l
                for n in range(3 * NT):
                    w, part = n // 3, n % 3
                    act.wait_ge(qkv_ps, 1 + it * 3 * NT + n + 1)
                    src = ps[:, n % 4, :]
                    if part < 2:
                        i = 2 * w + part
                        act.wait_ge(ssq_rdy, 1 + it * 2 * NT + max(0, i - 1))
                        act.wait_ge(rot_m, 1 + it * 2 * NT + i + 1)
                        nc.scalar.activation(sq[:, i % 2, :], src, ACT.Square).then_inc(qkv_act, 1)
                    else:
                        if w == 0:
                            act.wait_ge(o_ps, 1 + it * PAIRS * NT)
                        nc.scalar.activation(v[:, w, :], src, ACT.Copy).then_inc(qkv_act, 1)
                act.wait_ge(ssq_rdy, 1 + it * 2 * NT + 2 * NT)
                nc.scalar.activation(flat(nrm), flat(ssq), ACT.Sqrt).then_inc(nrm_rdy, 1)
                for n in range(2 * NT):
                    part, w = n // NT, n % NT
                    act.wait_ge(qkT_ps, 1 + it * 2 * NT + n + 1)
                    dst = (qT, kT)[part]
                    if n == 0:
                        act.wait_ge(sc_ps, 1 + it * PAIRS * NT)
                    nc.scalar.activation(dst[:, :, w * P:(w + 1) * P],
                                         ps[:, 4 + n % 2, :].rearrange("p (a t) -> p a t", a=PAIRS),
                                         ACT.Copy).then_inc(qkT_rdy, 1)
                for u in range(NT * PAIRS):
                    w = u // PAIRS
                    act.wait_ge(nb_rdy, 1 + it * NT * PAIRS + u + 1)
                    act.wait_ge(pT_ps, 1 + it * NT * PAIRS + max(0, u - 1))
                    k0 = P if w == 0 else 0
                    for j in range(2):
                        h = 2 * (u % PAIRS) + j
                        if u == 0 and j == 0:
                            act.wait_ge(o_rdy, 1 + it * NT)
                        nc.scalar.activation(pr[:, u % 2, j, k0:], sm[:, u % 2, j, k0:], ACT.Exp,
                                             bias=nb[:, u % 2, j:j + 1], scale=qsc[:, 0, w, h:h + 1],
                                             accum_out=rsum[:, w, h:h + 1]).then_inc(pr_rdy, 1)
                    if u % PAIRS == PAIRS - 1 and w > 0:
                        evac_oT(act, it, w - 1)
                evac_oT(act, it, NT - 1)
                for c in range(KC):
                    act.wait_ge(xc_rdy, 1 + it * KC + c + 1)
                    nc.scalar.activation(xsq[:, c, :], xc[:, c, :], ACT.Square).then_inc(xsq_rdy, 1)
                act.wait_ge(var_ps, 1 + it + 1)
                nc.scalar.activation(std[:, :], ps[:, 3, :], ACT.Sqrt, bias=eps_ap).then_inc(std_rdy, 1)
                for c in range(KC):
                    act.wait_ge(xh_rdy, 1 + it * KC + c + 1)
                    if c == 0:
                        act.wait_ge(up_ps, 1 + it * HM)
                    nc.scalar.activation(hn[:, c, :], xh[:, c, :], ACT.Identity, bias=vecs[:, l, 1, c:c + 1],
                                         scale=vecs[:, l, 0, c:c + 1]).then_inc(hn_rdy, 1)
                for m in range(HM):
                    r = HROWS[m]
                    act.wait_ge(up_ps, 1 + it * HM + m + 1)
                    act.wait_ge(hh_rdy, 1 + it * HM + max(0, m - 1))
                    nc.scalar.activation(gact[:r, m % 2, :], ps[:r, 5 + 2 * (m % 2), :], ACT.Gelu,
                                         bias=b1[:r, l, 1, m:m + 1]).then_inc(g_rdy, 1)
            for c in range(KC):
                act.wait_ge(x2_rdy, 1 + b * LAYERS * KC + (LAYERS - 1) * KC + c + 1)
                if c == 0:
                    act.wait_ge(gate_st, 1 + b * 16)
                nc.scalar.activation(gate[:, c, :], xT[:, c, 1:T + 1], ACT.Silu).then_inc(gate_rdy, 1)

    @block.vector
    def _(dve):
        nc.vector.memset(eps_t[:, :], LN_EPS).then_inc(rope_rdy, 1)
        dve.wait_ge(loaded, 1 + LOADED)
        for l in range(LAYERS):
            for k in range(4):
                nc.vector.tensor_tensor(rope[:, l, :, k, :], trig[:, :, k, :],
                                        scales[:, l, k:k + 1, :].to_broadcast([P, NT, DH]),
                                        ALU.mult).then_inc(rope_rdy, 1)
        dve.wait_ge(rope_rdy, 1 + 4 * LAYERS + 1)
        with dve.Fori(0, B) as b:
            dve.wait_ge(x_in, 1 + b * 16 + 16)
            for w in range(NT):
                nc.vector.bn_stats(stats[:, w, :], xin[:, w, :]).then_inc(bn_rdy, 1)
            dve.wait_ge(bn_rdy, 1 + b * 2 * NT + NT)
            dve.sem_inc(passed, 1)
            for w in range(NT):
                nc.vector.bn_aggr(mv[:, w, :], stats[:, w, :]).then_inc(bn_rdy, 1)
            dve.wait_ge(bn_rdy, 1 + b * 2 * NT + 2 * NT)
            nc.vector.tensor_scalar(mv[:, :, 1], mv[:, :, 1], LN_EPS, None, ALU.add).then_inc(ln_step, 1)
            dve.wait_ge(ln_std, 1 + b + 1)
            nc.vector.reciprocal(rstd[:, :], rstd[:, :]).then_inc(ln_step, 1)
            dve.wait_ge(ln_step, 1 + b * 5 + 2)
            nc.vector.tensor_tensor(nmr[:, :], mv[:, :, 0], rstd[:, :], ALU.mult).then_inc(ln_step, 1)
            dve.wait_ge(ln_step, 1 + b * 5 + 3)
            nc.vector.tensor_scalar(nmr[:, :], nmr[:, :], -1.0, None, ALU.mult).then_inc(ln_step, 2)
            dve.wait_ge(ln_step, 1 + b * 5 + 5)
            dve.wait_ge(xnT_ps, 1 + b * KC)
            for w in range(NT):
                nc.vector.tensor_scalar(xnorm[:, w, :], xin[:, w, :], mv[:, w, 0:1], rstd[:, w:w + 1],
                                        ALU.subtract, ALU.mult).then_inc(xn_rdy, 1)
            for l in range(LAYERS):
                it = b * LAYERS + l
                for n in range(2 * NT):
                    w, part = n // 2, n % 2
                    bank = (3 * w + part) % 4
                    dve.wait_ge(qkv_ps, 1 + it * 3 * NT + 3 * w + part + 1)
                    dve.wait_ge(rot_rdy, 1 + it * 2 * NT + max(0, n - 1))
                    src = ps[:, bank, :].rearrange("p (h d) -> p h d", h=FH)
                    a = m1[:, n % 2, :].rearrange("p (h d) -> p h d", h=FH)
                    c = m2[:, n % 2, :].rearrange("p (h d) -> p h d", h=FH)
                    H2 = DH // 2
                    nc.vector.tensor_tensor(a, src, rope[:, l, w, 2 * part:2 * part + 1, :]
                                            .to_broadcast([P, FH, DH]), ALU.mult).then_inc(rot_mid, 1)
                    nc.vector.tensor_tensor(c[:, :, 0:H2], src[:, :, H2:], rope[:, l, w, 2 * part + 1:2 * part + 2, 0:H2]
                                            .to_broadcast([P, FH, H2]), ALU.mult).then_inc(rot_mid, 1)
                    nc.vector.tensor_tensor(c[:, :, H2:], src[:, :, 0:H2], rope[:, l, w, 2 * part + 1:2 * part + 2, H2:]
                                            .to_broadcast([P, FH, H2]), ALU.mult).then_inc(rot_m, 1)
                    dve.wait_ge(qkv_act, 1 + it * 3 * NT + 3 * w + part + 1)
                    if n == 0:
                        dve.wait_ge(nrm_rdy, 1 + it)
                    nc.vector.tensor_reduce(ssq[:, w, part, :], sq[:, n % 2, :].rearrange("p (h d) -> p h d", h=FH),
                                            AX.X, ALU.add).then_inc(ssq_rdy, 1)
                dve.wait_ge(nrm_rdy, 1 + it + 1)
                nc.vector.tensor_scalar(flat(nrm), flat(nrm), 1e-12, None, ALU.max).then_inc(rn_step, 1)
                dve.wait_ge(rn_step, 1 + it * 4 + 1)
                dve.wait_ge(k_rdy, 1 + it * NT)
                nc.vector.reciprocal(flat(rn), flat(nrm)).then_inc(rn_step, 1)
                dve.wait_ge(rn_step, 1 + it * 4 + 2)
                dve.wait_ge(pr_rdy, 1 + it * FH * NT)
                nc.vector.tensor_scalar(qsc[:, 0, :, :], rn[:, :, 0, :], 8.0, None, ALU.mult).then_inc(rn_step, 1)
                nc.vector.tensor_scalar(qsc[:, 1, :, :], rn[:, :, 0, :], -8.0, None, ALU.mult).then_inc(rn_step, 1)
                dve.wait_ge(rn_step, 1 + it * 4 + 4)

                def masked_max(u):
                    w = u // PAIRS
                    k0 = P if w == 0 else 0
                    dve.wait_ge(sc_ps, 1 + it * NT * PAIRS + u + 1)
                    dve.wait_ge(pr_rdy, 1 + it * NT * FH + max(0, 2 * (u - 1)))
                    dve.sem_inc(passed, 1)
                    for j in range(2):
                        nc.vector.tensor_tensor_reduce(
                            out=sm[:, u % 2, j, k0:], in0=ps[:, 2 * (u % 2) + j, k0:2 * P],
                            in1=mask[:, k0:], scale=1.0, scalar=-3e38, op0=ALU.add, op1=ALU.max,
                            accum_out=mx[:, u % 2, j:j + 1]).then_inc(sm_rdy, 1)
                    dve.wait_ge(sm_rdy, 1 + it * NT * FH + 2 * u + 2)
                    h = 2 * (u % PAIRS)
                    nc.vector.tensor_tensor(nb[:, u % 2, :], mx[:, u % 2, :], qsc[:, 1, w, h:h + 2],
                                            ALU.mult).then_inc(nb_rdy, 1)

                def evac_pT(u):
                    w = u // PAIRS
                    dve.wait_ge(pT_ps, 1 + it * NT * PAIRS + u + 1)
                    dve.wait_ge(o_ps, 1 + it * NT * PAIRS + max(0, u - 1))
                    k0 = 1 if w == 0 else 0
                    nc.vector.tensor_copy(pT[:, u % 2, :, :].rearrange("p (j k) t -> p j k t", j=2)[:, :, k0:, :],
                                          ps[:, 4 + u % 2, :].rearrange("p (j k t) -> p j k t", j=2, k=2)[:, :, k0:, :]
                                          ).then_inc(pT_rdy, 1)

                def window_out(w):
                    dve.wait_ge(pr_rdy, 1 + it * NT * FH + FH * (w + 1))
                    nc.vector.reciprocal(rinv[:, w, :], rsum[:, w, :]).then_inc(ri_rdy, 1)
                    dve.wait_ge(ri_rdy, 1 + it * NT + w + 1)
                    dve.wait_ge(o_ps, 1 + it * NT * PAIRS + PAIRS * (w + 1))
                    dve.wait_ge(oT_ps, 1 + it * NT + max(0, w - 1))
                    nc.vector.tensor_tensor(osb[:, w % 2, :].rearrange("p (h d) -> p h d", h=FH),
                                            ps[:, 6, :].rearrange("p (h d) -> p h d", h=FH),
                                            rinv[:, w, :].rearrange("p (h o) -> p h o", o=1)
                                            .to_broadcast([P, FH, DH]), ALU.mult).then_inc(o_rdy, 1)

                U = NT * PAIRS
                masked_max(0)
                masked_max(1)
                for u in range(U):
                    evac_pT(u)
                    if u + 2 < U:
                        masked_max(u + 2)
                    if u % PAIRS == PAIRS - 1:
                        window_out(u // PAIRS)
                if l == 0:
                    dve.wait_ge(xn_st, 1 + b * 16 + 16)
                for c in range(KC):
                    dve.wait_ge(wo_ps, 1 + it * KC + c + 1)
                    nc.vector.tensor_tensor(xT[:, c, 1:T + 1], xT[:, c, 1:T + 1], ps[:, c, :],
                                            ALU.add).then_inc(x1_rdy, 1)
                dve.wait_ge(x1_rdy, 1 + it * KC + KC)
                dve.wait_ge(mean_ps, 1 + it + 1)
                for c in range(KC):
                    nc.vector.tensor_tensor(xc[:, c, :], xT[:, c, 1 - c:T + 1 - c], ps[:, 2, :],
                                            ALU.subtract).then_inc(xc_rdy, 1)
                dve.wait_ge(std_rdy, 1 + it + 1)
                nc.vector.reciprocal(rst[:, :], std[:, :]).then_inc(rst_rdy, 1)
                dve.wait_ge(rst_rdy, 1 + it + 1)
                dve.wait_ge(hn_rdy, 1 + it * KC)
                for c in range(KC):
                    nc.vector.tensor_tensor(xh[:, c, :], xc[:, c, :], rst[:, :], ALU.mult).then_inc(xh_rdy, 1)
                for m in range(HM):
                    r = HROWS[m]
                    dve.wait_ge(g_rdy, 1 + it * HM + m + 1)
                    nc.vector.scalar_tensor_tensor(out=hh[:r, m, :], in0=ps[:r, 4 + 2 * (m % 2), :],
                                                   scalar=b1[:r, l, 0, m:m + 1], in1=gact[:r, m % 2, :],
                                                   op0=ALU.add, op1=ALU.mult).then_inc(hh_rdy, 1)
                for c in range(KC):
                    dve.wait_ge(dn_ps, 1 + it * KC + c + 1)
                    nc.vector.scalar_tensor_tensor(out=xT[:, c, 1:T + 1], in0=ps[:, c, :],
                                                   scalar=vecs[:, l, 2, c:c + 1], in1=xT[:, c, 1:T + 1],
                                                   op0=ALU.add, op1=ALU.add).then_inc(x2_rdy, 1)
                dve.wait_ge(x2_rdy, 1 + it * KC + KC)

    @block.tensor
    def _(pe):
        pe.wait_ge(loaded, 1 + LOADED)
        mm = nc.tensor.matmul

        def shifted(c, t0, t1):
            return xT[:, c, 1 - c + t0:1 - c + t1]

        with pe.Fori(0, B) as b:
            for c in range(KC):
                if c == 0:
                    pe.wait_ge(x2_rdy, 1 + b * LAYERS * KC)
                    pe.wait_ge(xn_rdy, 1 + b * NT + NT)
                for w in range(NT):
                    last = nc.tensor.transpose(ps[:, 6 + c, w * P:(w + 1) * P], xnorm[:, w, c * P:(c + 1) * P], ident[:, :])
                last.then_inc(xnT_ps, 1)
            for l in range(LAYERS):
                it = b * LAYERS + l
                if l == 0:
                    pe.wait_ge(xT_rdy, 1 + b * KC + KC)
                pe.wait_ge(x2_rdy, 1 + it * KC)
                for n in range(3 * NT):
                    w, part = n // 3, n % 3
                    if n >= 4:
                        pe.wait_ge(qkv_act, 1 + it * 3 * NT + n - 3)
                        pe.wait_ge(rot_m, 1 + it * 2 * NT + 2 * ((n - 3) // 3) + min((n - 3) % 3, 2))
                    for c in range(KC):
                        last = mm(ps[:, n % 4, :], shifted(c, w * P, (w + 1) * P),
                                  wqkv[:, l, c, part * INNER:(part + 1) * INNER], start=c == 0, stop=c == KC - 1)
                    last.then_inc(qkv_ps, 1)
                for n in range(2 * NT):
                    part, w = n // NT, n % NT
                    if part == 0:
                        pe.wait_ge(rot_rdy, 1 + it * 2 * NT + 2 * w + 1)
                    else:
                        pe.wait_ge(k_rdy, 1 + it * NT + w + 1)
                    pe.wait_ge(qkT_rdy, 1 + it * 2 * NT + max(0, n - 1))
                    for a in range(PAIRS):
                        last = nc.tensor.transpose(ps[:, 4 + n % 2, a * P:(a + 1) * P],
                                                   qk[:, w, part, a * P:(a + 1) * P], ident[:, :])
                    last.then_inc(qkT_ps, 1)

                def scores(u):
                    w, a = u // PAIRS, u % PAIRS
                    if u < 2:
                        pe.wait_ge(qkv_act, 1 + it * 3 * NT + 3 * NT)
                        pe.wait_ge(rot_m, 1 + it * 2 * NT + 2 * NT)
                        pe.wait_ge(qkT_rdy, 1 + it * 2 * NT + 2 * NT)
                    else:
                        pe.wait_ge(sm_rdy, 1 + it * NT * FH + 2 * (u - 1))
                    k0 = P if w == 0 else 0
                    for j in range(2):
                        rows = slice(j * DH, (j + 1) * DH)
                        last = mm(ps[:, 2 * (u % 2) + j, k0:2 * P], qT[rows, a, w * P:(w + 1) * P],
                                  kT[rows, a, (w - 1) * P + k0:(w + 1) * P], start=True, stop=True)
                    last.then_inc(sc_ps, 1)

                def transpose_p(u):
                    w = u // PAIRS
                    pe.wait_ge(pr_rdy, 1 + it * NT * FH + 2 * u + 2)
                    pe.wait_ge(pT_rdy, 1 + it * NT * PAIRS + max(0, u - 1))
                    for j in range(2):
                        for k in range(1 if w == 0 else 0, 2):
                            last = nc.tensor.transpose(ps[:, 4 + u % 2, (2 * j + k) * P:(2 * j + k + 1) * P],
                                                       pr[:, u % 2, j, k * P:(k + 1) * P], ident[:, :])
                    last.then_inc(pT_ps, 1)

                def weigh_v(u):
                    w, a = u // PAIRS, u % PAIRS
                    pe.wait_ge(pT_rdy, 1 + it * NT * PAIRS + u + 1)
                    if a == 0:
                        pe.wait_ge(o_rdy, 1 + it * NT + w)
                    k0 = 1 if w == 0 else 0
                    for j in range(2):
                        h = 2 * a + j
                        for k in range(k0, 2):
                            last = mm(ps[:, 6, h * DH:(h + 1) * DH], pT[:, u % 2, 2 * j + k, :],
                                      v[:, w - 1 + k, h * DH:(h + 1) * DH], start=k == k0, stop=k == 1)
                    last.then_inc(o_ps, 1)

                def transpose_o(w):
                    pe.wait_ge(o_rdy, 1 + it * NT + w + 1)
                    if w == 0:
                        pe.wait_ge(x2_rdy, 1 + it * KC)
                    pe.wait_ge(oT_rdy, 1 + it * NT + w)
                    for a in range(PAIRS):
                        last = nc.tensor.transpose(ps[:, 7, a * P:(a + 1) * P], osb[:, w % 2, a * P:(a + 1) * P], ident[:, :])
                    last.then_inc(oT_ps, 1)

                U = NT * PAIRS
                scores(0)
                scores(1)
                for u in range(U):
                    if u == 0:
                        transpose_p(0)
                    if u + 2 < U:
                        scores(u + 2)
                    if u + 1 < U:
                        transpose_p(u + 1)
                    weigh_v(u)
                    if u % PAIRS == 0 and u > 0:
                        transpose_o(u // PAIRS - 1)
                transpose_o(NT - 1)
                pe.wait_ge(oT_rdy, 1 + it * NT + NT)
                pe.wait_ge(sm_rdy, 1 + it * NT * FH + NT * FH)
                for c in range(KC):
                    for a in range(PAIRS):
                        last = mm(ps[:, c, :], wo[:, l, a, c * P:(c + 1) * P], oT[:, a, :], start=a == 0, stop=a == PAIRS - 1)
                    last.then_inc(wo_ps, 1)
                for c in range(KC):
                    pe.wait_ge(x1_rdy, 1 + it * KC + c + 1)
                    last = mm(ps[:, 2, :], mean_w[:, :], shifted(c, 0, T), start=c == 0, stop=c == KC - 1)
                last.then_inc(mean_ps, 1)
                for c in range(KC):
                    pe.wait_ge(xsq_rdy, 1 + it * KC + c + 1)
                    last = mm(ps[:, 3, :], mean_w[:, :], xsq[:, c, :], start=c == 0, stop=c == KC - 1)
                last.then_inc(var_ps, 1)
                pe.wait_ge(hn_rdy, 1 + it * KC + KC)
                for m in range(HM):
                    r = HROWS[m]
                    if m >= 2:
                        pe.wait_ge(hh_rdy, 1 + it * HM + m - 1)
                    for part in range(2):
                        for c in range(KC):
                            last = mm(ps[:r, 4 + 2 * (m % 2) + part, :],
                                      w1[:, l, c, part * HID + m * P:part * HID + m * P + r], hn[:, c, :],
                                      start=c == 0, stop=c == KC - 1)
                    last.then_inc(up_ps, 1)
                for c in range(KC):
                    for m in range(HM):
                        r = HROWS[m]
                        if c == 0:
                            pe.wait_ge(hh_rdy, 1 + it * HM + m + 1)
                        last = mm(ps[:, c, :], w2[:r, l, m, c * P:(c + 1) * P], hh[:r, m, :], start=m == 0, stop=m == HM - 1)
                    last.then_inc(dn_ps, 1)


def ffn_constants():
    i = np.arange(0, DH, 2, dtype=np.float32)
    inv = (1.0 / 10000.0 ** (i / DH)).astype(np.float32)
    t = np.arange(T, dtype=np.float32)
    fr = t[:, None] * inv[None, :]
    fr = np.concatenate([fr, fr], -1)
    base = (i + 0.4 * DH) / (1.4 * DH)
    power = (t - T // 2) / 64.0
    s = base[None, :] ** power[:, None]
    s = np.concatenate([s, s], -1)
    sign = np.where(np.arange(DH) < DH // 2, -1.0, 1.0)
    trig = np.stack([np.cos(fr) * s, np.sin(fr) * s * sign, np.cos(fr) / s, np.sin(fr) / s * sign], 1)
    trig = trig.astype(np.float32).reshape(NT, P, 4, DH).transpose(1, 0, 2, 3)
    ii, jj = np.arange(P)[:, None], np.arange(P)[None, :]
    mask = np.concatenate([np.where(jj < ii, NEG, 0.0), np.where(jj > ii, NEG, 0.0)], 1).astype(np.float32)
    return dict(trig=np.ascontiguousarray(trig), mask=mask, ident=np.eye(P, dtype=np.float32),
                mean_w=np.full((P, P), 1.0 / D, np.float32))


def ffn_layout(i):
    c = ffn_constants()
    g = lambda n: np.asarray(i["L0_ffn_" + n])
    chunks = lambda a: np.ascontiguousarray(a.reshape(LAYERS, -1, P, a.shape[-1]).transpose(2, 0, 1, 3))
    w2 = np.zeros((LAYERS, HM * P, D), np.float32)
    w2[:, :HID] = g("w2")
    b1 = np.zeros((LAYERS, 2, HM * P), np.float32)
    b1[:, :, :HID] = g("b1").reshape(LAYERS, 2, HID)
    vec = np.stack([g("ln_g"), g("ln_b"), g("b2")], 1)
    swap = lambda a: np.concatenate([a[:, DH // 2:], a[:, :DH // 2]], 1)
    sc = np.stack([g("q_scale"), swap(g("q_scale")), g("k_scale"), swap(g("k_scale"))], 1)
    c |= dict(x=np.asarray(i["L0_attn_x"]), wqkv=chunks(g("wqkv")), wo=chunks(g("wo")), w1=chunks(g("w1")),
              w2=chunks(w2), b1=np.ascontiguousarray(b1.reshape(LAYERS, 2, HM, P).transpose(3, 0, 1, 2)),
              vecs=np.ascontiguousarray(vec.reshape(LAYERS, 3, KC, P).transpose(3, 0, 1, 2)),
              scales=np.ascontiguousarray(np.broadcast_to(sc[None], (P, LAYERS, 4, DH))))
    return c


H, TAPS = 16, 4
GH = 4
GW = GH * DH
NG = H // GH
GP = GH // 2
CT = GW // P
NQ = NT * GH
CV_BANK = (4, 5, 6, 7, 0, 1)
V_BANK = (0, 5, 5, 5)
BL = 16
NBL = P // BL
RMS_EPS = 1e-6
LOG_FLOOR = -200.0


def delta_phase(nc, ctx, io, scratch, out):

    def sb(name, shape):
        return ctx.enter_context(nc.sbuf_tensor("d_" + name, shape, F32))

    sems = []

    def sem(name):
        sems.append(ctx.enter_context(nc.semaphore("d_" + name)))
        return sems[-1]

    wqkv = sb("wqkv", [P, 3, KC, H * DH])
    wg = sb("wg", [P, KC, H * DH])
    wo = sb("wo", [P, H * DH // P, D])
    wgate = sb("wgate", [P, KC, 2 * H])
    cw = sb("cw", [P, 3, H * DH // P, TAPS + 1])
    rows = sb("rows", [P, 5, H])
    onw = sb("onw", [P, DH])
    rope = sb("rope", [P, NT, 2, 2, DH // 2])
    tri = sb("tri", [P, 4, P])
    mshift = sb("mshift", [P, P])
    m16 = sb("m16", [P, 2 * BL])
    ident = sb("ident", [P, P])
    INCL, EXCL, AFTER, ALL = range(4)

    xnT = sb("xnT", [P, KC, T])
    zg = sb("zg", [P, NT, 2 * H])
    eb = sb("eb", [P, NT, H])
    ab = sb("ab", [P, NT, H])
    sp1 = sb("sp1", [P, NT, H])
    expA = sb("expA", [P, H])
    la = sb("la", [P, NT, H])
    coef = sb("coef", [P, 6, NT, H])
    BETA, G_INCL, G_EXCL, G_AFTER, G_ALL, B_AFTER = range(6)
    acc = sb("acc", [P, 2, T])
    xc = sb("xc", [P, 3, CT, T])
    gsb = sb("gsb", [P, 2, NT, GW])
    m1 = sb("m1", [P, 2 * GW])
    m2 = sb("m2", [P, 2 * GW])
    qk = sb("qk", [P, 2, 2, GW])
    ss = sb("ss", [P, 2 * GH])
    rn = sb("rn", [P, 2 * GH])
    qkd = sb("qkd", [P, GH])
    sq = m1
    kbg = sb("kbg", [P, 2, GW])
    qg = sb("qg", [P, GW])
    kqT = sb("kqT", [P, GP, 2, P])
    kbT = sb("kbT", [P, GP, P])
    lm = sb("lm", [P, GH, P])
    ex = sb("ex", [P, GH, P])
    em = sb("em", [P, GH, P])
    LT = sb("LT", [P, NT, GH, P])
    AT = sb("AT", [P, 2, NT, GH, P])
    kgT = sb("kgT", [P, 2, NT, GP, P])
    qgT = sb("qgT", [P, 2, NT, GP, P])
    kl = sb("kl", [P, 2, NT, GW])
    v = sb("v", [P, 2, NT, GW])
    dq = sb("dq", [P, 2, NT, GH])
    gt = sb("gt", [P, 2, NT, GP])
    LB = sb("LB", [P, BL, BL])
    TB = sb("TB", [P, BL, BL])
    pb = sb("pb", [P, BL * BL])
    qkp = pb[:, 0:GW]
    T16 = sb("T16", [P, NQ, 2 * BL])
    R16 = sb("R16", [P, NQ, 2 * BL])
    Y16 = sb("Y16", [P, NQ, 2 * BL])
    T32 = kbg[:, :, :].rearrange("p k (q t) -> p (k q) t", t=32)
    R32, Y32 = R16, Y16
    T64 = sb("T64", [P, NQ, 64])
    Y64 = T64
    Rf = sb("Rf", [P, NQ, P])
    St = sb("St", [P, 2, GP, DH])
    Sg = sb("Sg", [P, GP, DH])
    rh = sb("rh", [P, GP, 2, DH])
    us = sb("us", [P, GH, DH])
    vq = sb("vq", [P, GP, 2, DH])
    ms = sb("ms", [P, NQ])
    ro = sb("ro", [P, NQ])
    on = sb("on", [P, NT, GW])
    oT = sb("oT", [P, H * DH // P, T])
    gate = sb("gate", [P, KC, T])
    z = on[:, :, :].rearrange("p (m a) n -> p m (a n)", m=KC)
    xio = sb("xio", [P, NT, D])
    mhalf = sb("mhalf", [P, NQ])
    ps = ctx.enter_context(nc.psum_tensor("d_ps", [P, 8, 512], F32))

    passed = sem("passed")
    loaded = sem("loaded")
    xn_in = sem("xn_in")
    gate_in = sem("gate_in")
    x_in = sem("x_in")
    ld_wr = sem("ld_wr")
    lb_rd = sem("lb_rd")
    tb_wr = sem("tb_wr")
    t16_rd = sem("t16_rd")
    out_st = sem("out_st")
    init0 = sem("init0")
    init1 = sem("init1")
    zg_ps = sem("zg_ps")
    zg_rdy = sem("zg_rdy")
    eb_rdy = sem("eb_rdy")
    ab_rdy = sem("ab_rdy")
    abe_rdy = sem("abe_rdy")
    sp_rdy = sem("sp_rdy")
    gstep = sem("gstep")
    la_rdy = sem("la_rdy")
    sum_ps = sem("sum_ps")
    sum_rdy = sem("sum_rdy")
    coef_rdy = sem("coef_rdy")
    cv_ps = sem("cv_ps")
    cv_t0 = sem("cv_t0")
    cv_mid = sem("cv_mid")
    cv_acc = sem("cv_acc")
    cv_rdy = sem("cv_rdy")
    g_ps = sem("g_ps")
    g_rdy = sem("g_rdy")
    in_ps = sem("in_ps")
    vin_ps = sem("vin_ps")
    td_zero = sem("td_zero")
    v_rdy = sem("v_rdy")
    rot_rdy = sem("rot_rdy")
    qk_rdy = sem("qk_rdy")
    sq_rdy = sem("sq_rdy")
    ss_mid = sem("ss_mid")
    ss_rdy = sem("ss_rdy")
    rn_rdy = sem("rn_rdy")
    qkn_rdy = sem("qkn_rdy")
    qkd_mid = sem("qkd_mid")
    dq_rdy = sem("dq_rdy")
    kbg_rdy = sem("kbg_rdy")
    kl_rdy = sem("kl_rdy")
    qg_rdy = sem("qg_rdy")
    gt_rdy = sem("gt_rdy")
    lm_rdy = sem("lm_rdy")
    e_ps = sem("e_ps")
    ex_rdy = sem("ex_rdy")
    em_rdy = sem("em_rdy")
    kq_ps = sem("kq_ps")
    kqT_rdy = sem("kqT_rdy")
    kb_ps = sem("kb_ps")
    kbT_rdy = sem("kbT_rdy")
    kgT_rdy = sem("kgT_rdy")
    qg_ps = sem("qg_ps")
    qgT_rdy = sem("qgT_rdy")
    kk_ps = sem("kk_ps")
    lt_rdy = sem("lt_rdy")
    at_rdy = sem("at_rdy")
    tb_step = sem("tb_step")
    tbs = sem("tbs")
    r16_rdy = sem("r16_rdy")
    y16_ps = sem("y16_ps")
    y16_rdy = sem("y16_rdy")
    t16_ps = sem("t16_ps")
    r32_rdy = sem("r32_rdy")
    t32_rdy = sem("t32_rdy")
    y32_ps = sem("y32_ps")
    y32_rdy = sem("y32_rdy")
    r32_ps = sem("r32_ps")
    t32_ps = sem("t32_ps")
    rf_a = sem("rf_a")
    rf_b = sem("rf_b")
    t64_rdy = sem("t64_rdy")
    y64_ps = sem("y64_ps")
    y64_rdy = sem("y64_rdy")
    r64_ps = sem("r64_ps")
    rf_c = sem("rf_c")
    x_ps = sem("x_ps")
    rh_rdy = sem("rh_rdy")
    u_ps = sem("u_ps")
    us_rdy = sem("us_rdy")
    o_ps = sem("o_ps")
    s_ps = sem("s_ps")
    sg_rdy = sem("sg_rdy")
    st_rdy = sem("st_rdy")
    vq_rdy = sem("vq_rdy")
    os_rdy = sem("os_rdy")
    osq_rdy = sem("osq_rdy")
    ms_mid = sem("ms_mid")
    ms_rdy = sem("ms_rdy")
    ro_rdy = sem("ro_rdy")
    on_mid = sem("on_mid")
    on_rdy = sem("on_rdy")
    sl_rdy = sem("sl_rdy")
    og_rdy = sem("og_rdy")
    oT_ps = sem("oT_ps")
    oT_rdy = sem("oT_rdy")
    wo_ps = sem("wo_ps")
    z_rdy = sem("z_rdy")
    zT_ps = sem("zT_ps")
    xo_rdy = sem("xo_rdy")

    loads = [(t, io[n]) for t, n in ((wqkv, "dwqkv"), (wg, "dwg"), (wo, "dwo"), (wgate, "dwgate"), (cw, "dcw"),
             (rows, "drows"), (onw, "donw"), (rope, "drope"), (tri, "dtri"), (mshift, "dmshift"), (m16, "dm16"),
             (ident, "ident"), (TB, "deye"))]
    LOADED = 16 * len(loads)
    one_t = sb("one", [P, 1])
    one_ap = one_t[:, 0:1]
    block = ctx.enter_context(nc.Block())

    def flat(t):
        return t[(slice(None),) * len(t.shape)]

    def heads(ap, n=GH):
        return ap.rearrange("p (h o) -> p h o", o=1).to_broadcast([P, n, DH])

    def hd(ap, n=GH):
        return ap.rearrange("p (h d) -> p h d", h=n)

    def osq(s):
        return oT[:, s * CT:(s + 1) * CT, :].rearrange("p a t -> p (a t)")

    def val(i, n, k):
        return i * n + k

    @block.sync
    def _(sp):
        for x in sems:
            sp.sem_inc(x, 1)

        def inverse_io(i):
            sp.wait_ge(lt_rdy, 1 + val(i, 2 * NT, 2 * NT))
            sp.sem_inc(passed, 1)
            sp.wait_ge(lb_rd, 1 + i * 32)
            sp.sem_inc(passed, 1)
            for r in range(4):
                q = slice(32 * r, 32 * r + 32)
                sp.dma_start(scratch["Ld"][r, :, :, :].rearrange("q j t -> j q t"), LT[q, :, :, q].rearrange("j c h t -> j (c h) t")).then_inc(ld_wr, 16)
            sp.wait_ge(ld_wr, 1 + val(i, 16 * 4, 16 * 4))
            sp.sem_inc(passed, 1)
            sp.wait_ge(tb_step, 1 + i)
            sp.sem_inc(passed, 1)
            for k in range(2):
                sp.dma_start(LB[64 * k:64 * k + 64, :, :],
                             scratch["Ld"][:, :, BL * k:BL * k + BL, BL * k:BL * k + BL].rearrange("r q j t -> (r q) j t")).then_inc(lb_rd, 16)

        def inverse_back(i):
            sp.wait_ge(tb_step, 1 + i + 1)
            sp.sem_inc(passed, 1)
            sp.wait_ge(t16_rd, 1 + i * 64)
            sp.sem_inc(passed, 1)
            for k in range(2):
                sp.dma_start(scratch["Td"][:, :, BL * k:BL * k + BL, BL * k:BL * k + BL].rearrange("r q t c -> (r q) t c"),
                             TB[64 * k:64 * k + 64, :, :]).then_inc(tb_wr, 16)
            sp.wait_ge(tb_wr, 1 + i * 32 + 32)
            sp.sem_inc(passed, 1)
            sp.wait_ge(t32_rdy, 1 + i)
            sp.sem_inc(passed, 1)
            sp.wait_ge(r16_rdy, 1 + i)
            sp.sem_inc(passed, 1)
            sp.wait_ge(t16_ps, 1 + i)
            sp.sem_inc(passed, 1)
            sp.wait_ge(y16_ps, 1 + i)
            sp.sem_inc(passed, 1)
            for r in range(4):
                sp.dma_start(T16[32 * r:32 * r + 32, :, :], scratch["Td"][r, :, :, :].rearrange("q t c -> t q c")).then_inc(t16_rd, 16)

        for dst, src in loads[::-1]:
            sp.dma_start(flat(dst), src).then_inc(loaded, 16)
        sp.dma_start(flat(xnT), scratch["xnT"][0, :, :, :]).then_inc(xn_in, 16)
        sp.wait_ge(init1, 1 + 2)
        for r in range(4):
            sp.dma_start(scratch["Td"][r, :, :, :].rearrange("q t c -> t q c"), T16[32 * r:32 * r + 32, :, :]).then_inc(td_zero, 16)
        sp.wait_ge(td_zero, 1 + 4 * 16)
        inverse_io(0)
        inverse_back(0)
        with sp.Fori(0, B) as b:
            for s in range(NG):
                i = b * NG + s
                if s == 0:
                    sp.wait_ge(z_rdy, 1 + b * KC)
                    sp.sem_inc(passed, 1)
                    sp.dma_start(flat(gate), scratch["gate"][b, :, :, :]).then_inc(gate_in, 16)
                    sp.wait_ge(out_st, 1 + b * 16)
                    sp.sem_inc(passed, 1)
                    sp.dma_start(flat(xio), io["x"][b, :, :, :]).then_inc(x_in, 16)
                inverse_io(i + 1)
                if s == 1:
                    sp.wait_ge(cv_ps, 1 + val(i + 2, 6, 6))
                    sp.sem_inc(passed, 1)
                    sp.wait_ge(g_ps, 1 + val(i + 2, NT, NT))
                    sp.sem_inc(passed, 1)
                    sp.dma_start(flat(xnT), scratch["xnT"][b + 1, :, :, :]).then_inc(xn_in, 16)
                inverse_back(i + 1)
            sp.wait_ge(xo_rdy, 1 + b * 2 + 2)
            sp.sem_inc(passed, 1)
            sp.dma_start(out[b, :, :, :], flat(xio)).then_inc(out_st, 16)
        sp.wait_ge(out_st, 1 + B * 16)
        sp.sem_inc(passed, 1)

    @block.gpsimd
    def _(pool):
        tt = nc.gpsimd.tensor_tensor

        nc.gpsimd.memset(em[:, :, 0:1], 0.0).then_inc(init1, 1)
        nc.gpsimd.memset(flat(T16), 0.0).then_inc(init1, 1)
        nc.gpsimd.memset(flat(T64), 0.0).then_inc(init1, 1)
        nc.gpsimd.memset(flat(Rf), 0.0).then_inc(init1, 1)
        nc.gpsimd.memset(flat(mhalf), -0.5).then_inc(init1, 1)
        pool.wait_ge(init1, 1 + 5)
        pool.wait_ge(loaded, 1 + LOADED)

        def decay_rhs(i, s, bt, c):
            n = lambda k=1, m=1: i * NT * m + c * m + k
            hs = slice(s * GH, (s + 1) * GH)
            pool.wait_ge(e_ps, 1 + n(0))
            pool.wait_ge(coef_rdy, 1 + bt + 1)
            tt(lm[:, :, :], tri[:, INCL:INCL + 1, :].to_broadcast([P, GH, P]),
               la[:, c, hs].rearrange("p (h o) -> p h o", o=1).to_broadcast([P, GH, P]), ALU.mult).then_inc(lm_rdy, 1)

        def rotate(i, s, bt, c):
            n = lambda k=1, m=1: i * NT * m + c * m + k
            pool.wait_ge(rot_rdy, 1 + 2 * n())
            if not (isinstance(i, int) and i == 0 and c < 2):
                pool.wait_ge(kq_ps, 1 + n(-1))
                pool.wait_ge(qkd_mid, 1 + 2 * n(-1))
                pool.wait_ge(kl_rdy, 1 + n(-1))
            tt(qk[:, c % 2, :, :].rearrange("p a n -> p (a n)"), m1[:, :], m2[:, :], ALU.add).then_inc(qk_rdy, 1)

        def normalise(i, s, bt, c):
            n = lambda k=1, m=1: i * NT * m + c * m + k
            pool.wait_ge(ss_rdy, 1 + n())
            tt(rn[:, :], ss[:, :], mhalf[:, 0:2 * GH], ALU.pow).then_inc(rn_rdy, 1)
            pool.wait_ge(rn_rdy, 1 + n())
            q8 = qk[:, c % 2, :, :].rearrange("p a (h d) -> p (a h) d", d=DH)
            tt(q8, q8, heads(rn[:, :], 2 * GH), ALU.mult).then_inc(qkn_rdy, 1)

        def prepare_q(i, s, bt, c):
            n = lambda k=1, m=1: i * NT * m + c * m + k
            hs = slice(s * GH, (s + 1) * GH)
            pool.wait_ge(qkn_rdy, 1 + n())
            pool.wait_ge(qg_ps, 1 + n(0))
            tt(hd(qg[:, :]), hd(qk[:, c % 2, 0, :]), heads(coef[:, G_EXCL, c, hs]), ALU.mult).then_inc(qg_rdy, 1)

        def prepare_k(i, s, bt, c):
            par = s % 2
            hs = slice(s * GH, (s + 1) * GH)
            tt(hd(kl[:, par, c, :]), hd(qk[:, c % 2, 1, :]), heads(coef[:, B_AFTER, c, hs]), ALU.mult).then_inc(kl_rdy, 1)

        def recur(i, s, bt, c):
            n = lambda k=1, m=1: i * NT * m + c * m + k
            par = s % 2
            if 0 < c < NT - 1:
                pool.wait_ge(st_rdy, 1 + val(i, NT - 1, c))
                pool.wait_ge(gt_rdy, 1 + 2 * n())
                tt(Sg[:, :, :], St[:, (c - 1) % 2, :, :], heads(gt[:, par, c, :], GP), ALU.mult).then_inc(sg_rdy, 1)
            pool.wait_ge(dq_rdy, 1 + val(i, NT, c + 1))
            pool.wait_ge(os_rdy, 1 + 2 * n(0))
            pool.wait_ge(v_rdy, 1 + val(i, NT, c + 1))
            tt(vq[:, :, :, :].rearrange("p a j d -> p (a j) d"), hd(v[:, par, c, :]), heads(dq[:, par, c, :]), ALU.mult).then_inc(vq_rdy, 1)

        def gate_heads(i, s):
            o3 = flat(on).rearrange("p c (h d) -> p (c h) d", d=DH)
            pool.wait_ge(ms_rdy, 1 + i + 1)
            tt(ro[:, :], ms[:, :], mhalf[:, :], ALU.pow).then_inc(ro_rdy, 1)
            pool.wait_ge(ro_rdy, 1 + i + 1)
            tt(o3, o3, heads(ro[:, :], NQ), ALU.mult).then_inc(on_mid, 1)
            pool.wait_ge(on_mid, 1 + i + 1)
            tt(o3, o3, onw[:, :].rearrange("p (o d) -> p o d", o=1).to_broadcast([P, NQ, DH]), ALU.mult).then_inc(on_rdy, 1)
            pool.wait_ge(sl_rdy, 1 + i + 1)
            pool.wait_ge(g_rdy, 1 + val(i, NT, NT))
            tt(flat(on).rearrange("p c n -> p (c n)"), flat(on).rearrange("p c n -> p (c n)"),
               gsb[:, s % 2, :, :].rearrange("p c n -> p (c n)"), ALU.mult).then_inc(og_rdy, 1)

        def tiles(i, s, bt, now=None):
            for c in range(NT):
                prepare_q(i, s, bt, c)
                if now:
                    recur(*now, c)
                if c + 1 < NT:
                    normalise(i, s, bt, c + 1)
                prepare_k(i, s, bt, c)
                if c + 1 < NT:
                    decay_rhs(i, s, bt, c + 1)
                if c + 2 < NT:
                    rotate(i, s, bt, c + 2)

        def begin(i, s, bt):
            decay_rhs(i, s, bt, 0)
            rotate(i, s, bt, 0)
            normalise(i, s, bt, 0)
            rotate(i, s, bt, 1)

        begin(0, 0, 0)
        tiles(0, 0, 0)
        begin(1, 1, 0)
        with pool.Fori(0, B) as b:
            for s in range(NG):
                i = b * NG + s
                tiles(i + 1, (s + 1) % NG, b + (s + 1) // NG, (i, s, b))
                gate_heads(i, s)
                begin(i + 2, (s + 2) % NG, b + (s + 2) // NG)

    @block.scalar
    def _(act):
        A = nc.scalar.activation

        def gates(nb):
            act.wait_ge(zg_rdy, 1 + 2 * nb + 2)
            A(eb[:, :, :], zg[:, :, 0:H], ACT.Exp, scale=-1.0).then_inc(eb_rdy, 1)
            A(ab[:, :, :], zg[:, :, H:], ACT.Abs).then_inc(ab_rdy, 1)
            act.wait_ge(ab_rdy, 1 + nb + 1)
            A(ab[:, :, :], ab[:, :, :], ACT.Exp, scale=-1.0).then_inc(abe_rdy, 1)
            act.wait_ge(abe_rdy, 1 + nb + 1)
            A(sp1[:, :, :], ab[:, :, :], ACT.Ln, bias=one_ap).then_inc(sp_rdy, 1)
            act.wait_ge(sum_ps, 1 + nb + 1)
            act.wait_ge(kl_rdy, 1 + nb * NG * NT)
            A(coef[:, G_INCL:G_ALL + 1, :, :].rearrange("p k c h -> p (k c h)"), ps[:, 4, 0:4 * NT * H], ACT.Exp).then_inc(sum_rdy, 1)

        def conv(i, s, ns):
            for n in ns:
                X, t = n // CT, n % CT
                act.wait_ge(cv_ps, 1 + val(i, 6, n + 1))
                act.wait_ge(cv_rdy, 1 + val(i, 6, max(0, n - 1)))
                A(acc[:, n % 2, :], ps[:, CV_BANK[n], :], ACT.Identity, bias=cw[:, X, s * CT + t, TAPS:TAPS + 1],
                  scale=cw[:, X, s * CT + t, TAPS - 1:TAPS]).then_inc(cv_t0, 1)
                if n > 0:
                    silu(i, n - 1)

        def silu(i, n):
            X, t = n // CT, n % CT
            act.wait_ge(cv_acc, 1 + val(i, 6, n + 1))
            if n == 0:
                act.wait_ge(in_ps, 1 + i * NT)
            A(xc[:, X, t, :], acc[:, n % 2, :], ACT.Silu).then_inc(cv_rdy, 1)

        def g_copies(i, s):
            if not (isinstance(i, int) and i < 2):
                act.wait_ge(og_rdy, 1 + i - 1)
            for c in range(NT):
                act.wait_ge(g_ps, 1 + val(i, NT, c + 1))
                A(gsb[:, s % 2, c, :], ps[:, 2 + c % 2, 0:GW], ACT.Copy).then_inc(g_rdy, 1)

        def intake(i, s, bt, c):
            n = lambda k=1, m=1: i * NT * m + c * m + k
            par = s % 2
            act.wait_ge(vin_ps, 1 + n())
            A(v[:, par, c, :], ps[:, V_BANK[c], 0:GW], ACT.Copy).then_inc(v_rdy, 1)
            act.wait_ge(coef_rdy, 1 + bt + 1)
            if not (isinstance(i, int) and i < 2):
                act.wait_ge(sg_rdy, 1 + (i - 1) * (NT - 2))
            for j in range(2):
                r = slice(j * DH, (j + 1) * DH)
                A(gt[r, par, c, :], coef[r, G_ALL, c, s * GH:(s + 1) * GH].rearrange("p (a j) -> p a j", j=2)[:, :, j],
                  ACT.Copy).then_inc(gt_rdy, 1)

        def squares(i, s, bt, c):
            n = lambda k=1, m=1: i * NT * m + c * m + k
            act.wait_ge(qk_rdy, 1 + n())
            A(sq[:, :], qk[:, c % 2, :, :].rearrange("p a n -> p (a n)"), ACT.Square).then_inc(sq_rdy, 1)

        def decay_exp(i, s, bt, c):
            n = lambda k=1, m=1: i * NT * m + c * m + k
            act.wait_ge(e_ps, 1 + n())
            act.wait_ge(lt_rdy, 1 + 2 * n(0))
            act.wait_ge(em_rdy, 1 + n(0))
            A(flat(ex).rearrange("p h t -> p (h t)"), ps[:, 6, :], ACT.Exp).then_inc(ex_rdy, 1)

        def prepare(i, s, bt, c):
            n = lambda k=1, m=1: i * NT * m + c * m + k
            par = s % 2
            act.wait_ge(kq_ps, 1 + n())
            act.wait_ge(kk_ps, 1 + n(0))
            A(flat(kqT).rearrange("p a k t -> p (a k t)"), ps[:, 7, :], ACT.Copy).then_inc(kqT_rdy, 1)
            act.wait_ge(kb_ps, 1 + n())
            A(flat(kbT).rearrange("p a t -> p (a t)"), ps[:, 4, 0:GW], ACT.Copy).then_inc(kbT_rdy, 1)
            A(kgT[:, par, c, :, :].rearrange("p a t -> p (a t)"), ps[:, 4, GW:2 * GW], ACT.Copy).then_inc(kgT_rdy, 1)
            act.wait_ge(qg_ps, 1 + n())
            A(qgT[:, par, c, :, :].rearrange("p a t -> p (a t)"), ps[:, 5, 0:GW], ACT.Copy).then_inc(qgT_rdy, 1)

        def recur(i, s, bt, c):
            n = lambda k=1, m=1: i * NT * m + c * m + k
            act.wait_ge(u_ps, 1 + n())
            act.wait_ge(o_ps, 1 + n(0))
            A(flat(us).rearrange("p h d -> p (h d)"), ps[:, 2, 0:GW], ACT.Copy).then_inc(us_rdy, 1)

        def out_squares(i, s, bt):
            act.wait_ge(os_rdy, 1 + val(i, 2 * NT, 2 * NT))
            if s == 0:
                act.wait_ge(wo_ps, 1 + KC * bt)
            A(osq(s), flat(on).rearrange("p c n -> p (c n)"), ACT.Square).then_inc(osq_rdy, 1)

        def out_heads(i, s):
            act.wait_ge(on_rdy, 1 + i + 1)
            A(flat(on), flat(on), ACT.Silu).then_inc(sl_rdy, 1)

        def out_heads_T(i, s, bt):
            for k in range(CT):
                act.wait_ge(oT_ps, 1 + 2 * i + k + 1)
                A(oT[:, s * CT + k, :], ps[:, 2 + k, :], ACT.Copy).then_inc(oT_rdy, 1)

        def merge(i, s, bt):
            act.wait_ge(y32_ps, 1 + i + 1)
            for r in range(2):
                q = slice(64 * r + 32, 64 * r + 64)
                A(Y32[q, :, :].rearrange("p q t -> p (q t)"), ps[q, 7, :], ACT.Copy).then_inc(y32_rdy, 1)
            intake(i + 1, s, bt, 0)
            act.wait_ge(r32_ps, 1 + i + 1)
            for r in range(2):
                q = slice(64 * r, 64 * r + 32)
                A(Rf[q, :, 64 * r + 32:64 * r + 64], ps[q, 4, :].rearrange("p (q t) -> p q t", q=NQ), ACT.Copy,
                  scale=-1.0).then_inc(rf_b, 1)
            squares(i + 1, s, bt, 0)
            act.wait_ge(y64_ps, 1 + i + 1)
            for k in range(2):
                A(Y64[64:, 8 * k:8 * k + 8, :].rearrange("p q t -> p (q t)"), ps[64:, 6 + k, :], ACT.Copy).then_inc(y64_rdy, 1)
            act.wait_ge(r64_ps, 1 + i + 1)
            for k in range(2):
                A(Rf[0:64, 8 * k:8 * k + 8, 64:], ps[0:64, 4 + k, :].rearrange("p (q t) -> p q t", q=8), ACT.Copy,
                  scale=-1.0).then_inc(rf_c, 1)
            squares(i + 1, s, bt, 1)

        act.wait_ge(loaded, 1 + LOADED)
        act.wait_ge(init0, 1 + 1)
        A(expA[:, :], rows[:, 3, :], ACT.Exp).then_inc(init0, 1)
        gates(0)
        conv(0, 0, range(6))
        silu(0, 5)
        g_copies(0, 0)

        def tiles(i, s, bt, now=None):
            for c in range(NT):
                decay_exp(i, s, bt, c)
                if now:
                    recur(*now, c)
                prepare(i, s, bt, c)
                if c + 1 < NT:
                    intake(i, s, bt, c + 1)
                if c + 2 < NT:
                    squares(i, s, bt, c + 2)

        intake(0, 0, 0, 0)
        squares(0, 0, 0, 0)
        squares(0, 0, 0, 1)
        tiles(0, 0, 0)
        conv(1, 1, range(6))
        silu(1, 5)
        g_copies(1, 1)
        act.wait_ge(init1, 1 + 5)
        merge(0, 1, 0)
        with act.Fori(0, B) as b:
            for s in range(NG):
                i = b * NG + s
                tiles(i + 1, (s + 1) % NG, b + (s + 1) // NG, (i, s, b))
                if s == 2:
                    gates(b + 1)
                out_squares(i, s, b)
                conv(i + 2, (s + 2) % NG, range(3))
                out_heads(i, s)
                conv(i + 2, (s + 2) % NG, range(3, 4))
                g_copies(i + 2, (s + 2) % NG)
                conv(i + 2, (s + 2) % NG, range(4, 6))
                silu(i + 2, 5)
                out_heads_T(i, s, b)
                merge(i + 1, (s + 2) % NG, b + (s + 2) // NG)

    @block.vector
    def _(dve):
        V = nc.vector
        V.memset(one_t[:, :], 1.0).then_inc(init0, 1)
        dve.wait_ge(loaded, 1 + LOADED)
        dve.wait_ge(init0, 1 + 2)

        def gates(nb):
            dve.wait_ge(zg_ps, 1 + nb + 1)
            dve.wait_ge(kl_rdy, 1 + nb * NG * NT)
            z3 = zg[:, :, :]
            dve.wait_ge(eb_rdy, 1 + nb)
            V.tensor_tensor(z3, ps[:, 5, 0:2 * H * NT].rearrange("p (c h) -> p c h", c=NT),
                            rows[:, 0:2, :].rearrange("p (o a) h -> p o (a h)", o=1).to_broadcast([P, NT, 2 * H]),
                            ALU.add).then_inc(zg_rdy, 1)
            dve.wait_ge(zg_rdy, 1 + 2 * nb + 1)
            V.tensor_tensor(zg[:, :, H:], zg[:, :, H:], rows[:, 2:3, :].to_broadcast([P, NT, H]), ALU.add).then_inc(zg_rdy, 1)
            dve.wait_ge(zg_rdy, 1 + 2 * nb + 2)
            dve.wait_ge(eb_rdy, 1 + nb + 1)
            V.tensor_scalar(eb[:, :, :], eb[:, :, :], 1.0, None, ALU.add).then_inc(gstep, 1)
            dve.wait_ge(gstep, 1 + nb * 4 + 1)
            V.reciprocal(coef[:, BETA, :, :], eb[:, :, :]).then_inc(gstep, 1)
            dve.wait_ge(sp_rdy, 1 + nb + 1)
            V.scalar_tensor_tensor(out=sp1[:, :, :], in0=zg[:, :, H:], scalar=0.0, in1=sp1[:, :, :],
                                   op0=ALU.max, op1=ALU.add).then_inc(gstep, 1)
            dve.wait_ge(gstep, 1 + nb * 4 + 3)
            V.scalar_tensor_tensor(out=sp1[:, :, :], in0=sp1[:, :, :], scalar=-1.0,
                                   in1=expA[:, :].rearrange("p (o h) -> p o h", o=1).to_broadcast([P, NT, H]),
                                   op0=ALU.mult, op1=ALU.mult).then_inc(gstep, 1)
            dve.wait_ge(gstep, 1 + nb * 4 + 4)
            V.tensor_scalar(la[:, :, :], sp1[:, :, :], LOG_FLOOR, None, ALU.max).then_inc(la_rdy, 1)
            dve.wait_ge(sum_rdy, 1 + nb + 1)
            V.tensor_tensor(coef[:, B_AFTER, :, :], coef[:, BETA, :, :], coef[:, G_AFTER, :, :], ALU.mult).then_inc(coef_rdy, 1)

        def conv_items(i, s, ns):
            for n in ns:
                X, t = n // CT, n % CT
                dve.wait_ge(cv_t0, 1 + val(i, 6, n + 1))
                a = acc[:, n % 2, :]
                for k in range(1, TAPS):
                    if k > 1:
                        dve.wait_ge(cv_mid, 1 + val(i, 12, 2 * n + k - 1))
                    V.scalar_tensor_tensor(out=a[:, k:], in0=ps[:, CV_BANK[n], 0:T - k],
                                           scalar=cw[:, X, s * CT + t, TAPS - 1 - k:TAPS - k], in1=a[:, k:],
                                           op0=ALU.mult, op1=ALU.add).then_inc(cv_mid if k < TAPS - 1 else cv_acc, 1)

        def intake(i, s, bt, c):
            n = lambda k=1, m=1: i * NT * m + c * m + k
            dve.wait_ge(in_ps, 1 + n())
            dve.wait_ge(qk_rdy, 1 + n(0))
            src = ps[:, 3, :].rearrange("p (h i e) -> p h e i", h=2 * GH, e=2)
            for e, m, name in ((0, m1, rot_rdy), (1, m2, rot_rdy)):
                V.tensor_tensor(m[:, :].rearrange("p (h a i) -> p h a i", h=2 * GH, a=2),
                                src[:, :, e:e + 1, :].to_broadcast([P, 2 * GH, 2, DH // 2]),
                                rope[:, c, e:e + 1, :, :].to_broadcast([P, 2 * GH, 2, DH // 2]), ALU.mult).then_inc(name, 1)

        def norms(i, s, bt, c):
            n = lambda k=1, m=1: i * NT * m + c * m + k
            dve.wait_ge(sq_rdy, 1 + n())
            dve.wait_ge(rn_rdy, 1 + n(0))
            V.tensor_reduce(ss[:, :], hd(sq[:, :], 2 * GH), AX.X, ALU.add).then_inc(ss_mid, 1)
            dve.wait_ge(ss_mid, 1 + n())
            V.tensor_scalar(ss[:, :], ss[:, :], RMS_EPS, None, ALU.add).then_inc(ss_rdy, 1)

        def scale_keys(i, s, bt, c):
            n = lambda k=1, m=1: i * NT * m + c * m + k
            dve.wait_ge(qkn_rdy, 1 + n())
            dve.wait_ge(kb_ps, 1 + n(0))
            for k, name in ((0, BETA), (1, G_INCL)):
                V.tensor_tensor(hd(kbg[:, k, :]), hd(qk[:, c % 2, 1, :]), heads(coef[:, name, c, s * GH:(s + 1) * GH]),
                                ALU.mult).then_inc(kbg_rdy, 1)

        def mask_decay(i, s, bt, c):
            n = lambda k=1, m=1: i * NT * m + c * m + k
            dve.wait_ge(ex_rdy, 1 + n())
            dve.wait_ge(at_rdy, 1 + 2 * n(0))
            V.tensor_tensor(em[:, :, 1:], ex[:, :, 0:P - 1], mshift[:, 1:].rearrange("p (o t) -> p o t", o=1).to_broadcast([P, GH, P - 1]),
                            ALU.mult).then_inc(em_rdy, 1)

        def products(i, s, bt, c):
            n = lambda k=1, m=1: i * NT * m + c * m + k
            par = s % 2
            dve.wait_ge(kk_ps, 1 + n())
            dve.wait_ge(em_rdy, 1 + n())
            for j in range(2):
                bank = ps[:, 6 + j, :].rearrange("p (a k t) -> p a k t", a=GP, k=2)
                pick = lambda t: t.rearrange("p (a j) t -> p a j t", j=2)[:, :, j, :]
                V.tensor_tensor(pick(LT[:, c, :, :]), bank[:, :, 0, :], pick(ex[:, :, :]), ALU.mult).then_inc(lt_rdy, 1)
                V.tensor_tensor(pick(AT[:, par, c, :, :]), bank[:, :, 1, :], pick(em[:, :, :]), ALU.mult).then_inc(at_rdy, 1)

        def dot_qk(i, s, bt, c):
            n = lambda k=1, m=1: i * NT * m + c * m + k
            dve.wait_ge(qkn_rdy, 1 + n())
            V.tensor_tensor(qkp, qk[:, c % 2, 0, :], qk[:, c % 2, 1, :], ALU.mult).then_inc(qkd_mid, 1)
            dve.wait_ge(qkd_mid, 1 + 2 * n(0) + 1)
            V.tensor_reduce(qkd[:, :], hd(qkp), AX.X, ALU.add).then_inc(qkd_mid, 1)
            dve.wait_ge(qkd_mid, 1 + 2 * n())
            V.tensor_tensor(dq[:, s % 2, c, :], qkd[:, :], rows[:, 4, s * GH:(s + 1) * GH], ALU.mult).then_inc(dq_rdy, 1)

        def substitute(i):
            dve.wait_ge(lb_rd, 1 + i * 32 + 32)
            dve.wait_ge(tb_wr, 1 + i * 32)
            for t in range(1, BL):
                k = val(i, 2 * (BL - 1), 2 * t - 1)
                pv = pb[:, 0:t * t].rearrange("p (c j) -> p c j", c=t)
                V.tensor_tensor(pv, LB[:, 0:t, t:t + 1].rearrange("p j o -> p o j").to_broadcast([P, t, t]),
                                TB[:, 0:t, 0:t].rearrange("p j c -> p c j"), ALU.mult).then_inc(tbs, 1)
                dve.wait_ge(tbs, 1 + k)
                last = V.tensor_reduce(TB[:, t, 0:t], pv, AX.X, ALU.add, negate=True).then_inc(tbs, 1)
                dve.wait_ge(tbs, 1 + k + 1)
            V.memset(pb[:, 0:1], 0.0).then_inc(tb_step, 1)

        def merge16(i):
            dve.wait_ge(t16_rd, 1 + i * 64 + 64)
            V.transpose(flat(R16).rearrange("p q t -> p (q t)"), flat(T16).rearrange("p q t -> p (q t)")).then_inc(r16_rdy, 1)
            dve.wait_ge(y16_ps, 1 + i + 1)
            dve.wait_ge(r32_ps, 1 + i)
            dve.wait_ge(t32_ps, 1 + i)
            V.tensor_tensor(flat(Y16), ps[:, 4, :].rearrange("p (q t) -> p q t", q=NQ),
                            m16[:, :].rearrange("p (o t) -> p o t", o=1).to_broadcast([P, NQ, 32]), ALU.mult).then_inc(y16_rdy, 1)

        def merge16_end(i):
            dve.wait_ge(t16_ps, 1 + i + 1)
            V.tensor_tensor(flat(kbg).rearrange("p k n -> p (k n)"), flat(T16).rearrange("p q t -> p (q t)"), ps[:, 6, :],
                            ALU.subtract).then_inc(t32_rdy, 1)
            dve.wait_ge(t32_rdy, 1 + i + 1)
            V.transpose(flat(R32).rearrange("p q t -> p (q t)"), flat(kbg).rearrange("p k n -> p (k n)")).then_inc(r32_rdy, 1)

        def merge32(i, s, bt):
            dve.wait_ge(r32_rdy, 1 + i + 1)
            dve.wait_ge(t32_rdy, 1 + i + 1)
            dve.wait_ge(u_ps, 1 + i * NT)
            for r in range(4):
                q = slice(32 * r, 32 * r + 32)
                V.tensor_copy(Rf[q, :, q], R32[q, :, :]).then_inc(rf_a, 1)
            dve.wait_ge(y64_ps, 1 + i)
            for r in range(2):
                q = slice(32 * r, 32 * r + 32)
                V.tensor_copy(T64[q, :, q], T32[q, :, :]).then_inc(t64_rdy, 1)
            intake(i + 1, s, bt, 0)
            dve.wait_ge(t32_ps, 1 + i + 1)
            V.tensor_scalar(T64[32:64, :, 0:32], ps[32:64, 5, :].rearrange("p (q t) -> p q t", q=NQ), -1.0, None,
                            ALU.mult).then_inc(t64_rdy, 1)
            norms(i + 1, s, bt, 0)
            intake(i + 1, s, bt, 1)

        def solve_rhs(i, s, bt, c):
            n = lambda k=1, m=1: i * NT * m + c * m + k
            par = s % 2
            if c > 0:
                dve.wait_ge(x_ps, 1 + val(i, NT - 1, c))
                dve.wait_ge(u_ps, 1 + n(0))
                dve.wait_ge(v_rdy, 1 + n())
                for j in range(2):
                    V.tensor_tensor(rh[:, :, j, :], v[:, par, c, :].rearrange("p (a j d) -> p a j d", a=GP, j=2)[:, :, j, :],
                                    ps[:, j, 0:GP * DH].rearrange("p (a d) -> p a d", a=GP), ALU.subtract).then_inc(rh_rdy, 1)

        def state(i, s, bt, c):
            if c < NT - 1:
                dve.wait_ge(s_ps, 1 + val(i, NT - 1, c + 1))
                dst = St[:, c % 2, :, :].rearrange("p a d -> p (a d)")
                src = ps[:, 2, GW:GW + GP * DH]
                if c == 0:
                    V.tensor_copy(dst, src).then_inc(st_rdy, 1)
                else:
                    dve.wait_ge(sg_rdy, 1 + val(i, NT - 2, c))
                    V.tensor_tensor(dst, flat(Sg).rearrange("p a d -> p (a d)"), src, ALU.add).then_inc(st_rdy, 1)

        def outputs(i, s, bt, c):
            n = lambda k=1, m=1: i * NT * m + c * m + k
            dve.wait_ge(o_ps, 1 + n())
            dve.wait_ge(vq_rdy, 1 + n())
            if c == 0:
                dve.wait_ge(oT_ps, 1 + 2 * i)
                dve.wait_ge(zT_ps, 1 + 2 * bt)
            o4 = on[:, c, :].rearrange("p (a j d) -> p a j d", a=GP, j=2)
            for j in range(2):
                V.tensor_tensor(o4[:, :, j, :], ps[:, j, 0:GP * DH].rearrange("p (a d) -> p a d", a=GP), vq[:, :, j, :],
                                ALU.add).then_inc(os_rdy, 1)

        def mean_squares(i, s):
            dve.wait_ge(osq_rdy, 1 + i + 1)
            dve.wait_ge(ro_rdy, 1 + i)
            V.tensor_reduce(ms[:, :], hd(osq(s), NQ), AX.X, ALU.add).then_inc(ms_mid, 1)
            dve.wait_ge(ms_mid, 1 + i + 1)
            V.tensor_scalar(ms[:, :], ms[:, :], 1.0 / DH, RMS_EPS, ALU.mult, ALU.add).then_inc(ms_rdy, 1)

        def output(b):
            for m in range(KC):
                dve.wait_ge(wo_ps, 1 + b * KC + m + 1)
                if m == 0:
                    dve.wait_ge(gate_in, 1 + b * 16 + 16)
                    dve.wait_ge(zT_ps, 1 + b * 2)
                V.tensor_tensor(z[:, m, :], ps[:, m, :], gate[:, m, :], ALU.mult).then_inc(z_rdy, 1)
            dve.wait_ge(x_in, 1 + b * 16 + 16)
            for k in range(2):
                dve.wait_ge(zT_ps, 1 + b * 2 + k + 1)
                xv = xio[:, 2 * k:2 * k + 2, :].rearrange("p w n -> p (w n)")
                V.tensor_tensor(xv, xv, ps[:, 2 + k, :], ALU.add).then_inc(xo_rdy, 1)

        gates(0)
        conv_items(0, 0, range(6))

        def tiles(i, s, bt, now=None):
            for c in range(NT):
                if now:
                    solve_rhs(*now, c)
                scale_keys(i, s, bt, c)
                mask_decay(i, s, bt, c)
                if c + 1 < NT:
                    norms(i, s, bt, c + 1)
                dot_qk(i, s, bt, c)
                if now:
                    state(*now, c)
                    outputs(*now, c)
                if c + 2 < NT:
                    intake(i, s, bt, c + 2)
                products(i, s, bt, c)

        intake(0, 0, 0, 0)
        norms(0, 0, 0, 0)
        intake(0, 0, 0, 1)
        tiles(0, 0, 0)
        conv_items(1, 1, range(0, 2))
        substitute(0)
        conv_items(1, 1, range(2, 6))
        dve.wait_ge(init1, 1 + 5)
        merge16(0)
        merge16_end(0)
        merge32(0, 1, 0)
        with dve.Fori(0, B) as b:
            for s in range(NG):
                i = b * NG + s
                tiles(i + 1, (s + 1) % NG, b + (s + 1) // NG, (i, s, b))
                if s == 2:
                    gates(b + 1)
                mean_squares(i, s)
                conv_items(i + 2, (s + 2) % NG, range(0, 2))
                substitute(i + 1)
                conv_items(i + 2, (s + 2) % NG, range(2, 4))
                merge16(i + 1)
                conv_items(i + 2, (s + 2) % NG, range(4, 6))
                merge16_end(i + 1)
                if s == NG - 1:
                    output(b)
                merge32(i + 1, (s + 2) % NG, b + (s + 2) // NG)

    @block.tensor
    def _(pe):
        mm, tr = nc.tensor.matmul, nc.tensor.transpose

        def gates(nb):
            pe.wait_ge(xn_in, 1 + nb * 16 + 16)
            pe.wait_ge(qgT_rdy, 1 + nb * NG * NT)
            for c in range(NT):
                for k in range(KC):
                    last = mm(ps[:, 5, c * 2 * H:(c + 1) * 2 * H], xnT[:, k, c * P:(c + 1) * P], wgate[:, k, :],
                              start=k == 0, stop=k == KC - 1)
            last.then_inc(zg_ps, 1)

        def gate_sums(nb):
            pe.wait_ge(la_rdy, 1 + nb + 1)
            for k in range(4):
                last = mm(ps[:, 4, k * NT * H:(k + 1) * NT * H], tri[:, k, :], la[:, :, :].rearrange("p c h -> p (c h)"),
                          start=True, stop=True)
            last.then_inc(sum_ps, 1)

        def g_proj(i, s):
            for c in range(NT):
                if c < 2:
                    if not (isinstance(i, int) and i < 2):
                        pe.wait_ge(us_rdy, 1 + (i - 1) * NT)
                        pe.wait_ge(st_rdy, 1 + (i - 1) * (NT - 1))
                    if not (isinstance(i, int) and i == 0):
                        pe.wait_ge(rot_rdy, 1 + 2 * i * NT)
                else:
                    pe.wait_ge(g_rdy, 1 + val(i, NT, c - 1))
                for k in range(KC):
                    last = mm(ps[:, 2 + c % 2, 0:GW], xnT[:, k, c * P:(c + 1) * P], wg[:, k, s * GW:(s + 1) * GW],
                              start=k == 0, stop=k == KC - 1)
                last.then_inc(g_ps, 1)

        def conv(i, s, bt):
            for n in range(6):
                X, t = n // CT, n % CT
                if n < 4:
                    if not (isinstance(i, int) and i == 0):
                        pe.wait_ge(at_rdy, 1 + i * 2 * NT)
                        pe.wait_ge(qgT_rdy, 1 + i * NT)
                    if s == 0:
                        pe.wait_ge(sum_rdy, 1 + bt + 1)
                elif not (isinstance(i, int) and i < 2):
                    pe.wait_ge(os_rdy, 1 + (i - 1) * 2 * NT)
                elif not (isinstance(i, int) and i == 0):
                    pe.wait_ge(v_rdy, 1 + i * NT)
                for k in range(KC):
                    last = mm(ps[:, CV_BANK[n], :], wqkv[:, X, k, s * GW + t * P:s * GW + (t + 1) * P], xnT[:, k, :],
                              start=k == 0, stop=k == KC - 1)
                last.then_inc(cv_ps, 1)

        def intake(i, s, bt, c):
            n = lambda k=1, m=1: i * NT * m + c * m + k
            if c == 0:
                pe.wait_ge(cv_rdy, 1 + val(i, 6, 6))
                pe.wait_ge(cv_acc, 1 + val(i, 6, 6))
                if isinstance(i, int):
                    pe.wait_ge(g_rdy, 1 + (i + 1) * NT)
                else:
                    pe.wait_ge(oT_rdy, 1 + (i - 1) * CT)
                    if s == 1:
                        pe.wait_ge(xo_rdy, 1 + 2 * bt)
            pe.wait_ge(rot_rdy, 1 + 2 * n(0))
            for X in range(2):
                for t in range(CT):
                    last = tr(ps[:, 3, X * GW + t * P:X * GW + (t + 1) * P], xc[:, X, t, c * P:(c + 1) * P], ident[:, :])
            last.then_inc(in_ps, 1)

        def intake_v(i, s, bt, c):
            n = lambda k=1, m=1: i * NT * m + c * m + k
            if c > 0:
                pe.wait_ge(qgT_rdy, 1 + n(0))
            for t in range(CT):
                last = tr(ps[:, V_BANK[c], t * P:(t + 1) * P], xc[:, 2, t, c * P:(c + 1) * P], ident[:, :])
            last.then_inc(vin_ps, 1)

        def decay_sums(i, s, bt, c):
            n = lambda k=1, m=1: i * NT * m + c * m + k
            if c == 0:
                pe.wait_ge(rf_c, 1 + 2 * i)
            pe.wait_ge(lm_rdy, 1 + n())
            pe.wait_ge(lt_rdy, 1 + 2 * n(0))
            pe.wait_ge(at_rdy, 1 + 2 * n(0))
            mm(ps[:, 6, :], tri[:, AFTER, :], lm[:, :, :].rearrange("p h t -> p (h t)"), start=True, stop=True).then_inc(e_ps, 1)

        def keys_T(i, s, bt, c):
            n = lambda k=1, m=1: i * NT * m + c * m + k
            pe.wait_ge(qkn_rdy, 1 + n())
            for t in range(GP):
                for k, part in ((0, 1), (1, 0)):
                    last = tr(ps[:, 7, (2 * t + k) * P:(2 * t + k + 1) * P], qk[:, c % 2, part, t * P:(t + 1) * P], ident[:, :])
            last.then_inc(kq_ps, 1)
            pe.wait_ge(kbg_rdy, 1 + 2 * n())
            pe.wait_ge(kgT_rdy, 1 + n(0))
            for k in range(2):
                for t in range(GP):
                    last = tr(ps[:, 4, k * GW + t * P:k * GW + (t + 1) * P], kbg[:, k, t * P:(t + 1) * P], ident[:, :])
            last.then_inc(kb_ps, 1)

        def queries_T(i, s, bt, c):
            n = lambda k=1, m=1: i * NT * m + c * m + k
            pe.wait_ge(qg_rdy, 1 + n())
            pe.wait_ge(v_rdy, 1 + n())
            for t in range(GP):
                last = tr(ps[:, 5, t * P:(t + 1) * P], qg[:, t * P:(t + 1) * P], ident[:, :])
            last.then_inc(qg_ps, 1)

        def products(i, s, bt, c):
            n = lambda k=1, m=1: i * NT * m + c * m + k
            pe.wait_ge(kqT_rdy, 1 + n())
            pe.wait_ge(kbT_rdy, 1 + n())
            pe.wait_ge(ex_rdy, 1 + n())
            for j in range(2):
                r = slice(j * DH, (j + 1) * DH)
                for a in range(GP):
                    last = mm(ps[:, 6 + j, a * 2 * P:(a + 1) * 2 * P], kbT[r, a, :],
                              kqT[r, a, :, :].rearrange("p k t -> p (k t)"), start=True, stop=True)
            last.then_inc(kk_ps, 1)

        LTq = LT[:, :, :, :].rearrange("p c h t -> p (c h) t")

        def merge16(i):
            pe.wait_ge(t16_rd, 1 + i * 64 + 64)
            pe.wait_ge(cv_acc, 1 + val(i + 1, 6, 4))
            pe.sem_inc(passed, 1)
            for r in range(4):
                q = slice(32 * r, 32 * r + 32)
                for m in range(NQ):
                    last = mm(ps[q, 4, 32 * m:32 * m + 32], LTq[q, m, q], T16[q, m, :], start=True, stop=True)
            last.then_inc(y16_ps, 1)
            pe.wait_ge(y16_rdy, 1 + i + 1)
            pe.wait_ge(r16_rdy, 1 + i + 1)
            pe.sem_inc(passed, 1)
            for r in range(4):
                q = slice(32 * r, 32 * r + 32)
                for m in range(NQ):
                    last = mm(ps[q, 6, 32 * m:32 * m + 32], R16[q, m, :], Y16[q, m, :], start=True, stop=True)
            last.then_inc(t16_ps, 1)

        def merge32(i, s, bt):
            pe.wait_ge(t32_rdy, 1 + i + 1)
            pe.sem_inc(passed, 1)
            for r in range(2):
                q1, q2 = slice(64 * r, 64 * r + 32), slice(64 * r + 32, 64 * r + 64)
                for m in range(NQ):
                    last = mm(ps[q2, 7, 32 * m:32 * m + 32], LTq[q1, m, q2], T32[q1, m, :], start=True, stop=True)
            last.then_inc(y32_ps, 1)
            intake(i + 1, s, bt, 0)
            intake_v(i + 1, s, bt, 0)
            pe.wait_ge(y32_rdy, 1 + 2 * i + 2)
            pe.wait_ge(r32_rdy, 1 + i + 1)
            pe.sem_inc(passed, 1)
            for r in range(2):
                q1, q2 = slice(64 * r, 64 * r + 32), slice(64 * r + 32, 64 * r + 64)
                for m in range(NQ):
                    last = mm(ps[q1, 4, 32 * m:32 * m + 32], Y32[q2, m, :], R32[q2, m, :], start=True, stop=True)
            last.then_inc(r32_ps, 1)
            q2 = slice(32, 64)
            for m in range(NQ):
                last = mm(ps[q2, 5, 32 * m:32 * m + 32], R32[q2, m, :], Y32[q2, m, :], start=True, stop=True)
            last.then_inc(t32_ps, 1)

        def merge64(i, s, bt):
            pe.wait_ge(t64_rdy, 1 + 3 * i + 3)
            pe.sem_inc(passed, 1)
            for m in range(NQ):
                last = mm(ps[64:, 6 + m // 8, 64 * (m % 8):64 * (m % 8) + 64], LTq[0:64, m, 64:], T64[0:64, m, :], start=True, stop=True)
            last.then_inc(y64_ps, 1)
            intake(i + 1, s, bt, 1)
            pe.wait_ge(y64_rdy, 1 + 2 * i + 2)
            pe.wait_ge(rf_a, 1 + 4 * i + 4)
            pe.wait_ge(rf_b, 1 + 2 * i + 2)
            pe.sem_inc(passed, 1)
            for m in range(NQ):
                last = mm(ps[0:64, 4 + m // 8, 64 * (m % 8):64 * (m % 8) + 64], Y64[64:, m, :], Rf[64:, m, 64:], start=True, stop=True)
            last.then_inc(r64_ps, 1)

        def carried(i, s, bt, c):
            n = lambda k=1, m=1: i * NT * m + c * m + k
            par = s % 2
            if c == 0:
                pe.wait_ge(rf_a, 1 + 4 * i + 4)
                pe.wait_ge(rf_b, 1 + 2 * i + 2)
                pe.wait_ge(rf_c, 1 + 2 * i + 2)
                pe.wait_ge(oT_rdy, 1 + CT * i)
                pe.wait_ge(kl_rdy, 1 + val(i, NT, NT))
                pe.wait_ge(v_rdy, 1 + val(i, NT, NT))
                pe.wait_ge(at_rdy, 1 + val(i, 2 * NT, 2 * NT))
                pe.wait_ge(xo_rdy, 1 + 2 * bt)
                pe.wait_ge(cv_acc, 1 + val(i + 1, 6, 6))
            pe.wait_ge(os_rdy, 1 + 2 * n(0))
            if c > 0:
                pe.wait_ge(st_rdy, 1 + val(i, NT - 1, c))
                for j in range(2):
                    r = slice(j * DH, (j + 1) * DH)
                    for a in range(GP):
                        last = mm(ps[:, j, a * DH:(a + 1) * DH], kgT[r, par, c, a, :], St[r, (c - 1) % 2, a, :], start=True, stop=True)
                last.then_inc(x_ps, 1)

        def solve(i, s, bt, c):
            par = s % 2
            if c > 0:
                pe.wait_ge(rh_rdy, 1 + val(i, 2 * (NT - 1), 2 * c))
            for h in range(GH):
                rhs = rh[:, h // 2, h % 2, :] if c > 0 else v[:, par, c, h * DH:(h + 1) * DH]
                last = mm(ps[:, 2, h * DH:(h + 1) * DH], Rf[:, c * GH + h, :], rhs, start=True, stop=True)
            last.then_inc(u_ps, 1)

        def recur(i, s, bt, c):
            n = lambda k=1, m=1: i * NT * m + c * m + k
            par = s % 2
            pe.wait_ge(us_rdy, 1 + n())
            if c < NT - 1:
                for h in range(GH):
                    a, j = h // 2, h % 2
                    last = mm(ps[j * DH:(j + 1) * DH, 2, GW + a * DH:GW + (a + 1) * DH], kl[:, par, c, h * DH:(h + 1) * DH],
                              us[:, h, :], start=True, stop=True)
                last.then_inc(s_ps, 1)
            pe.wait_ge(v_rdy, 1 + val(i + 1, NT, 1))
            for h in range(GH):
                a, j = h // 2, h % 2
                r = slice(j * DH, (j + 1) * DH)
                dst = ps[:, j, a * DH:(a + 1) * DH]
                if c > 0:
                    mm(dst, qgT[r, par, c, a, :], St[r, (c - 1) % 2, a, :], start=True, stop=False)
                last = mm(dst, AT[:, par, c, h, :], us[:, h, :], start=c == 0, stop=True)
            last.then_inc(o_ps, 1)

        def out_heads(i, s):
            pe.wait_ge(og_rdy, 1 + i + 1)
            pe.wait_ge(g_rdy, 1 + val(i + 2, NT, NT))
            for k in range(CT):
                for c in range(NT):
                    last = tr(ps[:, 2 + k, c * P:(c + 1) * P], on[:, c, k * P:(k + 1) * P], ident[:, :])
                last.then_inc(oT_ps, 1)

        def output(b):
            pe.wait_ge(oT_rdy, 1 + b * NG * CT + NG * CT)
            for m in range(KC):
                for k in range(H * DH // P):
                    last = mm(ps[:, m, :], wo[:, k, m * P:(m + 1) * P], oT[:, k, :], start=k == 0, stop=k == H * DH // P - 1)
                last.then_inc(wo_ps, 1)
            pe.wait_ge(z_rdy, 1 + b * KC + KC)
            for k in range(2):
                for w in range(2):
                    for m in range(KC):
                        last = tr(ps[:, 2 + k, w * D + m * P:w * D + (m + 1) * P], z[:, m, (2 * k + w) * P:(2 * k + w + 1) * P], ident[:, :])
                last.then_inc(zT_ps, 1)

        pe.wait_ge(loaded, 1 + LOADED)
        gates(0)
        gate_sums(0)
        conv(0, 0, 0)
        g_proj(0, 0)

        def tiles(i, s, bt, now=None):
            for c in range(NT):
                if now:
                    carried(*now, c)
                decay_sums(i, s, bt, c)
                if c + 2 < NT:
                    intake(i, s, bt, c + 2)
                if now:
                    solve(*now, c)
                keys_T(i, s, bt, c)
                queries_T(i, s, bt, c)
                if now:
                    recur(*now, c)
                products(i, s, bt, c)
                if c + 1 < NT:
                    intake_v(i, s, bt, c + 1)

        intake(0, 0, 0, 0)
        intake_v(0, 0, 0, 0)
        intake(0, 0, 0, 1)
        tiles(0, 0, 0)
        conv(1, 1, 0)
        g_proj(1, 1)
        pe.wait_ge(init1, 1 + 5)
        merge16(0)
        merge32(0, 1, 0)
        merge64(0, 1, 0)
        with pe.Fori(0, B) as b:
            for s in range(NG):
                i = b * NG + s
                tiles(i + 1, (s + 1) % NG, b + (s + 1) // NG, (i, s, b))
                if s == 2:
                    gates(b + 1)
                    gate_sums(b + 1)
                conv(i + 2, (s + 2) % NG, b + (s + 2) // NG)
                g_proj(i + 2, (s + 2) % NG)
                merge16(i + 1)
                out_heads(i, s)
                if s == NG - 1:
                    output(b)
                merge32(i + 1, (s + 2) % NG, b + (s + 2) // NG)
                merge64(i + 1, (s + 2) % NG, b + (s + 2) // NG)


def delta_layout(i):
    g = lambda n: np.asarray(i["L0_attn_" + n])
    chunks = lambda a: np.ascontiguousarray(a.reshape(-1, P, a.shape[-1]).transpose(1, 0, 2))
    w = np.stack([chunks(g("W" + n)) for n in "qkv"], 1)
    wg, wo = chunks(g("Wg")), chunks(g("Wo"))
    wgate = chunks(np.concatenate([g("bw"), g("gkw")], 1))
    cw = np.stack([np.concatenate([g(n + "cw").reshape(-1, TAPS), g(n + "cb")[:, None]], 1) for n in "qkv"], 0)
    cw = np.ascontiguousarray(cw.reshape(3, -1, P, TAPS + 1).transpose(2, 0, 1, 3))
    rows = np.stack([g(n) for n in ("bb", "gkb", "dt_bias", "A_log", "D_param")])
    full = lambda a: np.ascontiguousarray(np.broadcast_to(a[None], (P,) + a.shape))
    t = np.arange(T, dtype=np.float32)
    inv = (1.0 / 10000.0 ** (np.arange(0, DH, 2, dtype=np.float32) / DH)).astype(np.float32)
    emb = np.concatenate([np.outer(t, inv)] * 2, -1).astype(np.float32)
    co, si = np.cos(emb)[:, ::2], np.sin(emb)[:, ::2]
    rope = np.stack([np.stack([co, si], 1), np.stack([-si, co], 1)], 1).astype(np.float32)
    rope = np.ascontiguousarray(rope.reshape(NT, P, 2, 2, DH // 2).transpose(1, 0, 2, 3, 4))
    a, c = np.arange(P)[:, None], np.arange(P)[None, :]
    tri = np.stack([a <= c, a < c, a > c, np.ones((P, P), bool)], 1).astype(np.float32)
    r, k = np.arange(P)[:, None] % 32, np.arange(32)[None, :]
    return dict(dwqkv=w, dwg=wg, dwo=wo, dwgate=wgate, dcw=cw, drows=full(rows), donw=full(g("onorm_w")), drope=rope,
                dtri=tri, dmshift=(c > a).astype(np.float32), dm16=((r >= 16) & (k < 16)).astype(np.float32),
                deye=full(np.eye(BL, dtype=np.float32)))


def program(nc, io, out):
    xnT = nc.dram_tensor("xnT_scratch", (B + 1, P, KC, T), F32).ap()
    gate = nc.dram_tensor("gate_scratch", (B, P, KC, T), F32).ap()
    Ld = nc.dram_tensor("blocks_scratch", (4, NQ, 2 * BL, 2 * BL), F32).ap()
    Td = nc.dram_tensor("inverse_scratch", (4, NQ, 2 * BL, 2 * BL), F32).ap()
    scratch = dict(xnT=xnT, gate=gate, Ld=Ld, Td=Td)
    tiles = lambda ap: ap.rearrange("b (w p) d -> b p w d", p=P)
    io = dict(io, x=tiles(io["x"]))
    with ExitStack() as ctx:
        ffn_phase(nc, ctx, io, scratch)
    with ExitStack() as ctx:
        delta_phase(nc, ctx, io, scratch, tiles(out))


def kernel(**inputs):
    import concourse.bacc as bacc
    from concourse.bass_utils import run_bass_kernel_spmd

    nc = bacc.Bacc("TRN2", target_bir_lowering=False, num_devices=1)
    arrays = {"in_" + n: a for n, a in (ffn_layout(inputs) | delta_layout(inputs)).items()}
    io = {n[3:]: nc.dram_tensor(n, a.shape, F32, kind="ExternalInput").ap() for n, a in arrays.items()}
    out = nc.dram_tensor("out", (B, T, D), F32, kind="ExternalOutput").ap()
    program(nc, io, out)
    got = run_bass_kernel_spmd(nc, [arrays], core_ids=[0])
    return got.results[0]["out"]
```

```python
import numpy as np
import concourse.bass as bass
from concourse import mybir
from contextlib import ExitStack

F32 = mybir.dt.float32
ALU = mybir.AluOpType
ACT = mybir.ActivationFunctionType
AX = mybir.AxisListType

B, T, D = 8, 512, 256
P = 128
NT = T // P
KC = D // P
LAYERS, FH, DH = 2, 8, 64
INNER = FH * DH
HID = int(D * 4 * 2 / 3)
HM = -(-HID // P)
HROWS = [min(P, HID - m * P) for m in range(HM)]
PAIRS = FH // 2
LN_EPS = 1e-5
NEG = -1e30
W1C = 2 * HID
TURN = ((1, 0), (1, 1), (0, 0), (0, 1), (1, 2), (0, 2), (0, 3), (1, 3))
WARM = 2
UP_BANK = (4, 6, 0)


def ffn_phase(nc, ctx, io, scratch):

    def sb(name, shape):
        return ctx.enter_context(nc.sbuf_tensor("f_" + name, shape, F32))

    sems = []

    def sem(name):
        sems.append(ctx.enter_context(nc.semaphore("f_" + name)))
        return sems[-1]

    wqkv = sb("wqkv", [P, LAYERS, KC, 3 * INNER])
    wo = sb("wo", [P, LAYERS, PAIRS, D])
    w1 = sb("w1", [P, LAYERS, KC, W1C])
    w2 = sb("w2", [P, LAYERS, HM, D])
    b1 = sb("b1", [P, LAYERS, 2, HM])
    vecs = sb("vecs", [P, LAYERS, 3, KC])
    scales = sb("scales", [P, LAYERS, 4, DH])
    trig = sb("trig", [P, NT, 4, DH])
    rope = sb("rope", [P, LAYERS, NT, 4, DH])
    ident = sb("ident", [P, P])
    mask = sb("mask", [P, 2 * P])
    mean_w = sb("mean_w", [P, P])

    xin = sb("xin", [P, NT, D])
    xnorm = sb("xnorm", [P, NT, D])
    stats = sb("stats", [P, NT, 6])
    mv = sb("mv", [P, NT, 2])
    rstd = sb("rstd", [P, NT])
    xT = sb("xT", [P, KC, T + 2])
    qk = sb("qk", [P, NT, 2, INNER])
    v = sb("v", [P, NT, INNER])
    m1 = sb("m1", [P, 2, INNER])
    m2 = sb("m2", [P, 2, INNER])
    sq = sb("sq", [P, 2, INNER])
    ssq = sb("ssq", [P, 2, NT, FH])
    nrm = sb("nrm", [P, 2, NT, FH])
    rn = sb("rn", [P, 2, NT, FH])
    qsc = sb("qsc", [P, 2, NT, FH])
    qT = sb("qT", [P, PAIRS, T])
    kT = sb("kT", [P, PAIRS, T])
    sm = sb("sm", [P, 2, 2, 2 * P])
    pr = sb("pr", [P, 2, 2, 2 * P])
    mx = sb("mx", [P, 2, 2])
    nb = sb("nb", [P, 2, 2])
    rsum = sb("rsum", [P, NT, FH])
    rinv = sb("rinv", [P, NT, FH])
    pT = sb("pT", [P, 2, 4, P])
    osb = sb("osb", [P, 2, INNER])
    oT = sb("oT", [P, PAIRS, T])
    xc, xsq = m1, m2
    std = sb("std", [P, T])
    rst = sb("rst", [P, T])
    gm = sq
    xo = sb("xo", [P, KC, T])
    gact = sb("gact", [P, 2, T])
    hh = qk[:, :, :, :].rearrange("p w k n -> p (w k) n")
    gate = sb("gate", [P, KC, T])
    ps = ctx.enter_context(nc.psum_tensor("f_ps", [P, 8, 512], F32))

    loaded = sem("loaded")
    x_in = sem("x_in")
    xn_st = sem("xn_st")
    gate_st = sem("gate_st")
    rope_rdy = sem("rope_rdy")
    ln_step = sem("ln_step")
    ln_std = sem("ln_std")
    xn_rdy = sem("xn_rdy")
    w1_rdy = sem("w1_rdy")
    b1_ps = sem("b1_ps")
    xnT_ps = sem("xnT_ps")
    xT_rdy = sem("xT_rdy")
    qkv_ps = sem("qkv_ps")
    qkv_act = sem("qkv_act")
    v_ps = sem("v_ps")
    v_rdy = sem("v_rdy")
    rot_m = sem("rot_m")
    rot_rdy = sem("rot_rdy")
    ssq_rdy = sem("ssq_rdy")
    nrm_rdy = sem("nrm_rdy")
    rn_step = sem("rn_step")
    k_rdy = sem("k_rdy")
    qkT_ps = sem("qkT_ps")
    qkT_rdy = sem("qkT_rdy")
    sc_ps = sem("sc_ps")
    sm_rdy = sem("sm_rdy")
    nb_rdy = sem("nb_rdy")
    pr_rdy = sem("pr_rdy")
    pT_ps = sem("pT_ps")
    pT_rdy = sem("pT_rdy")
    o_ps = sem("o_ps")
    ri_rdy = sem("ri_rdy")
    o_rdy = sem("o_rdy")
    oT_ps = sem("oT_ps")
    oT_rdy = sem("oT_rdy")
    wo_ps = sem("wo_ps")
    x1_rdy = sem("x1_rdy")
    mean_ps = sem("mean_ps")
    xc_rdy = sem("xc_rdy")
    xsq_rdy = sem("xsq_rdy")
    var_ps = sem("var_ps")
    std_rdy = sem("std_rdy")
    rst_rdy = sem("rst_rdy")
    gm_rdy = sem("gm_rdy")
    am_rdy = sem("am_rdy")
    up_ps = sem("up_ps")
    g_rdy = sem("g_rdy")
    hh_rdy = sem("hh_rdy")
    dn_ps = sem("dn_ps")
    x2_rdy = sem("x2_rdy")
    gate_rdy = sem("gate_rdy")
    passed = sem("passed")
    bn_rdy = sem("bn_rdy")
    tables = sem("tables")
    eps_t = sb("eps", [P, 1])
    tiny = sb("tiny", [P, 1])
    eps_ap = eps_t[:, 0:1]

    loads = [(wqkv, io["wqkv"]), (wo, io["wo"]), (w1, io["w1"]), (w2, io["w2"]), (b1, io["b1"]), (vecs, io["vecs"]),
             (scales, io["scales"]), (trig, io["trig"]), (ident, io["ident"]), (mask, io["mask"]), (mean_w, io["mean_w"])]
    LOADED = 16 * len(loads)

    block = ctx.enter_context(nc.Block())

    def flat(t):
        return t[(slice(None),) * len(t.shape)]

    @block.sync
    def _(sp):
        for x in sems:
            sp.sem_inc(x, 1)
        sp.dma_start(flat(xin), io["x"][0, :, :, :]).then_inc(x_in, 16)
        for dst, src in loads[::-1]:
            sp.dma_start(flat(dst), src).then_inc(loaded, 16)
        def store(b):
            sp.wait_ge(xT_rdy, 1 + b * KC + KC)
            sp.sem_inc(passed, 1)
            sp.dma_start(scratch["xnT"][b, :, :, :], xT[:, :, 1:T + 1]).then_inc(xn_st, 16)

        def store_gate(b):
            sp.wait_ge(gate_rdy, 1 + b * KC + KC)
            sp.sem_inc(passed, 1)
            sp.dma_start(scratch["gate"][b, :, :, :], flat(gate)).then_inc(gate_st, 16)

        with sp.Fori(0, B - 1) as b:
            store(b)
            sp.wait_ge(xn_rdy, 1 + b * NT + NT)
            sp.sem_inc(passed, 1)
            sp.dma_start(flat(xin), io["x"][b + 1, :, :, :]).then_inc(x_in, 16)
            store_gate(b)
        store(B - 1)
        sp.wait_ge(xn_rdy, 1 + B * NT)
        sp.dma_start(flat(xin), io["x"][0, :, :, :]).then_inc(x_in, 16)
        store_gate(B - 1)
        sp.wait_ge(xn_st, 1 + B * 16)
        sp.dma_start(scratch["xnT"][B, :, :, :], scratch["xnT"][0, :, :, :]).then_inc(xn_st, 16)
        sp.wait_ge(xn_st, 1 + (B + 1) * 16)
        sp.wait_ge(gate_st, 1 + B * 16)

    @block.gpsimd
    def _(pool):
        nc.gpsimd.memset(xT[:, :, 0:1], 0.0).then_inc(w1_rdy, 1)
        pool.wait_ge(b1_ps, 1 + 1)
        for l in range(LAYERS):
            for c in range(KC):
                nc.gpsimd.tensor_tensor(w1[:, l, c, :], w1[:, l, c, :], vecs[:, l, 0, c:c + 1].to_broadcast([P, W1C]),
                                        ALU.mult).then_inc(w1_rdy, 1)
        with pool.Fori(0, B) as b:
            for l in range(LAYERS):
                it = b * LAYERS + l

                def normalise_k(w):
                    if w == 0:
                        pool.wait_ge(rn_step, 1 + it * 6 + 2)
                        pool.wait_ge(rot_rdy, 1 + it * 2 * NT + NT)
                    kw = qk[:, w, 1, :].rearrange("p (h d) -> p h d", h=FH)
                    nc.gpsimd.tensor_tensor(kw, kw, rn[:, 1, w, :].rearrange("p (h o) -> p h o", o=1)
                                            .to_broadcast([P, FH, DH]), ALU.mult).then_inc(k_rdy, 1)

                for n in range(2 * NT):
                    w, part = n % NT, 1 - n // NT
                    pool.wait_ge(rot_m, 1 + it * 2 * NT + n + 1)
                    if n == 0:
                        pool.wait_ge(qkT_ps, 1 + it * 2 * NT)
                    nc.gpsimd.tensor_tensor(qk[:, w, part, :], m1[:, n % 2, :], m2[:, n % 2, :],
                                            ALU.add).then_inc(rot_rdy, 1)
                    if n > NT:
                        normalise_k(n - NT - 1)
                normalise_k(NT - 1)

    def evac_oT(act, it, w):
        act.wait_ge(oT_ps, 1 + it * NT + w + 1)
        if w == 0:
            act.wait_ge(wo_ps, 1 + it * KC)
        nc.scalar.activation(oT[:, :, w * P:(w + 1) * P], ps[:, 7, :].rearrange("p (a t) -> p a t", a=PAIRS),
                             ACT.Copy).then_inc(oT_rdy, 1)

    @block.scalar
    def _(act):
        act.wait_ge(loaded, 1 + LOADED)
        act.wait_ge(rope_rdy, 1 + 1)

        def copy_xn(b):
            for c in range(KC):
                act.wait_ge(xnT_ps, 1 + b * KC + c + 1)
                if c == 0:
                    act.wait_ge(w1_rdy, 1 + 1)
                act.wait_ge(x2_rdy, 1 + b * LAYERS * KC - (KC - 1 - c) if not isinstance(b, int) else 1)
                nc.scalar.activation(xT[:, c, 1:T + 1], ps[:, 2 + c, :], ACT.Copy).then_inc(xT_rdy, 1)

        def table(it, k, func):
            act.wait_ge(tables, 1 + it * 4 + k)
            nc.scalar.activation(tiny[:, :], eps_ap, func).then_inc(tables, 1)

        def first_std(b):
            act.wait_ge(ln_step, 1 + b * 2 + 1)
            nc.scalar.activation(rstd[:, :], mv[:, :, 1], ACT.Sqrt).then_inc(ln_std, 1)

        first_std(0)
        copy_xn(0)
        with act.Fori(0, B) as b:
            for l in range(LAYERS):
                it = b * LAYERS + l
                def copy_v(w):
                    act.wait_ge(v_ps, 1 + it * NT + w + 1)
                    nc.scalar.activation(v[:, w, :], ps[:, 6 + w % 2, :], ACT.Copy).then_inc(v_rdy, 1)

                table(it, 0, ACT.Sqrt)
                for i in range(2 * NT):
                    act.wait_ge(qkv_ps, 1 + it * 2 * NT + i + 1)
                    act.wait_ge(ssq_rdy, 1 + it * 2 * NT + max(0, i - 1))
                    act.wait_ge(rot_m, 1 + it * 2 * NT + i + 1)
                    nc.scalar.activation(sq[:, i % 2, :], ps[:, i % 4, :], ACT.Square).then_inc(qkv_act, 1)
                    if i == NT:
                        act.wait_ge(ssq_rdy, 1 + it * 2 * NT + NT)
                        nc.scalar.activation(nrm[:, 1, :, :], ssq[:, 1, :, :], ACT.Sqrt).then_inc(nrm_rdy, 1)
                    if i == 6:
                        copy_v(0)

                for n, (part, w) in enumerate(TURN):
                    if n == 2:
                        act.wait_ge(ssq_rdy, 1 + it * 2 * NT + 2 * NT)
                        nc.scalar.activation(nrm[:, 0, :, :], ssq[:, 0, :, :], ACT.Sqrt).then_inc(nrm_rdy, 1)
                    if n == 1:
                        copy_v(1)
                    if n == 5:
                        copy_v(2)
                    act.wait_ge(qkT_ps, 1 + it * 2 * NT + n + 1)
                    dst = (qT, kT)[part]
                    nc.scalar.activation(dst[:, :, w * P:(w + 1) * P],
                                         ps[:, 4 + n % 2, :].rearrange("p (a t) -> p a t", a=PAIRS),
                                         ACT.Copy).then_inc(qkT_rdy, 1)
                table(it, 1, ACT.Exp)
                copy_v(3)
                for u in range(NT * PAIRS):
                    w = u // PAIRS
                    act.wait_ge(nb_rdy, 1 + it * NT * PAIRS + u + 1)
                    act.wait_ge(pT_ps, 1 + it * NT * PAIRS + max(0, u - 1))
                    k0 = P if w == 0 else 0
                    for j in range(2):
                        h = 2 * (u % PAIRS) + j
                        if u == 0 and j == 0:
                            act.wait_ge(o_rdy, 1 + it * NT)
                        nc.scalar.activation(pr[:, u % 2, j, k0:], sm[:, u % 2, j, k0:], ACT.Exp,
                                             bias=nb[:, u % 2, j:j + 1], scale=qsc[:, 0, w, h:h + 1],
                                             accum_out=rsum[:, w, h:h + 1]).then_inc(pr_rdy, 1)
                    if u % PAIRS == PAIRS - 1 and w > 0:
                        evac_oT(act, it, w - 1)
                evac_oT(act, it, NT - 1)
                table(it, 2, ACT.Sqrt)
                for c in range(KC):
                    act.wait_ge(xc_rdy, 1 + it * KC + c + 1)
                    nc.scalar.activation(xsq[:, c, :], xc[:, c, :], ACT.Square).then_inc(xsq_rdy, 1)
                if l == LAYERS - 1:
                    first_std(b + 1)
                act.wait_ge(var_ps, 1 + it + 1)
                nc.scalar.activation(std[:, :], ps[:, 3, :], ACT.Sqrt, bias=eps_ap).then_inc(std_rdy, 1)
                table(it, 3, ACT.Gelu)
                for m in range(HM):
                    r = HROWS[m]
                    act.wait_ge(gm_rdy, 1 + it * HM + m + 1)
                    act.wait_ge(hh_rdy, 1 + it * HM + max(0, m - 1))
                    nc.scalar.activation(gact[:r, m % 2, :], gm[:r, m % 2, :], ACT.Gelu,
                                         bias=b1[:r, l, 1, m:m + 1]).then_inc(g_rdy, 1)
            copy_xn(b + 1)
            for c in range(KC):
                if c == 0:
                    act.wait_ge(gate_st, 1 + b * 16)
                nc.scalar.activation(gate[:, c, :], xo[:, c, :], ACT.Silu).then_inc(gate_rdy, 1)

    @block.vector
    def _(dve):
        nc.vector.memset(eps_t[:, :], LN_EPS).then_inc(rope_rdy, 1)
        dve.wait_ge(loaded, 1 + LOADED)
        for l in range(LAYERS):
            for k in range(4):
                nc.vector.tensor_tensor(rope[:, l, :, k, :], trig[:, :, k, :],
                                        scales[:, l, k:k + 1, :].to_broadcast([P, NT, DH]),
                                        ALU.mult).then_inc(rope_rdy, 1)
        dve.wait_ge(rope_rdy, 1 + 4 * LAYERS + 1)
        dve.wait_ge(b1_ps, 1 + 1)
        bt = ps[:, 7, 0:2 * LAYERS * HM].rearrange("p (l k m) -> p l k m", l=LAYERS, k=2)
        for rows, ms in ((slice(0, P), slice(0, HM - 1)), (slice(0, HROWS[HM - 1]), slice(HM - 1, HM))):
            nc.vector.tensor_tensor(b1[rows, :, :, ms], b1[rows, :, :, ms], bt[rows, :, :, ms], ALU.add).then_inc(rope_rdy, 1)

        def first_norm(b):
            dve.wait_ge(x_in, 1 + b * 16 + 16)
            for w in range(NT):
                nc.vector.bn_stats(stats[:, w, :], xin[:, w, :]).then_inc(bn_rdy, 1)
            dve.wait_ge(bn_rdy, 1 + b * 2 * NT + NT)
            dve.sem_inc(passed, 1)
            for w in range(NT):
                nc.vector.bn_aggr(mv[:, w, :], stats[:, w, :]).then_inc(bn_rdy, 1)
            dve.wait_ge(bn_rdy, 1 + b * 2 * NT + 2 * NT)
            nc.vector.tensor_scalar(mv[:, :, 1], mv[:, :, 1], LN_EPS, None, ALU.add).then_inc(ln_step, 1)

        def first_norm_end(b):
            dve.wait_ge(ln_std, 1 + b + 1)
            nc.vector.reciprocal(rstd[:, :], rstd[:, :]).then_inc(ln_step, 1)
            dve.wait_ge(ln_step, 1 + b * 2 + 2)
            dve.wait_ge(xnT_ps, 1 + b * KC)
            for w in range(NT):
                nc.vector.tensor_scalar(xnorm[:, w, :], xin[:, w, :], mv[:, w, 0:1], rstd[:, w:w + 1],
                                        ALU.subtract, ALU.mult).then_inc(xn_rdy, 1)

        first_norm(0)
        first_norm_end(0)
        with dve.Fori(0, B) as b:
            for l in range(LAYERS):
                it = b * LAYERS + l
                def sum_squares(n):
                    w, part = n % NT, 1 - n // NT
                    dve.wait_ge(qkv_act, 1 + it * 2 * NT + n + 1)
                    nc.vector.tensor_reduce(ssq[:, part, w, :], sq[:, n % 2, :].rearrange("p (h d) -> p h d", h=FH),
                                            AX.X, ALU.add).then_inc(ssq_rdy, 1)

                def inverse_norm(part):
                    first = it * 6 + 2 * (1 - part)
                    dve.wait_ge(nrm_rdy, 1 + it * 2 + 2 - part)
                    nc.vector.tensor_scalar(nrm[:, part, :, :], nrm[:, part, :, :], 1e-12, None, ALU.max).then_inc(rn_step, 1)
                    dve.wait_ge(rn_step, 1 + first + 1)
                    if part == 1:
                        dve.wait_ge(k_rdy, 1 + it * NT)
                    nc.vector.reciprocal(rn[:, part, :, :], nrm[:, part, :, :]).then_inc(rn_step, 1)

                for n in range(2 * NT):
                    w, part = n % NT, 1 - n // NT
                    bank = n % 4
                    dve.wait_ge(qkv_ps, 1 + it * 2 * NT + n + 1)
                    dve.wait_ge(rot_rdy, 1 + it * 2 * NT + max(0, n - 1))
                    src = ps[:, bank, :].rearrange("p (h d) -> p h d", h=FH)
                    a = m1[:, n % 2, :].rearrange("p (h d) -> p h d", h=FH)
                    c = m2[:, n % 2, :].rearrange("p (h d) -> p h d", h=FH)
                    H2 = DH // 2
                    nc.vector.tensor_tensor(a, src, rope[:, l, w, 2 * part:2 * part + 1, :]
                                            .to_broadcast([P, FH, DH]), ALU.mult).then_inc(passed, 1)
                    nc.vector.tensor_tensor(c[:, :, 0:H2], src[:, :, H2:], rope[:, l, w, 2 * part + 1:2 * part + 2, 0:H2]
                                            .to_broadcast([P, FH, H2]), ALU.mult).then_inc(passed, 1)
                    nc.vector.tensor_tensor(c[:, :, H2:], src[:, :, 0:H2], rope[:, l, w, 2 * part + 1:2 * part + 2, H2:]
                                            .to_broadcast([P, FH, H2]), ALU.mult).then_inc(rot_m, 1)
                    if n > 0:
                        sum_squares(n - 1)
                    if n == NT + 1:
                        inverse_norm(1)
                sum_squares(2 * NT - 1)
                inverse_norm(0)
                dve.wait_ge(rn_step, 1 + it * 6 + 4)
                dve.wait_ge(pr_rdy, 1 + it * FH * NT)
                nc.vector.tensor_scalar(qsc[:, 0, :, :], rn[:, 0, :, :], 8.0, None, ALU.mult).then_inc(rn_step, 1)
                nc.vector.tensor_scalar(qsc[:, 1, :, :], rn[:, 0, :, :], -8.0, None, ALU.mult).then_inc(rn_step, 1)
                dve.wait_ge(rn_step, 1 + it * 6 + 6)

                def masked_max(u):
                    w = u // PAIRS
                    k0 = P if w == 0 else 0
                    dve.wait_ge(sc_ps, 1 + it * NT * PAIRS + u + 1)
                    dve.wait_ge(pr_rdy, 1 + it * NT * FH + max(0, 2 * (u - 1)))
                    dve.sem_inc(passed, 1)
                    for j in range(2):
                        nc.vector.tensor_tensor_reduce(
                            out=sm[:, u % 2, j, k0:], in0=ps[:, 2 * (u % 2) + j, k0:2 * P],
                            in1=mask[:, k0:], scale=1.0, scalar=-3e38, op0=ALU.add, op1=ALU.max,
                            accum_out=mx[:, u % 2, j:j + 1]).then_inc(sm_rdy, 1)
                    dve.wait_ge(sm_rdy, 1 + it * NT * FH + 2 * u + 2)
                    h = 2 * (u % PAIRS)
                    nc.vector.tensor_tensor(nb[:, u % 2, :], mx[:, u % 2, :], qsc[:, 1, w, h:h + 2],
                                            ALU.mult).then_inc(nb_rdy, 1)

                def evac_pT(u):
                    w = u // PAIRS
                    dve.wait_ge(pT_ps, 1 + it * NT * PAIRS + u + 1)
                    dve.wait_ge(o_ps, 1 + it * NT * PAIRS + max(0, u - 1))
                    k0 = 1 if w == 0 else 0
                    nc.vector.tensor_copy(pT[:, u % 2, :, :].rearrange("p (j k) t -> p j k t", j=2)[:, :, k0:, :],
                                          ps[:, 4 + u % 2, :].rearrange("p (j k t) -> p j k t", j=2, k=2)[:, :, k0:, :]
                                          ).then_inc(pT_rdy, 1)

                def window_out(w):
                    dve.wait_ge(pr_rdy, 1 + it * NT * FH + FH * (w + 1))
                    nc.vector.reciprocal(rinv[:, w, :], rsum[:, w, :]).then_inc(ri_rdy, 1)
                    dve.wait_ge(ri_rdy, 1 + it * NT + w + 1)
                    dve.wait_ge(o_ps, 1 + it * NT * PAIRS + PAIRS * (w + 1))
                    dve.wait_ge(oT_ps, 1 + it * NT + max(0, w - 1))
                    nc.vector.tensor_tensor(osb[:, w % 2, :].rearrange("p (h d) -> p h d", h=FH),
                                            ps[:, 6, :].rearrange("p (h d) -> p h d", h=FH),
                                            rinv[:, w, :].rearrange("p (h o) -> p h o", o=1)
                                            .to_broadcast([P, FH, DH]), ALU.mult).then_inc(o_rdy, 1)

                U = NT * PAIRS
                masked_max(0)
                masked_max(1)
                for u in range(U):
                    evac_pT(u)
                    if u + 2 < U:
                        masked_max(u + 2)
                    if u % PAIRS == PAIRS - 1:
                        window_out(u // PAIRS)
                if l == 0:
                    dve.wait_ge(xT_rdy, 1 + b * KC + KC)
                    dve.wait_ge(xn_st, 1 + b * 16 + 16)
                for c in range(KC):
                    dve.wait_ge(wo_ps, 1 + it * KC + c + 1)
                    nc.vector.tensor_tensor(xT[:, c, 1:T + 1], xT[:, c, 1:T + 1], ps[:, c, :],
                                            ALU.add).then_inc(x1_rdy, 1)
                dve.wait_ge(x1_rdy, 1 + it * KC + KC)
                dve.wait_ge(mean_ps, 1 + it + 1)
                for c in range(KC):
                    nc.vector.tensor_tensor(xc[:, c, :], xT[:, c, 1 - c:T + 1 - c], ps[:, 2, :],
                                            ALU.subtract).then_inc(xc_rdy, 1)
                if l == LAYERS - 1:
                    first_norm(b + 1)
                dve.wait_ge(std_rdy, 1 + it + 1)
                nc.vector.reciprocal(rst[:, :], std[:, :]).then_inc(rst_rdy, 1)
                dve.wait_ge(rst_rdy, 1 + it + 1)

                def gated(m):
                    r = HROWS[m]
                    dve.wait_ge(g_rdy, 1 + it * HM + m + 1)
                    dve.wait_ge(am_rdy, 1 + it * HM + m + 1)
                    nc.vector.scalar_tensor_tensor(out=hh[:r, m, :], in0=hh[:r, m, :],
                                                   scalar=b1[:r, l, 0, m:m + 1], in1=gact[:r, m % 2, :],
                                                   op0=ALU.add, op1=ALU.mult).then_inc(hh_rdy, 1)

                for m in range(HM):
                    r = HROWS[m]
                    dve.wait_ge(up_ps, 1 + it * HM + m + 1)
                    dve.wait_ge(g_rdy, 1 + it * HM + max(0, m - 1))
                    nc.vector.tensor_tensor(gm[:r, m % 2, :], ps[:r, UP_BANK[m % 3] + 1, :], rst[:r, :],
                                            ALU.mult).then_inc(gm_rdy, 1)
                    nc.vector.tensor_tensor(hh[:r, m, :], ps[:r, UP_BANK[m % 3], :], rst[:r, :], ALU.mult).then_inc(am_rdy, 1)
                    if m > 0:
                        gated(m - 1)
                    if m == 2 and l == LAYERS - 1:
                        first_norm_end(b + 1)
                gated(HM - 1)
                dst = xT[:, :, 1:T + 1] if l < LAYERS - 1 else xo
                for c in range(KC):
                    dve.wait_ge(dn_ps, 1 + it * KC + c + 1)
                    if l == LAYERS - 1 and c == 0:
                        dve.wait_ge(gate_rdy, 1 + b * KC)
                    nc.vector.scalar_tensor_tensor(out=dst[:, c, :], in0=ps[:, 4 + c, :],
                                                   scalar=vecs[:, l, 2, c:c + 1], in1=xT[:, c, 1:T + 1],
                                                   op0=ALU.add, op1=ALU.add).then_inc(x2_rdy, 1)
                dve.wait_ge(x2_rdy, 1 + it * KC + KC)

    @block.tensor
    def _(pe):
        pe.wait_ge(loaded, 1 + LOADED)
        mm = nc.tensor.matmul

        def shifted(c, t0, t1):
            return xT[:, c, 1 - c + t0:1 - c + t1]

        for l in range(LAYERS):
            for k in range(2):
                for m in range(HM):
                    r, col = HROWS[m], (l * 2 + k) * HM + m
                    for c in range(KC):
                        last = mm(ps[:r, 7, col:col + 1], w1[:, l, c, k * HID + m * P:k * HID + m * P + r],
                                  vecs[:, l, 1, c:c + 1], start=c == 0, stop=c == KC - 1)
        last.then_inc(b1_ps, 1)

        def transpose_xn(b):
            pe.wait_ge(xn_rdy, 1 + b * NT + NT)
            for c in range(KC):
                for w in range(NT):
                    last = nc.tensor.transpose(ps[:, 2 + c, w * P:(w + 1) * P], xnorm[:, w, c * P:(c + 1) * P], ident[:, :])
                last.then_inc(xnT_ps, 1)

        transpose_xn(0)
        with pe.Fori(0, B) as b:
            for l in range(LAYERS):
                it = b * LAYERS + l
                if l == 0:
                    pe.wait_ge(xT_rdy, 1 + b * KC + KC)
                pe.wait_ge(x2_rdy, 1 + it * KC)
                def project_v(w):
                    if w == 0:
                        pe.wait_ge(rope_rdy, 1 + 4 * LAYERS + 1 + 2)
                    if w >= 2:
                        pe.wait_ge(v_rdy, 1 + it * NT + w - 1)
                    for c in range(KC):
                        last = mm(ps[:, 6 + w % 2, :], shifted(c, w * P, (w + 1) * P),
                                  wqkv[:, l, c, 2 * INNER:3 * INNER], start=c == 0, stop=c == KC - 1)
                    last.then_inc(v_ps, 1)

                for n in range(2 * NT):
                    w, part = n % NT, 1 - n // NT
                    if n >= 4:
                        pe.wait_ge(qkv_act, 1 + it * 2 * NT + n - 3)
                        pe.wait_ge(rot_m, 1 + it * 2 * NT + n - 3)
                    for c in range(KC):
                        last = mm(ps[:, n % 4, :], shifted(c, w * P, (w + 1) * P),
                                  wqkv[:, l, c, part * INNER:(part + 1) * INNER], start=c == 0, stop=c == KC - 1)
                    last.then_inc(qkv_ps, 1)
                    if n == 5:
                        project_v(0)
                project_v(1)
                for n, (part, w) in enumerate(TURN):
                    if n == 4:
                        project_v(2)
                    if part == 0:
                        pe.wait_ge(rot_rdy, 1 + it * 2 * NT + NT + w + 1)
                    else:
                        pe.wait_ge(k_rdy, 1 + it * NT + w + 1)
                    pe.wait_ge(qkT_rdy, 1 + it * 2 * NT + max(0, n - 1))
                    for a in range(PAIRS):
                        last = nc.tensor.transpose(ps[:, 4 + n % 2, a * P:(a + 1) * P],
                                                   qk[:, w, part, a * P:(a + 1) * P], ident[:, :])
                    last.then_inc(qkT_ps, 1)

                def scores(u):
                    w, a = u // PAIRS, u % PAIRS
                    if u < 2:
                        pe.wait_ge(qkv_act, 1 + it * 2 * NT + 2 * NT)
                        pe.wait_ge(rot_m, 1 + it * 2 * NT + 2 * NT)
                        pe.wait_ge(qkT_rdy, 1 + it * 2 * NT + 2 * NT)
                    else:
                        pe.wait_ge(sm_rdy, 1 + it * NT * FH + 2 * (u - 1))
                    k0 = P if w == 0 else 0
                    for j in range(2):
                        rows = slice(j * DH, (j + 1) * DH)
                        last = mm(ps[:, 2 * (u % 2) + j, k0:2 * P], qT[rows, a, w * P:(w + 1) * P],
                                  kT[rows, a, (w - 1) * P + k0:(w + 1) * P], start=True, stop=True)
                    last.then_inc(sc_ps, 1)

                def transpose_p(u):
                    w = u // PAIRS
                    pe.wait_ge(pr_rdy, 1 + it * NT * FH + 2 * u + 2)
                    pe.wait_ge(pT_rdy, 1 + it * NT * PAIRS + max(0, u - 1))
                    for j in range(2):
                        for k in range(1 if w == 0 else 0, 2):
                            last = nc.tensor.transpose(ps[:, 4 + u % 2, (2 * j + k) * P:(2 * j + k + 1) * P],
                                                       pr[:, u % 2, j, k * P:(k + 1) * P], ident[:, :])
                    last.then_inc(pT_ps, 1)

                def weigh_v(u):
                    w, a = u // PAIRS, u % PAIRS
                    pe.wait_ge(pT_rdy, 1 + it * NT * PAIRS + u + 1)
                    if u == 0:
                        pe.wait_ge(v_rdy, 1 + it * NT + NT)
                    if a == 0:
                        pe.wait_ge(o_rdy, 1 + it * NT + w)
                    k0 = 1 if w == 0 else 0
                    for j in range(2):
                        h = 2 * a + j
                        for k in range(k0, 2):
                            last = mm(ps[:, 6, h * DH:(h + 1) * DH], pT[:, u % 2, 2 * j + k, :],
                                      v[:, w - 1 + k, h * DH:(h + 1) * DH], start=k == k0, stop=k == 1)
                    last.then_inc(o_ps, 1)

                def transpose_o(w):
                    pe.wait_ge(o_rdy, 1 + it * NT + w + 1)
                    if w == 0:
                        pe.wait_ge(x2_rdy, 1 + it * KC)
                    pe.wait_ge(oT_rdy, 1 + it * NT + w)
                    for a in range(PAIRS):
                        last = nc.tensor.transpose(ps[:, 7, a * P:(a + 1) * P], osb[:, w % 2, a * P:(a + 1) * P], ident[:, :])
                    last.then_inc(oT_ps, 1)

                U = NT * PAIRS
                scores(0)
                scores(1)
                project_v(3)
                for _ in range(WARM):
                    mm(ps[:, 4, :], ident[:, :], wqkv[:, l, 0, 0:512], start=True, stop=True)
                for u in range(U):
                    if u == 0:
                        transpose_p(0)
                    if u + 2 < U:
                        scores(u + 2)
                    if u + 1 < U:
                        transpose_p(u + 1)
                    weigh_v(u)
                    if u % PAIRS == 0 and u > 0:
                        transpose_o(u // PAIRS - 1)
                transpose_o(NT - 1)
                pe.wait_ge(oT_rdy, 1 + it * NT + NT)
                pe.wait_ge(sm_rdy, 1 + it * NT * FH + NT * FH)
                for c in range(KC):
                    for a in range(PAIRS):
                        last = mm(ps[:, c, :], wo[:, l, a, c * P:(c + 1) * P], oT[:, a, :], start=a == 0, stop=a == PAIRS - 1)
                    last.then_inc(wo_ps, 1)
                for c in range(KC):
                    pe.wait_ge(x1_rdy, 1 + it * KC + c + 1)
                    last = mm(ps[:, 2, :], mean_w[:, :], shifted(c, 0, T), start=c == 0, stop=c == KC - 1)
                last.then_inc(mean_ps, 1)

                def variance():
                    for c in range(KC):
                        pe.wait_ge(xsq_rdy, 1 + it * KC + c + 1)
                        last = mm(ps[:, 3, :], mean_w[:, :], xsq[:, c, :], start=c == 0, stop=c == KC - 1)
                    last.then_inc(var_ps, 1)

                pe.wait_ge(xc_rdy, 1 + it * KC + KC)
                pe.wait_ge(w1_rdy, 1 + 1 + LAYERS * KC)
                for m in range(HM):
                    r = HROWS[m]
                    if m >= 3:
                        pe.wait_ge(am_rdy, 1 + it * HM + m - 2)
                    for part in range(2):
                        for c in range(KC):
                            last = mm(ps[:r, UP_BANK[m % 3] + part, :],
                                      w1[:, l, c, part * HID + m * P:part * HID + m * P + r], xc[:, c, :],
                                      start=c == 0, stop=c == KC - 1)
                    last.then_inc(up_ps, 1)
                    if m == 0:
                        variance()
                if l == LAYERS - 1:
                    pe.wait_ge(std_rdy, 1 + it + 1)
                    transpose_xn(b + 1)
                pe.wait_ge(am_rdy, 1 + it * HM + 4)
                for c in range(KC):
                    for m in range(HM):
                        r = HROWS[m]
                        if c == 0:
                            pe.wait_ge(hh_rdy, 1 + it * HM + m + 1)
                        last = mm(ps[:, 4 + c, :], w2[:r, l, m, c * P:(c + 1) * P], hh[:r, m, :], start=m == 0, stop=m == HM - 1)
                    last.then_inc(dn_ps, 1)


def ffn_constants():
    i = np.arange(0, DH, 2, dtype=np.float32)
    inv = (1.0 / 10000.0 ** (i / DH)).astype(np.float32)
    t = np.arange(T, dtype=np.float32)
    fr = t[:, None] * inv[None, :]
    fr = np.concatenate([fr, fr], -1)
    base = (i + 0.4 * DH) / (1.4 * DH)
    power = (t - T // 2) / 64.0
    s = base[None, :] ** power[:, None]
    s = np.concatenate([s, s], -1)
    sign = np.where(np.arange(DH) < DH // 2, -1.0, 1.0)
    trig = np.stack([np.cos(fr) * s, np.sin(fr) * s * sign, np.cos(fr) / s, np.sin(fr) / s * sign], 1)
    trig = trig.astype(np.float32).reshape(NT, P, 4, DH).transpose(1, 0, 2, 3)
    ii, jj = np.arange(P)[:, None], np.arange(P)[None, :]
    mask = np.concatenate([np.where(jj < ii, NEG, 0.0), np.where(jj > ii, NEG, 0.0)], 1).astype(np.float32)
    return dict(trig=np.ascontiguousarray(trig), mask=mask, ident=np.eye(P, dtype=np.float32),
                mean_w=np.full((P, P), 1.0 / D, np.float32))


def ffn_layout(i):
    c = ffn_constants()
    g = lambda n: np.asarray(i["L0_ffn_" + n])
    chunks = lambda a: np.ascontiguousarray(a.reshape(LAYERS, -1, P, a.shape[-1]).transpose(2, 0, 1, 3))
    w2 = np.zeros((LAYERS, HM * P, D), np.float32)
    w2[:, :HID] = g("w2")
    b1 = np.zeros((LAYERS, 2, HM * P), np.float32)
    b1[:, :, :HID] = g("b1").reshape(LAYERS, 2, HID)
    vec = np.stack([g("ln_g"), g("ln_b"), g("b2")], 1)
    swap = lambda a: np.concatenate([a[:, DH // 2:], a[:, :DH // 2]], 1)
    sc = np.stack([g("q_scale"), swap(g("q_scale")), g("k_scale"), swap(g("k_scale"))], 1)
    c |= dict(x=np.asarray(i["L0_attn_x"]), wqkv=chunks(g("wqkv")), wo=chunks(g("wo")), w1=chunks(g("w1")),
              w2=chunks(w2), b1=np.ascontiguousarray(b1.reshape(LAYERS, 2, HM, P).transpose(3, 0, 1, 2)),
              vecs=np.ascontiguousarray(vec.reshape(LAYERS, 3, KC, P).transpose(3, 0, 1, 2)),
              scales=np.ascontiguousarray(np.broadcast_to(sc[None], (P, LAYERS, 4, DH))))
    return c


H, TAPS = 16, 4
GH = 4
GW = GH * DH
NG = H // GH
GP = GH // 2
CT = GW // P
NQ = NT * GH
CV_BANK = (4, 5, 6, 7, 0, 1)
V_BANK = (0, 5, 5, 5)
IN_BANK = (5, 4, 3, 3)
BL = 16
NBL = P // BL
RMS_EPS = 1e-6
LOG_FLOOR = -200.0


def delta_phase(nc, ctx, io, scratch, out):

    def sb(name, shape):
        return ctx.enter_context(nc.sbuf_tensor("d_" + name, shape, F32))

    sems = []

    def sem(name):
        sems.append(ctx.enter_context(nc.semaphore("d_" + name)))
        return sems[-1]

    wqkv = sb("wqkv", [P, 3, KC, H * DH])
    wg = sb("wg", [P, KC, H * DH])
    wo = sb("wo", [P, H * DH // P, D])
    wgate = sb("wgate", [P, KC, 2 * H])
    cw = sb("cw", [P, 3, H * DH // P, TAPS + 1])
    rows = sb("rows", [P, 5, H])
    onw = sb("onw", [P, DH])
    rope = sb("rope", [P, NT, 2, 2, DH // 2])
    tri = sb("tri", [P, 4, P])
    mshift = sb("mshift", [P, P])
    m16 = sb("m16", [P, 2 * BL])
    ident = sb("ident", [P, P])
    INCL, EXCL, AFTER, ALL = range(4)

    xnT = sb("xnT", [P, KC, T])
    zg = sb("zg", [P, NT, 2 * H])
    eb = sb("eb", [P, NT, H])
    ab = sb("ab", [P, NT, H])
    sp1 = sb("sp1", [P, NT, H])
    expA = sb("expA", [P, H])
    la = sb("la", [P, NT, H])
    coef = sb("coef", [P, 6, NT, H])
    BETA, G_INCL, G_EXCL, G_AFTER, G_ALL, B_AFTER = range(6)
    acc = sb("acc", [P, 2, T])
    xc = sb("xc", [P, 3, CT, T])
    gsb = sb("gsb", [P, 2, NT, GW])
    m1 = sb("m1", [P, 2 * GW])
    m2 = sb("m2", [P, 2 * GW])
    qk = sb("qk", [P, 2, 2, GW])
    ss = sb("ss", [P, 2 * GH])
    rn = sb("rn", [P, 2 * GH])
    qkd = sb("qkd", [P, GH])
    sq = m1
    kbg = sb("kbg", [P, 2, GW])
    qg = sb("qg", [P, GW])
    kqT = sb("kqT", [P, GP, 2, P])
    kbT = sb("kbT", [P, GP, P])
    lm = sb("lm", [P, GH, P])
    ex = sb("ex", [P, GH, P])
    em = sb("em", [P, GH, P])
    LT = sb("LT", [P, NT, GH, P])
    AT = sb("AT", [P, 2, NT, GH, P])
    kgT = sb("kgT", [P, 2, NT, GP, P])
    qgT = sb("qgT", [P, 2, NT, GP, P])
    kl = sb("kl", [P, 2, NT, GW])
    v = sb("v", [P, 2, NT, GW])
    dq = sb("dq", [P, 2, NT, GH])
    gt = sb("gt", [P, 2, NT, GP])
    LB = sb("LB", [P, BL, BL])
    TB = sb("TB", [P, BL, BL])
    pb = sb("pb", [P, BL * BL])
    qkp = pb[:, 0:GW]
    T16 = sb("T16", [P, NQ, 2 * BL])
    R16 = sb("R16", [P, NQ, 2 * BL])
    Y16 = sb("Y16", [P, NQ, 2 * BL])
    T32 = kbg[:, :, :].rearrange("p k (q t) -> p (k q) t", t=32)
    R32, Y32 = R16, Y16
    T64 = sb("T64", [P, NQ, 64])
    Y64 = T64
    Rf = sb("Rf", [P, NQ, P])
    St = sb("St", [P, 2, GP, DH])
    Sg = sb("Sg", [P, GP, DH])
    rh = sb("rh", [P, GP, 2, DH])
    us = sb("us", [P, GH, DH])
    vq = sb("vq", [P, GP, 2, DH])
    ms = sb("ms", [P, NQ])
    ro = sb("ro", [P, NQ])
    on = sb("on", [P, NT, GW])
    oT = sb("oT", [P, H * DH // P, T])
    gate = sb("gate", [P, KC, T])
    z = on[:, :, :].rearrange("p (m a) n -> p m (a n)", m=KC)
    xio = sb("xio", [P, NT, D])
    mhalf = sb("mhalf", [P, NQ])
    ps = ctx.enter_context(nc.psum_tensor("d_ps", [P, 8, 512], F32))

    passed = sem("passed")
    loaded = sem("loaded")
    xn_in = sem("xn_in")
    gate_in = sem("gate_in")
    x_in = sem("x_in")
    ld_wr = sem("ld_wr")
    lb_rd = sem("lb_rd")
    tb_wr = sem("tb_wr")
    t16_rd = sem("t16_rd")
    out_st = sem("out_st")
    init0 = sem("init0")
    init1 = sem("init1")
    zg_ps = sem("zg_ps")
    zg_rdy = sem("zg_rdy")
    eb_rdy = sem("eb_rdy")
    ab_rdy = sem("ab_rdy")
    abe_rdy = sem("abe_rdy")
    sp_rdy = sem("sp_rdy")
    gstep = sem("gstep")
    la_rdy = sem("la_rdy")
    sum_ps = sem("sum_ps")
    sum_rdy = sem("sum_rdy")
    coef_rdy = sem("coef_rdy")
    cv_ps = sem("cv_ps")
    cv_t0 = sem("cv_t0")
    cv_mid = sem("cv_mid")
    cv_acc = sem("cv_acc")
    cv_rdy = sem("cv_rdy")
    g_ps = sem("g_ps")
    g_rdy = sem("g_rdy")
    in_ps = sem("in_ps")
    vin_ps = sem("vin_ps")
    td_zero = sem("td_zero")
    v_rdy = sem("v_rdy")
    rot_rdy = sem("rot_rdy")
    qk_rdy = sem("qk_rdy")
    sq_rdy = sem("sq_rdy")
    ss_mid = sem("ss_mid")
    ss_rdy = sem("ss_rdy")
    rn_rdy = sem("rn_rdy")
    qkn_rdy = sem("qkn_rdy")
    qkd_mid = sem("qkd_mid")
    dq_rdy = sem("dq_rdy")
    kbg_rdy = sem("kbg_rdy")
    kl_rdy = sem("kl_rdy")
    qg_rdy = sem("qg_rdy")
    gt_rdy = sem("gt_rdy")
    lm_rdy = sem("lm_rdy")
    e_ps = sem("e_ps")
    ex_rdy = sem("ex_rdy")
    em_rdy = sem("em_rdy")
    kq_ps = sem("kq_ps")
    kqT_rdy = sem("kqT_rdy")
    kb_ps = sem("kb_ps")
    kbT_rdy = sem("kbT_rdy")
    kgT_rdy = sem("kgT_rdy")
    qg_ps = sem("qg_ps")
    qgT_rdy = sem("qgT_rdy")
    kk_ps = sem("kk_ps")
    lt_rdy = sem("lt_rdy")
    at_rdy = sem("at_rdy")
    tb_step = sem("tb_step")
    tbs = sem("tbs")
    b16_rdy = sem("b16_rdy")
    b16_ps = sem("b16_ps")
    b32_rdy = sem("b32_rdy")
    y32_ps = sem("y32_ps")
    y32_rdy = sem("y32_rdy")
    r32_ps = sem("r32_ps")
    t32_ps = sem("t32_ps")
    rf_a = sem("rf_a")
    rf_b = sem("rf_b")
    t64_rdy = sem("t64_rdy")
    y64_ps = sem("y64_ps")
    y64_rdy = sem("y64_rdy")
    r64_ps = sem("r64_ps")
    rf_c = sem("rf_c")
    x_ps = sem("x_ps")
    rh_rdy = sem("rh_rdy")
    u_ps = sem("u_ps")
    us_rdy = sem("us_rdy")
    o_ps = sem("o_ps")
    s_ps = sem("s_ps")
    sg_rdy = sem("sg_rdy")
    st_rdy = sem("st_rdy")
    vq_rdy = sem("vq_rdy")
    os_rdy = sem("os_rdy")
    osq_rdy = sem("osq_rdy")
    ms_mid = sem("ms_mid")
    ms_rdy = sem("ms_rdy")
    ro_rdy = sem("ro_rdy")
    on_mid = sem("on_mid")
    on_rdy = sem("on_rdy")
    sl_rdy = sem("sl_rdy")
    og_rdy = sem("og_rdy")
    oT_ps = sem("oT_ps")
    oT_rdy = sem("oT_rdy")
    wo_ps = sem("wo_ps")
    z_rdy = sem("z_rdy")
    zT_ps = sem("zT_ps")
    xo_rdy = sem("xo_rdy")

    loads = [(t, io[n]) for t, n in ((wqkv, "dwqkv"), (wg, "dwg"), (wo, "dwo"), (wgate, "dwgate"), (cw, "dcw"),
             (rows, "drows"), (onw, "donw"), (rope, "drope"), (tri, "dtri"), (mshift, "dmshift"), (m16, "dm16"),
             (ident, "ident"), (TB, "deye"))]
    LOADED = 16 * len(loads)
    one_t = sb("one", [P, 1])
    one_ap = one_t[:, 0:1]
    block = ctx.enter_context(nc.Block())

    def flat(t):
        return t[(slice(None),) * len(t.shape)]

    def heads(ap, n=GH):
        return ap.rearrange("p (h o) -> p h o", o=1).to_broadcast([P, n, DH])

    def hd(ap, n=GH):
        return ap.rearrange("p (h d) -> p h d", h=n)

    def osq(s):
        return oT[:, s * CT:(s + 1) * CT, :].rearrange("p a t -> p (a t)")

    def val(i, n, k):
        return i * n + k

    @block.sync
    def _(sp):
        for x in sems:
            sp.sem_inc(x, 1)

        def inverse_io(i):
            sp.wait_ge(lt_rdy, 1 + val(i, 2 * NT, 2 * NT))
            sp.sem_inc(passed, 1)
            sp.wait_ge(lb_rd, 1 + i * 32)
            sp.sem_inc(passed, 1)
            for r in range(4):
                q = slice(32 * r, 32 * r + 32)
                sp.dma_start(scratch["Ld"][r, :, :, :].rearrange("q j t -> j q t"), LT[q, :, :, q].rearrange("j c h t -> j (c h) t")).then_inc(ld_wr, 16)
            sp.wait_ge(ld_wr, 1 + val(i, 16 * 4, 16 * 4))
            sp.sem_inc(passed, 1)
            sp.wait_ge(tb_step, 1 + i)
            sp.sem_inc(passed, 1)
            for k in range(2):
                sp.dma_start(LB[64 * k:64 * k + 64, :, :],
                             scratch["Ld"][:, :, BL * k:BL * k + BL, BL * k:BL * k + BL].rearrange("r q j t -> (r q) j t")).then_inc(lb_rd, 16)

        def inverse_back(i):
            sp.wait_ge(tb_step, 1 + i + 1)
            sp.sem_inc(passed, 1)
            sp.wait_ge(t16_rd, 1 + i * 64)
            sp.sem_inc(passed, 1)
            for k in range(2):
                sp.dma_start(scratch["Td"][:, :, BL * k:BL * k + BL, BL * k:BL * k + BL].rearrange("r q t c -> (r q) t c"),
                             TB[64 * k:64 * k + 64, :, :]).then_inc(tb_wr, 16)
            sp.wait_ge(tb_wr, 1 + i * 32 + 32)
            sp.sem_inc(passed, 1)
            sp.wait_ge(b32_rdy, 1 + 2 * i)
            sp.sem_inc(passed, 1)
            sp.wait_ge(b16_rdy, 1 + 2 * i)
            sp.sem_inc(passed, 1)
            sp.wait_ge(b16_ps, 1 + 2 * i)
            sp.sem_inc(passed, 1)
            for r in range(4):
                sp.dma_start(T16[32 * r:32 * r + 32, :, :], scratch["Td"][r, :, :, :].rearrange("q t c -> t q c")).then_inc(t16_rd, 16)

        for dst, src in loads[::-1]:
            sp.dma_start(flat(dst), src).then_inc(loaded, 16)
        sp.dma_start(flat(xnT), scratch["xnT"][0, :, :, :]).then_inc(xn_in, 16)
        sp.wait_ge(init1, 1 + 2)
        for r in range(4):
            sp.dma_start(scratch["Td"][r, :, :, :].rearrange("q t c -> t q c"), T16[32 * r:32 * r + 32, :, :]).then_inc(td_zero, 16)
        sp.wait_ge(td_zero, 1 + 4 * 16)
        inverse_io(0)
        inverse_back(0)
        with sp.Fori(0, B) as b:
            for s in range(NG):
                i = b * NG + s
                if s == 0:
                    sp.wait_ge(z_rdy, 1 + b * KC)
                    sp.sem_inc(passed, 1)
                    sp.dma_start(flat(gate), scratch["gate"][b, :, :, :]).then_inc(gate_in, 16)
                    sp.wait_ge(out_st, 1 + b * 16)
                    sp.sem_inc(passed, 1)
                    sp.dma_start(flat(xio), io["x"][b, :, :, :]).then_inc(x_in, 16)
                inverse_io(i + 1)
                inverse_back(i + 1)
                if s == 1:
                    sp.wait_ge(cv_ps, 1 + val(i + 2, 6, 6))
                    sp.sem_inc(passed, 1)
                    sp.wait_ge(g_ps, 1 + val(i + 2, NT, NT))
                    sp.sem_inc(passed, 1)
                    sp.dma_start(flat(xnT), scratch["xnT"][b + 1, :, :, :]).then_inc(xn_in, 16)
            sp.wait_ge(xo_rdy, 1 + b * 2 + 2)
            sp.sem_inc(passed, 1)
            sp.dma_start(out[b, :, :, :], flat(xio)).then_inc(out_st, 16)
        sp.wait_ge(out_st, 1 + B * 16)
        sp.sem_inc(passed, 1)

    @block.gpsimd
    def _(pool):
        tt = nc.gpsimd.tensor_tensor

        nc.gpsimd.memset(em[:, :, 0:1], 0.0).then_inc(init1, 1)
        nc.gpsimd.memset(flat(T16), 0.0).then_inc(init1, 1)
        nc.gpsimd.memset(flat(T64), 0.0).then_inc(init1, 1)
        nc.gpsimd.memset(flat(Rf), 0.0).then_inc(init1, 1)
        nc.gpsimd.memset(flat(mhalf), -0.5).then_inc(init1, 1)
        pool.wait_ge(init1, 1 + 5)
        pool.wait_ge(loaded, 1 + LOADED)

        def decay_rhs(i, s, bt, c):
            n = lambda k=1, m=1: i * NT * m + c * m + k
            hs = slice(s * GH, (s + 1) * GH)
            pool.wait_ge(e_ps, 1 + n(0))
            pool.wait_ge(coef_rdy, 1 + bt + 1)
            tt(lm[:, :, :], tri[:, INCL:INCL + 1, :].to_broadcast([P, GH, P]),
               la[:, c, hs].rearrange("p (h o) -> p h o", o=1).to_broadcast([P, GH, P]), ALU.mult).then_inc(lm_rdy, 1)

        def rotate(i, s, bt, c):
            n = lambda k=1, m=1: i * NT * m + c * m + k
            pool.wait_ge(rot_rdy, 1 + 2 * n())
            if not (isinstance(i, int) and i == 0 and c < 2):
                pool.wait_ge(kq_ps, 1 + n(-1))
                pool.wait_ge(qkd_mid, 1 + 2 * n(-1))
                pool.wait_ge(kl_rdy, 1 + n(-1))
            tt(qk[:, c % 2, :, :].rearrange("p a n -> p (a n)"), m1[:, :], m2[:, :], ALU.add).then_inc(qk_rdy, 1)

        def normalise(i, s, bt, c):
            n = lambda k=1, m=1: i * NT * m + c * m + k
            pool.wait_ge(ss_rdy, 1 + n())
            tt(rn[:, :], ss[:, :], mhalf[:, 0:2 * GH], ALU.pow).then_inc(rn_rdy, 1)
            pool.wait_ge(rn_rdy, 1 + n())
            q8 = qk[:, c % 2, :, :].rearrange("p a (h d) -> p (a h) d", d=DH)
            tt(q8, q8, heads(rn[:, :], 2 * GH), ALU.mult).then_inc(qkn_rdy, 1)

        def prepare_q(i, s, bt, c):
            n = lambda k=1, m=1: i * NT * m + c * m + k
            hs = slice(s * GH, (s + 1) * GH)
            pool.wait_ge(qkn_rdy, 1 + n())
            pool.wait_ge(qg_ps, 1 + n(0))
            tt(hd(qg[:, :]), hd(qk[:, c % 2, 0, :]), heads(coef[:, G_EXCL, c, hs]), ALU.mult).then_inc(qg_rdy, 1)

        def prepare_k(i, s, bt, c):
            par = s % 2
            hs = slice(s * GH, (s + 1) * GH)
            tt(hd(kl[:, par, c, :]), hd(qk[:, c % 2, 1, :]), heads(coef[:, B_AFTER, c, hs]), ALU.mult).then_inc(kl_rdy, 1)

        def recur(i, s, bt, c):
            n = lambda k=1, m=1: i * NT * m + c * m + k
            par = s % 2
            if 0 < c < NT - 1:
                pool.wait_ge(st_rdy, 1 + val(i, NT - 1, c))
                pool.wait_ge(gt_rdy, 1 + 2 * n())
                tt(Sg[:, :, :], St[:, (c - 1) % 2, :, :], heads(gt[:, par, c, :], GP), ALU.mult).then_inc(sg_rdy, 1)
            pool.wait_ge(dq_rdy, 1 + val(i, NT, c + 1))
            pool.wait_ge(os_rdy, 1 + 2 * n(0))
            pool.wait_ge(v_rdy, 1 + val(i, NT, c + 1))
            tt(vq[:, :, :, :].rearrange("p a j d -> p (a j) d"), hd(v[:, par, c, :]), heads(dq[:, par, c, :]), ALU.mult).then_inc(vq_rdy, 1)

        def gate_heads(i, s):
            o3 = flat(on).rearrange("p c (h d) -> p (c h) d", d=DH)
            pool.wait_ge(ms_rdy, 1 + i + 1)
            tt(ro[:, :], ms[:, :], mhalf[:, :], ALU.pow).then_inc(ro_rdy, 1)
            pool.wait_ge(ro_rdy, 1 + i + 1)
            tt(o3, o3, heads(ro[:, :], NQ), ALU.mult).then_inc(on_mid, 1)
            pool.wait_ge(on_mid, 1 + i + 1)
            tt(o3, o3, onw[:, :].rearrange("p (o d) -> p o d", o=1).to_broadcast([P, NQ, DH]), ALU.mult).then_inc(on_rdy, 1)
            pool.wait_ge(sl_rdy, 1 + i + 1)
            pool.wait_ge(g_rdy, 1 + val(i, NT, NT))
            tt(flat(on).rearrange("p c n -> p (c n)"), flat(on).rearrange("p c n -> p (c n)"),
               gsb[:, s % 2, :, :].rearrange("p c n -> p (c n)"), ALU.mult).then_inc(og_rdy, 1)

        def tiles(i, s, bt, now=None):
            for c in range(NT):
                prepare_q(i, s, bt, c)
                if now and c > 0:
                    recur(*now, c - 1)
                if c + 1 < NT:
                    normalise(i, s, bt, c + 1)
                prepare_k(i, s, bt, c)
                if c + 1 < NT:
                    decay_rhs(i, s, bt, c + 1)
                if c + 2 < NT:
                    rotate(i, s, bt, c + 2)

        def begin(i, s, bt):
            decay_rhs(i, s, bt, 0)
            rotate(i, s, bt, 0)
            normalise(i, s, bt, 0)
            rotate(i, s, bt, 1)

        begin(0, 0, 0)
        tiles(0, 0, 0)
        begin(1, 1, 0)
        with pool.Fori(0, B) as b:
            for s in range(NG):
                i = b * NG + s
                tiles(i + 1, (s + 1) % NG, b + (s + 1) // NG, (i, s, b))
                recur(i, s, b, NT - 1)
                gate_heads(i, s)
                begin(i + 2, (s + 2) % NG, b + (s + 2) // NG)

    @block.scalar
    def _(act):
        A = nc.scalar.activation

        def gates(nb):
            act.wait_ge(zg_rdy, 1 + 2 * nb + 2)
            A(eb[:, :, :], zg[:, :, 0:H], ACT.Exp, scale=-1.0).then_inc(eb_rdy, 1)
            A(ab[:, :, :], zg[:, :, H:], ACT.Abs).then_inc(ab_rdy, 1)
            act.wait_ge(ab_rdy, 1 + nb + 1)
            A(ab[:, :, :], ab[:, :, :], ACT.Exp, scale=-1.0).then_inc(abe_rdy, 1)
            act.wait_ge(abe_rdy, 1 + nb + 1)
            A(sp1[:, :, :], ab[:, :, :], ACT.Ln, bias=one_ap).then_inc(sp_rdy, 1)
            act.wait_ge(sum_ps, 1 + nb + 1)
            act.wait_ge(kl_rdy, 1 + nb * NG * NT)
            A(coef[:, G_INCL:G_ALL + 1, :, :].rearrange("p k c h -> p (k c h)"), ps[:, 2, 0:4 * NT * H], ACT.Exp).then_inc(sum_rdy, 1)

        def conv(i, s, ns):
            for n in ns:
                first_tap(i, s, n)
                if n > 0:
                    silu(i, n - 1)

        def first_tap(i, s, n):
            X, t = n // CT, n % CT
            act.wait_ge(cv_ps, 1 + val(i, 6, n + 1))
            act.wait_ge(cv_rdy, 1 + val(i, 6, max(0, n - 1)))
            A(acc[:, n % 2, :], ps[:, CV_BANK[n], :], ACT.Identity, bias=cw[:, X, s * CT + t, TAPS:TAPS + 1],
              scale=cw[:, X, s * CT + t, TAPS - 1:TAPS]).then_inc(cv_t0, 1)

        def silu(i, n):
            X, t = n // CT, n % CT
            act.wait_ge(cv_acc, 1 + val(i, 6, n + 1))
            if n == 0:
                act.wait_ge(in_ps, 1 + i * NT)
            A(xc[:, X, t, :], acc[:, n % 2, :], ACT.Silu).then_inc(cv_rdy, 1)

        def g_copies(i, s, cs):
            if cs[0] == 0 and not (isinstance(i, int) and i < 2):
                act.wait_ge(og_rdy, 1 + i - 1)
            for c in cs:
                act.wait_ge(g_ps, 1 + val(i, NT, c + 1))
                A(gsb[:, s % 2, c, :], ps[:, 2 + c % 2, 0:GW], ACT.Copy).then_inc(g_rdy, 1)

        def intake(i, s, bt, c):
            n = lambda k=1, m=1: i * NT * m + c * m + k
            par = s % 2
            act.wait_ge(vin_ps, 1 + n())
            A(v[:, par, c, :], ps[:, V_BANK[c], 0:GW], ACT.Copy).then_inc(v_rdy, 1)
            act.wait_ge(coef_rdy, 1 + bt + 1)
            if not (isinstance(i, int) and i < 2):
                act.wait_ge(sg_rdy, 1 + (i - 1) * (NT - 2))
            for j in range(2):
                r = slice(j * DH, (j + 1) * DH)
                A(gt[r, par, c, :], coef[r, G_ALL, c, s * GH:(s + 1) * GH].rearrange("p (a j) -> p a j", j=2)[:, :, j],
                  ACT.Copy).then_inc(gt_rdy, 1)

        def squares(i, s, bt, c):
            n = lambda k=1, m=1: i * NT * m + c * m + k
            act.wait_ge(qk_rdy, 1 + n())
            A(sq[:, :], qk[:, c % 2, :, :].rearrange("p a n -> p (a n)"), ACT.Square).then_inc(sq_rdy, 1)

        def decay_exp(i, s, bt, c):
            n = lambda k=1, m=1: i * NT * m + c * m + k
            act.wait_ge(e_ps, 1 + n())
            act.wait_ge(lt_rdy, 1 + 2 * n(0))
            act.wait_ge(em_rdy, 1 + n(0))
            A(flat(ex).rearrange("p h t -> p (h t)"), ps[:, 6, :], ACT.Exp).then_inc(ex_rdy, 1)

        def prepare(i, s, bt, c, now):
            n = lambda k=1, m=1: i * NT * m + c * m + k
            par = s % 2
            act.wait_ge(kq_ps, 1 + n())
            act.wait_ge(kk_ps, 1 + n(0))
            A(flat(kqT).rearrange("p a k t -> p (a k t)"), ps[:, 7, :], ACT.Copy).then_inc(kqT_rdy, 1)
            if now and c == 0:
                merge64(now[0])
            act.wait_ge(kb_ps, 1 + n())
            A(flat(kbT).rearrange("p a t -> p (a t)"), ps[:, 4, 0:GW], ACT.Copy).then_inc(kbT_rdy, 1)
            A(kgT[:, par, c, :, :].rearrange("p a t -> p (a t)"), ps[:, 4, GW:2 * GW], ACT.Copy).then_inc(kgT_rdy, 1)
            act.wait_ge(qg_ps, 1 + n())
            A(qgT[:, par, c, :, :].rearrange("p a t -> p (a t)"), ps[:, 5, 0:GW], ACT.Copy).then_inc(qgT_rdy, 1)

        def recur(i, s, bt, c):
            n = lambda k=1, m=1: i * NT * m + c * m + k
            act.wait_ge(u_ps, 1 + n())
            act.wait_ge(o_ps, 1 + n(0))
            A(flat(us).rearrange("p h d -> p (h d)"), ps[:, 2, 0:GW], ACT.Copy).then_inc(us_rdy, 1)

        def out_squares(i, s, bt):
            act.wait_ge(os_rdy, 1 + val(i, 2 * NT, 2 * NT))
            if s == 0:
                act.wait_ge(wo_ps, 1 + KC * bt)
            A(osq(s), flat(on).rearrange("p c n -> p (c n)"), ACT.Square).then_inc(osq_rdy, 1)

        def out_heads(i, s):
            act.wait_ge(on_rdy, 1 + i + 1)
            A(flat(on), flat(on), ACT.Silu).then_inc(sl_rdy, 1)

        def out_heads_T(i, s, bt):
            for k in range(CT):
                act.wait_ge(oT_ps, 1 + 2 * i + k + 1)
                A(oT[:, s * CT + k, :], ps[:, 2 + k, :], ACT.Copy).then_inc(oT_rdy, 1)

        def merge32(i):
            act.wait_ge(y32_ps, 1 + i + 1)
            for r in range(2):
                q = slice(64 * r + 32, 64 * r + 64)
                A(Y32[q, :, :].rearrange("p q t -> p (q t)"), ps[q, 7, :], ACT.Copy).then_inc(y32_rdy, 1)

        def merge32_end(i):
            act.wait_ge(r32_ps, 1 + i + 1)
            for r in range(2):
                q = slice(64 * r, 64 * r + 32)
                A(Rf[q, :, 64 * r + 32:64 * r + 64], ps[q, 1, :].rearrange("p (q t) -> p q t", q=NQ), ACT.Copy,
                  scale=-1.0).then_inc(rf_b, 1)

        def merge64(i):
            act.wait_ge(y64_ps, 1 + i + 1)
            for k in range(2):
                A(Y64[64:, 8 * k:8 * k + 8, :].rearrange("p q t -> p (q t)"), ps[64:, k, :], ACT.Copy).then_inc(y64_rdy, 1)

        def merge64_end(i):
            act.wait_ge(r64_ps, 1 + i + 1)
            for k in range(2):
                A(Rf[0:64, 8 * k:8 * k + 8, 64:], ps[0:64, k, :].rearrange("p (q t) -> p q t", q=8), ACT.Copy,
                  scale=-1.0).then_inc(rf_c, 1)

        act.wait_ge(loaded, 1 + LOADED)
        act.wait_ge(init0, 1 + 1)
        A(expA[:, :], rows[:, 3, :], ACT.Exp).then_inc(init0, 1)
        gates(0)
        conv(0, 0, range(6))
        silu(0, 5)
        g_copies(0, 0, range(NT))

        def tiles(i, s, bt, now=None):
            for c in range(NT):
                if c > 0:
                    decay_exp(i, s, bt, c)
                if now and c > 0:
                    recur(*now, c - 1)
                prepare(i, s, bt, c, now)
                if c + 1 < NT:
                    intake(i, s, bt, c + 1)
                if now and c == 0:
                    merge64_end(now[0])
                if c + 2 < NT:
                    squares(i, s, bt, c + 2)

        squares(0, 0, 0, 0)
        intake(0, 0, 0, 0)
        decay_exp(0, 0, 0, 0)
        squares(0, 0, 0, 1)
        tiles(0, 0, 0)
        conv(1, 1, range(5))
        first_tap(1, 1, 5)
        g_copies(1, 1, range(2))
        squares(1, 1, 0, 0)
        silu(1, 4)
        g_copies(1, 1, range(2, NT))
        silu(1, 5)
        act.wait_ge(init1, 1 + 5)
        merge32(0)
        intake(1, 1, 0, 0)
        decay_exp(1, 1, 0, 0)
        merge32_end(0)
        squares(1, 1, 0, 1)
        with act.Fori(0, B) as b:
            for s in range(NG):
                i = b * NG + s
                tiles(i + 1, (s + 1) % NG, b + (s + 1) // NG, (i, s, b))
                conv(i + 2, (s + 2) % NG, range(1))
                recur(i, s, b, NT - 1)
                out_squares(i, s, b)
                conv(i + 2, (s + 2) % NG, range(1, 2))
                if s == 2:
                    gates(b + 1)
                conv(i + 2, (s + 2) % NG, range(2, 5))
                first_tap(i + 2, (s + 2) % NG, 5)
                out_heads(i, s)
                g_copies(i + 2, (s + 2) % NG, range(2))
                squares(i + 2, (s + 2) % NG, b + (s + 2) // NG, 0)
                silu(i + 2, 4)
                g_copies(i + 2, (s + 2) % NG, range(2, NT))
                silu(i + 2, 5)
                merge32(i + 1)
                intake(i + 2, (s + 2) % NG, b + (s + 2) // NG, 0)
                decay_exp(i + 2, (s + 2) % NG, b + (s + 2) // NG, 0)
                merge32_end(i + 1)
                out_heads_T(i, s, b)
                squares(i + 2, (s + 2) % NG, b + (s + 2) // NG, 1)

    @block.vector
    def _(dve):
        V = nc.vector
        V.memset(one_t[:, :], 1.0).then_inc(init0, 1)
        dve.wait_ge(loaded, 1 + LOADED)
        dve.wait_ge(init0, 1 + 2)

        def gates(nb):
            dve.wait_ge(zg_ps, 1 + nb + 1)
            dve.wait_ge(kl_rdy, 1 + nb * NG * NT)
            z3 = zg[:, :, :]
            dve.wait_ge(eb_rdy, 1 + nb)
            V.tensor_tensor(z3, ps[:, 3, 0:2 * H * NT].rearrange("p (c h) -> p c h", c=NT),
                            rows[:, 0:2, :].rearrange("p (o a) h -> p o (a h)", o=1).to_broadcast([P, NT, 2 * H]),
                            ALU.add).then_inc(zg_rdy, 1)
            dve.wait_ge(zg_rdy, 1 + 2 * nb + 1)
            V.tensor_tensor(zg[:, :, H:], zg[:, :, H:], rows[:, 2:3, :].to_broadcast([P, NT, H]), ALU.add).then_inc(zg_rdy, 1)
            dve.wait_ge(zg_rdy, 1 + 2 * nb + 2)
            dve.wait_ge(eb_rdy, 1 + nb + 1)
            V.tensor_scalar(eb[:, :, :], eb[:, :, :], 1.0, None, ALU.add).then_inc(gstep, 1)
            dve.wait_ge(gstep, 1 + nb * 4 + 1)
            V.reciprocal(coef[:, BETA, :, :], eb[:, :, :]).then_inc(gstep, 1)
            dve.wait_ge(sp_rdy, 1 + nb + 1)
            V.scalar_tensor_tensor(out=sp1[:, :, :], in0=zg[:, :, H:], scalar=0.0, in1=sp1[:, :, :],
                                   op0=ALU.max, op1=ALU.add).then_inc(gstep, 1)
            dve.wait_ge(gstep, 1 + nb * 4 + 3)
            V.scalar_tensor_tensor(out=sp1[:, :, :], in0=sp1[:, :, :], scalar=-1.0,
                                   in1=expA[:, :].rearrange("p (o h) -> p o h", o=1).to_broadcast([P, NT, H]),
                                   op0=ALU.mult, op1=ALU.mult).then_inc(gstep, 1)
            dve.wait_ge(gstep, 1 + nb * 4 + 4)
            V.tensor_scalar(la[:, :, :], sp1[:, :, :], LOG_FLOOR, None, ALU.max).then_inc(la_rdy, 1)
            dve.wait_ge(sum_rdy, 1 + nb + 1)
            V.tensor_tensor(coef[:, B_AFTER, :, :], coef[:, BETA, :, :], coef[:, G_AFTER, :, :], ALU.mult).then_inc(coef_rdy, 1)

        def conv_items(i, s, ns):
            for n in ns:
                X, t = n // CT, n % CT
                dve.wait_ge(cv_t0, 1 + val(i, 6, n + 1))
                a = acc[:, n % 2, :]
                for k in range(1, TAPS):
                    if k > 1:
                        dve.wait_ge(cv_mid, 1 + val(i, 12, 2 * n + k - 1))
                    V.scalar_tensor_tensor(out=a[:, k:], in0=ps[:, CV_BANK[n], 0:T - k],
                                           scalar=cw[:, X, s * CT + t, TAPS - 1 - k:TAPS - k], in1=a[:, k:],
                                           op0=ALU.mult, op1=ALU.add).then_inc(cv_mid if k < TAPS - 1 else cv_acc, 1)

        def intake(i, s, bt, c):
            n = lambda k=1, m=1: i * NT * m + c * m + k
            dve.wait_ge(in_ps, 1 + n())
            dve.wait_ge(qk_rdy, 1 + n(0))
            src = ps[:, IN_BANK[c], :].rearrange("p (h i e) -> p h e i", h=2 * GH, e=2)
            for e, m, name in ((0, m1, rot_rdy), (1, m2, rot_rdy)):
                V.tensor_tensor(m[:, :].rearrange("p (h a i) -> p h a i", h=2 * GH, a=2),
                                src[:, :, e:e + 1, :].to_broadcast([P, 2 * GH, 2, DH // 2]),
                                rope[:, c, e:e + 1, :, :].to_broadcast([P, 2 * GH, 2, DH // 2]), ALU.mult).then_inc(name, 1)

        def norms(i, s, bt, c):
            n = lambda k=1, m=1: i * NT * m + c * m + k
            dve.wait_ge(sq_rdy, 1 + n())
            dve.wait_ge(rn_rdy, 1 + n(0))
            V.tensor_reduce(ss[:, :], hd(sq[:, :], 2 * GH), AX.X, ALU.add).then_inc(ss_mid, 1)
            dve.wait_ge(ss_mid, 1 + n())
            V.tensor_scalar(ss[:, :], ss[:, :], RMS_EPS, None, ALU.add).then_inc(ss_rdy, 1)

        def scale_keys(i, s, bt, c):
            n = lambda k=1, m=1: i * NT * m + c * m + k
            dve.wait_ge(qkn_rdy, 1 + n())
            dve.wait_ge(kb_ps, 1 + n(0))
            for k, name in ((0, BETA), (1, G_INCL)):
                V.tensor_tensor(hd(kbg[:, k, :]), hd(qk[:, c % 2, 1, :]), heads(coef[:, name, c, s * GH:(s + 1) * GH]),
                                ALU.mult).then_inc(kbg_rdy, 1)

        def mask_decay(i, s, bt, c):
            n = lambda k=1, m=1: i * NT * m + c * m + k
            dve.wait_ge(ex_rdy, 1 + n())
            dve.wait_ge(at_rdy, 1 + 2 * n(0))
            V.tensor_tensor(em[:, :, 1:], ex[:, :, 0:P - 1], mshift[:, 1:].rearrange("p (o t) -> p o t", o=1).to_broadcast([P, GH, P - 1]),
                            ALU.mult).then_inc(em_rdy, 1)

        def products(i, s, bt, c):
            n = lambda k=1, m=1: i * NT * m + c * m + k
            par = s % 2
            dve.wait_ge(kk_ps, 1 + n())
            dve.wait_ge(em_rdy, 1 + n())
            for j in range(2):
                bank = ps[:, 6 + j, :].rearrange("p (a k t) -> p a k t", a=GP, k=2)
                pick = lambda t: t.rearrange("p (a j) t -> p a j t", j=2)[:, :, j, :]
                V.tensor_tensor(pick(LT[:, c, :, :]), bank[:, :, 0, :], pick(ex[:, :, :]), ALU.mult).then_inc(lt_rdy, 1)
                V.tensor_tensor(pick(AT[:, par, c, :, :]), bank[:, :, 1, :], pick(em[:, :, :]), ALU.mult).then_inc(at_rdy, 1)

        def dot_qk(i, s, bt, c):
            n = lambda k=1, m=1: i * NT * m + c * m + k
            dve.wait_ge(qkn_rdy, 1 + n())
            V.tensor_tensor(qkp, qk[:, c % 2, 0, :], qk[:, c % 2, 1, :], ALU.mult).then_inc(qkd_mid, 1)
            dve.wait_ge(qkd_mid, 1 + 2 * n(0) + 1)
            V.tensor_reduce(qkd[:, :], hd(qkp), AX.X, ALU.add).then_inc(qkd_mid, 1)
            dve.wait_ge(qkd_mid, 1 + 2 * n())
            V.tensor_tensor(dq[:, s % 2, c, :], qkd[:, :], rows[:, 4, s * GH:(s + 1) * GH], ALU.mult).then_inc(dq_rdy, 1)

        def substitute(i):
            dve.wait_ge(lb_rd, 1 + i * 32 + 32)
            dve.wait_ge(tb_wr, 1 + i * 32)
            for t in range(1, BL):
                k = val(i, 2 * (BL - 1), 2 * t - 1)
                pv = pb[:, 0:t * t].rearrange("p (c j) -> p c j", c=t)
                V.tensor_tensor(pv, LB[:, 0:t, t:t + 1].rearrange("p j o -> p o j").to_broadcast([P, t, t]),
                                TB[:, 0:t, 0:t].rearrange("p j c -> p c j"), ALU.mult).then_inc(tbs, 1)
                dve.wait_ge(tbs, 1 + k)
                last = V.tensor_reduce(TB[:, t, 0:t], pv, AX.X, ALU.add, negate=True).then_inc(tbs, 1)
                dve.wait_ge(tbs, 1 + k + 1)
            V.memset(pb[:, 0:1], 0.0).then_inc(tb_step, 1)

        def merge16(i):
            dve.wait_ge(t16_rd, 1 + i * 64 + 64)
            V.transpose(flat(R16).rearrange("p q t -> p (q t)"), flat(T16).rearrange("p q t -> p (q t)")).then_inc(b16_rdy, 1)
            dve.wait_ge(b16_ps, 1 + 2 * i + 1)
            dve.wait_ge(r32_ps, 1 + i)
            dve.wait_ge(t32_ps, 1 + i)
            V.tensor_tensor(flat(Y16), ps[:, 4, :].rearrange("p (q t) -> p q t", q=NQ),
                            m16[:, :].rearrange("p (o t) -> p o t", o=1).to_broadcast([P, NQ, 32]), ALU.mult).then_inc(b16_rdy, 1)

        def merge16_end(i):
            dve.wait_ge(b16_ps, 1 + 2 * i + 2)
            V.tensor_tensor(flat(kbg).rearrange("p k n -> p (k n)"), flat(T16).rearrange("p q t -> p (q t)"), ps[:, 6, :],
                            ALU.subtract).then_inc(b32_rdy, 1)
            dve.wait_ge(b32_rdy, 1 + 2 * i + 1)
            V.transpose(flat(R32).rearrange("p q t -> p (q t)"), flat(kbg).rearrange("p k n -> p (k n)")).then_inc(b32_rdy, 1)

        def merge32(i):
            dve.wait_ge(b32_rdy, 1 + 2 * i + 2)
            dve.wait_ge(u_ps, 1 + i * NT)
            for r in range(4):
                q = slice(32 * r, 32 * r + 32)
                V.tensor_copy(Rf[q, :, q], R32[q, :, :]).then_inc(rf_a, 1)
            dve.wait_ge(y64_ps, 1 + i)
            for r in range(2):
                q = slice(32 * r, 32 * r + 32)
                V.tensor_copy(T64[q, :, q], T32[q, :, :]).then_inc(t64_rdy, 1)

        def merge32_end(i):
            dve.wait_ge(t32_ps, 1 + i + 1)
            V.tensor_scalar(T64[32:64, :, 0:32], ps[32:64, 0, :].rearrange("p (q t) -> p q t", q=NQ), -1.0, None,
                            ALU.mult).then_inc(t64_rdy, 1)

        def solve_rhs(i, s, bt, c):
            n = lambda k=1, m=1: i * NT * m + c * m + k
            par = s % 2
            if c > 0:
                dve.wait_ge(x_ps, 1 + val(i, NT - 1, c))
                dve.wait_ge(u_ps, 1 + n(0))
                dve.wait_ge(v_rdy, 1 + n())
                for j in range(2):
                    V.tensor_tensor(rh[:, :, j, :], v[:, par, c, :].rearrange("p (a j d) -> p a j d", a=GP, j=2)[:, :, j, :],
                                    ps[:, j, 0:GP * DH].rearrange("p (a d) -> p a d", a=GP), ALU.subtract).then_inc(rh_rdy, 1)

        def state(i, s, bt, c):
            if c < NT - 1:
                dve.wait_ge(s_ps, 1 + val(i, NT - 1, c + 1))
                dst = St[:, c % 2, :, :].rearrange("p a d -> p (a d)")
                src = ps[:, 2, GW:GW + GP * DH]
                if c == 0:
                    V.tensor_copy(dst, src).then_inc(st_rdy, 1)
                else:
                    dve.wait_ge(sg_rdy, 1 + val(i, NT - 2, c))
                    V.tensor_tensor(dst, flat(Sg).rearrange("p a d -> p (a d)"), src, ALU.add).then_inc(st_rdy, 1)

        def outputs(i, s, bt, c):
            n = lambda k=1, m=1: i * NT * m + c * m + k
            dve.wait_ge(o_ps, 1 + n())
            dve.wait_ge(vq_rdy, 1 + n())
            if c == 0:
                dve.wait_ge(oT_ps, 1 + 2 * i)
                dve.wait_ge(zT_ps, 1 + 2 * bt)
            o4 = on[:, c, :].rearrange("p (a j d) -> p a j d", a=GP, j=2)
            for j in range(2):
                V.tensor_tensor(o4[:, :, j, :], ps[:, j, 0:GP * DH].rearrange("p (a d) -> p a d", a=GP), vq[:, :, j, :],
                                ALU.add).then_inc(os_rdy, 1)

        def mean_squares(i, s):
            dve.wait_ge(osq_rdy, 1 + i + 1)
            dve.wait_ge(ro_rdy, 1 + i)
            V.tensor_reduce(ms[:, :], hd(osq(s), NQ), AX.X, ALU.add).then_inc(ms_mid, 1)
            dve.wait_ge(ms_mid, 1 + i + 1)
            V.tensor_scalar(ms[:, :], ms[:, :], 1.0 / DH, RMS_EPS, ALU.mult, ALU.add).then_inc(ms_rdy, 1)

        def output(b):
            for m in range(KC):
                dve.wait_ge(wo_ps, 1 + b * KC + m + 1)
                if m == 0:
                    dve.wait_ge(gate_in, 1 + b * 16 + 16)
                    dve.wait_ge(zT_ps, 1 + b * 2)
                V.tensor_tensor(z[:, m, :], ps[:, m, :], gate[:, m, :], ALU.mult).then_inc(z_rdy, 1)
            dve.wait_ge(x_in, 1 + b * 16 + 16)
            for k in range(2):
                dve.wait_ge(zT_ps, 1 + b * 2 + k + 1)
                xv = xio[:, 2 * k:2 * k + 2, :].rearrange("p w n -> p (w n)")
                V.tensor_tensor(xv, xv, ps[:, 2 + k, :], ALU.add).then_inc(xo_rdy, 1)

        gates(0)
        conv_items(0, 0, range(6))

        def tiles(i, s, bt, now=None):
            for c in range(NT):
                if now and c > 0:
                    solve_rhs(*now, c - 1)
                scale_keys(i, s, bt, c)
                mask_decay(i, s, bt, c)
                if c + 1 < NT:
                    norms(i, s, bt, c + 1)
                dot_qk(i, s, bt, c)
                if now and c > 0:
                    state(*now, c - 1)
                    outputs(*now, c - 1)
                if c + 2 < NT:
                    intake(i, s, bt, c + 2)
                if now and c == 0:
                    dve.wait_ge(y64_ps, 1 + now[0] + 1)
                products(i, s, bt, c)

        intake(0, 0, 0, 0)
        norms(0, 0, 0, 0)
        intake(0, 0, 0, 1)
        tiles(0, 0, 0)
        conv_items(1, 1, range(0, 2))
        substitute(0)
        conv_items(1, 1, range(2, 4))
        dve.wait_ge(init1, 1 + 5)
        merge16(0)
        intake(1, 1, 0, 0)
        conv_items(1, 1, range(4, 6))
        merge16_end(0)
        merge32(0)
        norms(1, 1, 0, 0)
        merge32_end(0)
        intake(1, 1, 0, 1)
        with dve.Fori(0, B) as b:
            for s in range(NG):
                i = b * NG + s
                tiles(i + 1, (s + 1) % NG, b + (s + 1) // NG, (i, s, b))
                solve_rhs(i, s, b, NT - 1)
                conv_items(i + 2, (s + 2) % NG, range(0, 1))
                outputs(i, s, b, NT - 1)
                substitute(i + 1)
                mean_squares(i, s)
                if s == 2:
                    gates(b + 1)
                conv_items(i + 2, (s + 2) % NG, range(1, 2))
                conv_items(i + 2, (s + 2) % NG, range(2, 4))
                merge16(i + 1)
                intake(i + 2, (s + 2) % NG, b + (s + 2) // NG, 0)
                conv_items(i + 2, (s + 2) % NG, range(4, 6))
                merge16_end(i + 1)
                merge32(i + 1)
                norms(i + 2, (s + 2) % NG, b + (s + 2) // NG, 0)
                intake(i + 2, (s + 2) % NG, b + (s + 2) // NG, 1)
                merge32_end(i + 1)
                if s == NG - 1:
                    output(b)

    @block.tensor
    def _(pe):
        mm, tr = nc.tensor.matmul, nc.tensor.transpose

        def gates(nb):
            pe.wait_ge(xn_in, 1 + nb * 16 + 16)
            if not isinstance(nb, int):
                pe.wait_ge(us_rdy, 1 + (nb * NG - 1) * NT)
                pe.wait_ge(st_rdy, 1 + (nb * NG - 1) * (NT - 1))
                pe.wait_ge(rot_rdy, 1 + 2 * nb * NG * NT)
            for c in range(NT):
                for k in range(KC):
                    last = mm(ps[:, 3, c * 2 * H:(c + 1) * 2 * H], xnT[:, k, c * P:(c + 1) * P], wgate[:, k, :],
                              start=k == 0, stop=k == KC - 1)
            last.then_inc(zg_ps, 1)

        def gate_sums(nb):
            pe.wait_ge(la_rdy, 1 + nb + 1)
            for k in range(4):
                last = mm(ps[:, 2, k * NT * H:(k + 1) * NT * H], tri[:, k, :], la[:, :, :].rearrange("p c h -> p (c h)"),
                          start=True, stop=True)
            last.then_inc(sum_ps, 1)

        def g_proj(i, s, bt, cs):
            for c in cs:
                if c < 2:
                    if s == 0:
                        pe.wait_ge(sum_rdy, 1 + bt + 1)
                    if not (isinstance(i, int) and i < 2):
                        pe.wait_ge(us_rdy, 1 + (i - 1) * NT)
                        pe.wait_ge(st_rdy, 1 + (i - 1) * (NT - 1))
                    if not (isinstance(i, int) and i == 0):
                        pe.wait_ge(rot_rdy, 1 + 2 * i * NT)
                else:
                    pe.wait_ge(g_rdy, 1 + val(i, NT, c - 1))
                for k in range(KC):
                    last = mm(ps[:, 2 + c % 2, 0:GW], xnT[:, k, c * P:(c + 1) * P], wg[:, k, s * GW:(s + 1) * GW],
                              start=k == 0, stop=k == KC - 1)
                last.then_inc(g_ps, 1)

        def conv(i, s, bt, ns):
            for n in ns:
                X, t = n // CT, n % CT
                if n < 4:
                    if not (isinstance(i, int) and i == 0):
                        pe.wait_ge(at_rdy, 1 + i * 2 * NT)
                        pe.wait_ge(qgT_rdy, 1 + i * NT)
                    if s == 0:
                        pe.wait_ge(xn_in, 1 + bt * 16 + 16)
                elif not (isinstance(i, int) and i < 2):
                    pe.wait_ge(os_rdy, 1 + (i - 1) * 2 * NT)
                elif not (isinstance(i, int) and i == 0):
                    pe.wait_ge(v_rdy, 1 + i * NT)
                for k in range(KC):
                    last = mm(ps[:, CV_BANK[n], :], wqkv[:, X, k, s * GW + t * P:s * GW + (t + 1) * P], xnT[:, k, :],
                              start=k == 0, stop=k == KC - 1)
                last.then_inc(cv_ps, 1)

        def intake(i, s, bt, c):
            n = lambda k=1, m=1: i * NT * m + c * m + k
            if c == 0:
                pe.wait_ge(cv_rdy, 1 + val(i, 6, 4))
            if c == 1:
                pe.wait_ge(b16_rdy, 1 + 2 * i)
            if c == 2:
                if isinstance(i, int):
                    pe.wait_ge(g_rdy, 1 + (i + 1) * NT)
                else:
                    pe.wait_ge(oT_rdy, 1 + (i - 1) * CT)
                    if s == 1:
                        pe.wait_ge(xo_rdy, 1 + 2 * bt)
            pe.wait_ge(rot_rdy, 1 + 2 * n(0))
            for X in range(2):
                for t in range(CT):
                    last = tr(ps[:, IN_BANK[c], X * GW + t * P:X * GW + (t + 1) * P], xc[:, X, t, c * P:(c + 1) * P], ident[:, :])
            last.then_inc(in_ps, 1)

        def intake_v(i, s, bt, c):
            n = lambda k=1, m=1: i * NT * m + c * m + k
            if c == 0:
                pe.wait_ge(cv_rdy, 1 + val(i, 6, 6))
            else:
                pe.wait_ge(qgT_rdy, 1 + n(0))
            for t in range(CT):
                last = tr(ps[:, V_BANK[c], t * P:(t + 1) * P], xc[:, 2, t, c * P:(c + 1) * P], ident[:, :])
            last.then_inc(vin_ps, 1)

        def decay_sums(i, s, bt, c):
            n = lambda k=1, m=1: i * NT * m + c * m + k
            if c == 0:
                pe.wait_ge(y32_rdy, 1 + 2 * i)
                pe.wait_ge(b32_rdy, 1 + 2 * i)
            pe.wait_ge(lm_rdy, 1 + n())
            pe.wait_ge(lt_rdy, 1 + 2 * n(0))
            pe.wait_ge(at_rdy, 1 + 2 * n(0))
            mm(ps[:, 6, :], tri[:, AFTER, :], lm[:, :, :].rearrange("p h t -> p (h t)"), start=True, stop=True).then_inc(e_ps, 1)

        def keys_T(i, s, bt, c):
            n = lambda k=1, m=1: i * NT * m + c * m + k
            pe.wait_ge(qkn_rdy, 1 + n())
            if c == 0:
                pe.wait_ge(rot_rdy, 1 + 2 * n(2))
            for t in range(GP):
                for k, part in ((0, 1), (1, 0)):
                    last = tr(ps[:, 7, (2 * t + k) * P:(2 * t + k + 1) * P], qk[:, c % 2, part, t * P:(t + 1) * P], ident[:, :])
            last.then_inc(kq_ps, 1)
            pe.wait_ge(kbg_rdy, 1 + 2 * n())
            pe.wait_ge(kgT_rdy, 1 + n(0))
            for k in range(2):
                for t in range(GP):
                    last = tr(ps[:, 4, k * GW + t * P:k * GW + (t + 1) * P], kbg[:, k, t * P:(t + 1) * P], ident[:, :])
            last.then_inc(kb_ps, 1)

        def queries_T(i, s, bt, c):
            n = lambda k=1, m=1: i * NT * m + c * m + k
            pe.wait_ge(qg_rdy, 1 + n())
            pe.wait_ge(v_rdy, 1 + n())
            for t in range(GP):
                last = tr(ps[:, 5, t * P:(t + 1) * P], qg[:, t * P:(t + 1) * P], ident[:, :])
            last.then_inc(qg_ps, 1)

        def products(i, s, bt, c):
            n = lambda k=1, m=1: i * NT * m + c * m + k
            pe.wait_ge(kqT_rdy, 1 + n())
            pe.wait_ge(kbT_rdy, 1 + n())
            pe.wait_ge(ex_rdy, 1 + n())
            for j in range(2):
                r = slice(j * DH, (j + 1) * DH)
                for a in range(GP):
                    last = mm(ps[:, 6 + j, a * 2 * P:(a + 1) * 2 * P], kbT[r, a, :],
                              kqT[r, a, :, :].rearrange("p k t -> p (k t)"), start=True, stop=True)
            last.then_inc(kk_ps, 1)

        LTq = LT[:, :, :, :].rearrange("p c h t -> p (c h) t")

        def merge16(i, s, bt):
            pe.wait_ge(t16_rd, 1 + i * 64 + 64)
            pe.wait_ge(cv_acc, 1 + val(i + 1, 6, 4))
            pe.sem_inc(passed, 1)
            for r in range(4):
                q = slice(32 * r, 32 * r + 32)
                for m in range(NQ):
                    last = mm(ps[q, 4, 32 * m:32 * m + 32], LTq[q, m, q], T16[q, m, :], start=True, stop=True)
            last.then_inc(b16_ps, 1)
            intake(i + 1, s, bt, 0)
            g_proj(i + 1, s, bt, range(2))
            pe.wait_ge(b16_rdy, 1 + 2 * i + 2)
            pe.sem_inc(passed, 1)
            for r in range(4):
                q = slice(32 * r, 32 * r + 32)
                for m in range(NQ):
                    last = mm(ps[q, 6, 32 * m:32 * m + 32], R16[q, m, :], Y16[q, m, :], start=True, stop=True)
            last.then_inc(b16_ps, 1)
            g_proj(i + 1, s, bt, range(2, NT))

        def merge32(i):
            pe.wait_ge(b32_rdy, 1 + 2 * i + 1)
            pe.sem_inc(passed, 1)
            for r in range(2):
                q1, q2 = slice(64 * r, 64 * r + 32), slice(64 * r + 32, 64 * r + 64)
                for m in range(NQ):
                    last = mm(ps[q2, 7, 32 * m:32 * m + 32], LTq[q1, m, q2], T32[q1, m, :], start=True, stop=True)
            last.then_inc(y32_ps, 1)

        def merge32_end(i):
            pe.wait_ge(y32_rdy, 1 + 2 * i + 2)
            pe.wait_ge(b32_rdy, 1 + 2 * i + 2)
            pe.sem_inc(passed, 1)
            for r in range(2):
                q1, q2 = slice(64 * r, 64 * r + 32), slice(64 * r + 32, 64 * r + 64)
                for m in range(NQ):
                    last = mm(ps[q1, 1, 32 * m:32 * m + 32], Y32[q2, m, :], R32[q2, m, :], start=True, stop=True)
            last.then_inc(r32_ps, 1)
            q2 = slice(32, 64)
            pe.wait_ge(v_rdy, 1 + val(i + 1, NT, 1))
            pe.sem_inc(passed, 1)
            for m in range(NQ):
                last = mm(ps[q2, 0, 32 * m:32 * m + 32], R32[q2, m, :], Y32[q2, m, :], start=True, stop=True)
            last.then_inc(t32_ps, 1)

        def merge64(i, s, bt):
            if s == 0:
                pe.wait_ge(z_rdy, 1 + KC * bt)
            pe.wait_ge(t64_rdy, 1 + 3 * i + 3)
            pe.wait_ge(rf_b, 1 + 2 * i + 2)
            pe.sem_inc(passed, 1)
            for m in range(NQ):
                last = mm(ps[64:, m // 8, 64 * (m % 8):64 * (m % 8) + 64], LTq[0:64, m, 64:], T64[0:64, m, :], start=True, stop=True)
            last.then_inc(y64_ps, 1)

        def merge64_end(i):
            pe.wait_ge(y64_rdy, 1 + 2 * i + 2)
            pe.wait_ge(rf_a, 1 + 4 * i + 4)
            pe.sem_inc(passed, 1)
            for m in range(NQ):
                last = mm(ps[0:64, m // 8, 64 * (m % 8):64 * (m % 8) + 64], Y64[64:, m, :], Rf[64:, m, 64:], start=True, stop=True)
            last.then_inc(r64_ps, 1)

        def carried(i, s, bt, c):
            n = lambda k=1, m=1: i * NT * m + c * m + k
            par = s % 2
            if c == 0:
                pe.wait_ge(rf_a, 1 + 4 * i + 4)
                pe.wait_ge(rf_b, 1 + 2 * i + 2)
                pe.wait_ge(rf_c, 1 + 2 * i + 2)
                pe.wait_ge(oT_rdy, 1 + CT * i)
                pe.wait_ge(kl_rdy, 1 + val(i, NT, NT))
                pe.wait_ge(v_rdy, 1 + val(i, NT, NT))
                pe.wait_ge(at_rdy, 1 + val(i, 2 * NT, 2 * NT))
                pe.wait_ge(xo_rdy, 1 + 2 * bt)
                pe.wait_ge(cv_acc, 1 + val(i + 1, 6, 6))
            pe.wait_ge(os_rdy, 1 + 2 * n(0))
            if c > 0:
                pe.wait_ge(st_rdy, 1 + val(i, NT - 1, c))
                for j in range(2):
                    r = slice(j * DH, (j + 1) * DH)
                    for a in range(GP):
                        last = mm(ps[:, j, a * DH:(a + 1) * DH], kgT[r, par, c, a, :], St[r, (c - 1) % 2, a, :], start=True, stop=True)
                last.then_inc(x_ps, 1)

        def solve(i, s, bt, c):
            par = s % 2
            if c > 0:
                pe.wait_ge(rh_rdy, 1 + val(i, 2 * (NT - 1), 2 * c))
            for h in range(GH):
                rhs = rh[:, h // 2, h % 2, :] if c > 0 else v[:, par, c, h * DH:(h + 1) * DH]
                last = mm(ps[:, 2, h * DH:(h + 1) * DH], Rf[:, c * GH + h, :], rhs, start=True, stop=True)
            last.then_inc(u_ps, 1)

        def recur(i, s, bt, c):
            n = lambda k=1, m=1: i * NT * m + c * m + k
            par = s % 2
            pe.wait_ge(us_rdy, 1 + n())
            if c < NT - 1:
                for h in range(GH):
                    a, j = h // 2, h % 2
                    last = mm(ps[j * DH:(j + 1) * DH, 2, GW + a * DH:GW + (a + 1) * DH], kl[:, par, c, h * DH:(h + 1) * DH],
                              us[:, h, :], start=True, stop=True)
                last.then_inc(s_ps, 1)
            pe.wait_ge(v_rdy, 1 + val(i + 1, NT, 1))
            for h in range(GH):
                a, j = h // 2, h % 2
                r = slice(j * DH, (j + 1) * DH)
                dst = ps[:, j, a * DH:(a + 1) * DH]
                if c > 0:
                    mm(dst, qgT[r, par, c, a, :], St[r, (c - 1) % 2, a, :], start=True, stop=False)
                last = mm(dst, AT[:, par, c, h, :], us[:, h, :], start=c == 0, stop=True)
            last.then_inc(o_ps, 1)

        def out_heads(i, s):
            pe.wait_ge(og_rdy, 1 + i + 1)
            pe.wait_ge(g_rdy, 1 + val(i + 2, NT, NT))
            for k in range(CT):
                for c in range(NT):
                    last = tr(ps[:, 2 + k, c * P:(c + 1) * P], on[:, c, k * P:(k + 1) * P], ident[:, :])
                last.then_inc(oT_ps, 1)

        def output(b, i):
            pe.wait_ge(rf_b, 1 + 2 * (i + 1) + 2)
            pe.wait_ge(t64_rdy, 1 + 3 * (i + 1) + 3)
            pe.wait_ge(oT_rdy, 1 + b * NG * CT + NG * CT)
            for m in range(KC):
                for k in range(H * DH // P):
                    last = mm(ps[:, m, :], wo[:, k, m * P:(m + 1) * P], oT[:, k, :], start=k == 0, stop=k == H * DH // P - 1)
                last.then_inc(wo_ps, 1)
            pe.wait_ge(z_rdy, 1 + b * KC + KC)
            for k in range(2):
                for w in range(2):
                    for m in range(KC):
                        last = tr(ps[:, 2 + k, w * D + m * P:w * D + (m + 1) * P], z[:, m, (2 * k + w) * P:(2 * k + w + 1) * P], ident[:, :])
                last.then_inc(zT_ps, 1)

        pe.wait_ge(loaded, 1 + LOADED)
        gates(0)
        gate_sums(0)
        conv(0, 0, 0, range(6))
        g_proj(0, 0, 0, range(NT))

        def tiles(i, s, bt, now=None):
            for c in range(NT):
                if now and c > 1:
                    carried(*now, c - 1)
                if c > 0:
                    decay_sums(i, s, bt, c)
                if now and c == 0:
                    merge64(*now)
                if now and c == 1:
                    carried(*now, 0)
                if now and c > 0:
                    solve(*now, c - 1)
                keys_T(i, s, bt, c)
                queries_T(i, s, bt, c)
                if c + 2 < NT:
                    intake(i, s, bt, c + 2)
                if now and c > 0:
                    recur(*now, c - 1)
                products(i, s, bt, c)
                if c + 1 < NT:
                    intake_v(i, s, bt, c + 1)
                if now and c == 0:
                    merge64_end(now[0])

        intake(0, 0, 0, 0)
        intake_v(0, 0, 0, 0)
        intake(0, 0, 0, 1)
        decay_sums(0, 0, 0, 0)
        tiles(0, 0, 0)
        conv(1, 1, 0, range(6))
        pe.wait_ge(init1, 1 + 5)
        merge16(0, 1, 0)
        merge32(0)
        intake_v(1, 1, 0, 0)
        intake(1, 1, 0, 1)
        decay_sums(1, 1, 0, 0)
        merge32_end(0)
        with pe.Fori(0, B) as b:
            for s in range(NG):
                i = b * NG + s
                tiles(i + 1, (s + 1) % NG, b + (s + 1) // NG, (i, s, b))
                carried(i, s, b, NT - 1)
                conv(i + 2, (s + 2) % NG, b + (s + 2) // NG, range(0, 1))
                solve(i, s, b, NT - 1)
                conv(i + 2, (s + 2) % NG, b + (s + 2) // NG, range(1, 2))
                recur(i, s, b, NT - 1)
                conv(i + 2, (s + 2) % NG, b + (s + 2) // NG, range(2, 6))
                if s == 2:
                    gates(b + 1)
                    gate_sums(b + 1)
                merge16(i + 1, (s + 2) % NG, b + (s + 2) // NG)
                merge32(i + 1)
                intake_v(i + 2, (s + 2) % NG, b + (s + 2) // NG, 0)
                intake(i + 2, (s + 2) % NG, b + (s + 2) // NG, 1)
                decay_sums(i + 2, (s + 2) % NG, b + (s + 2) // NG, 0)
                merge32_end(i + 1)
                out_heads(i, s)
                if s == NG - 1:
                    output(b, i)


def delta_layout(i):
    g = lambda n: np.asarray(i["L0_attn_" + n])
    chunks = lambda a: np.ascontiguousarray(a.reshape(-1, P, a.shape[-1]).transpose(1, 0, 2))
    w = np.stack([chunks(g("W" + n)) for n in "qkv"], 1)
    wg, wo = chunks(g("Wg")), chunks(g("Wo"))
    wgate = chunks(np.concatenate([g("bw"), g("gkw")], 1))
    cw = np.stack([np.concatenate([g(n + "cw").reshape(-1, TAPS), g(n + "cb")[:, None]], 1) for n in "qkv"], 0)
    cw = np.ascontiguousarray(cw.reshape(3, -1, P, TAPS + 1).transpose(2, 0, 1, 3))
    rows = np.stack([g(n) for n in ("bb", "gkb", "dt_bias", "A_log", "D_param")])
    full = lambda a: np.ascontiguousarray(np.broadcast_to(a[None], (P,) + a.shape))
    t = np.arange(T, dtype=np.float32)
    inv = (1.0 / 10000.0 ** (np.arange(0, DH, 2, dtype=np.float32) / DH)).astype(np.float32)
    emb = np.concatenate([np.outer(t, inv)] * 2, -1).astype(np.float32)
    co, si = np.cos(emb)[:, ::2], np.sin(emb)[:, ::2]
    rope = np.stack([np.stack([co, si], 1), np.stack([-si, co], 1)], 1).astype(np.float32)
    rope = np.ascontiguousarray(rope.reshape(NT, P, 2, 2, DH // 2).transpose(1, 0, 2, 3, 4))
    a, c = np.arange(P)[:, None], np.arange(P)[None, :]
    tri = np.stack([a <= c, a < c, a > c, np.ones((P, P), bool)], 1).astype(np.float32)
    r, k = np.arange(P)[:, None] % 32, np.arange(32)[None, :]
    return dict(dwqkv=w, dwg=wg, dwo=wo, dwgate=wgate, dcw=cw, drows=full(rows), donw=full(g("onorm_w")), drope=rope,
                dtri=tri, dmshift=(c > a).astype(np.float32), dm16=((r >= 16) & (k < 16)).astype(np.float32),
                deye=full(np.eye(BL, dtype=np.float32)))


def program(nc, io, out):
    xnT = nc.dram_tensor("xnT_scratch", (B + 1, P, KC, T), F32).ap()
    gate = nc.dram_tensor("gate_scratch", (B, P, KC, T), F32).ap()
    Ld = nc.dram_tensor("blocks_scratch", (4, NQ, 2 * BL, 2 * BL), F32).ap()
    Td = nc.dram_tensor("inverse_scratch", (4, NQ, 2 * BL, 2 * BL), F32).ap()
    scratch = dict(xnT=xnT, gate=gate, Ld=Ld, Td=Td)
    tiles = lambda ap: ap.rearrange("b (w p) d -> b p w d", p=P)
    io = dict(io, x=tiles(io["x"]))
    with ExitStack() as ctx:
        ffn_phase(nc, ctx, io, scratch)
    with ExitStack() as ctx:
        delta_phase(nc, ctx, io, scratch, tiles(out))


def kernel(**inputs):
    import concourse.bacc as bacc
    from concourse.bass_utils import run_bass_kernel_spmd

    nc = bacc.Bacc("TRN2", target_bir_lowering=False, num_devices=1)
    arrays = {"in_" + n: a for n, a in (ffn_layout(inputs) | delta_layout(inputs)).items()}
    io = {n[3:]: nc.dram_tensor(n, a.shape, F32, kind="ExternalInput").ap() for n, a in arrays.items()}
    out = nc.dram_tensor("out", (B, T, D), F32, kind="ExternalOutput").ap()
    program(nc, io, out)
    got = run_bass_kernel_spmd(nc, [arrays], core_ids=[0])
    return got.results[0]["out"]
```
